# Optimizing a Trainium2 kernel written in Bass

```python
import numpy as np
import jax
import jax.numpy as jnp

def _softmax(x, axis=-1):
    return jax.nn.softmax(x, axis=axis)

def _gelu(x):
    return jax.nn.gelu(x, approximate=True)

def _silu(x):
    return jax.nn.silu(x)

def _sigmoid(x):
    return jax.nn.sigmoid(x)

def _layernorm(x, axis=-1, eps=1e-05):
    m = jnp.mean(x, axis=axis, keepdims=True)
    v = jnp.var(x, axis=axis, keepdims=True)
    return (x - m) / jnp.sqrt(v + eps)

def _scatter_add(tgt, idx, src, axis=0):
    return tgt.at[idx].add(src)

def _segment_sum(src, seg, n):
    return jax.ops.segment_sum(src, seg, n)
kernel_name = 'mk_decoder_preln_d1_seqx_r2_07b9dd'

def setup_inputs(seed: int=0):
    np.random.seed(seed)
    _w = jnp.asarray

    def _rec_inputs():
        import jax
        import jax.numpy as jnp
        _rk = jax.random.key(seed)
        x = 7.22e-05 + 1 * jax.random.normal(jax.random.fold_in(_rk, 1), (2, 2048, 512), jnp.float32)
        _lenS = 2048 - jax.random.randint(jax.random.fold_in(_rk, 7), (2,), 0, max(1, 2048 // 4) + 1, jnp.int32)
        _lenS2 = 154 - jax.random.randint(jax.random.fold_in(_rk, 8), (2,), 0, max(1, 154 // 4) + 1, jnp.int32)
        _ctx_1024P = jax.random.normal(jax.random.fold_in(_rk, 11), (2, 16, 512), jnp.float32)
        _ctx_1024c = jax.random.dirichlet(jax.random.fold_in(_rk, 511), 0.3 * jnp.ones((16,), jnp.float32), (2, 154))
        _ctx_1024t = jnp.einsum('bsk,bkd->bsd', _ctx_1024c, _ctx_1024P)
        _ctx_1024t = _ctx_1024t * jax.lax.rsqrt(jnp.mean(jnp.square(_ctx_1024t)) + 1e-12) * 0.953939
        ctx_1024 = 4.13588e-05 + 0.999923 * (_ctx_1024t + 0.3 * jax.random.normal(jax.random.fold_in(_rk, 611), (2, 154, 512), jnp.float32))
        return (x, ctx_1024)
    x, ctx_1024 = _rec_inputs()

    def _L0_attn_setup():
        import jax, jax.numpy as jnp
        import numpy as np
        DIM = 512
        HEADS = 16
        HEAD_DIM = DIM // HEADS
        FEAT = 128
        B, N = (4, 2048)

        def _elu1(x):
            return jnp.where(x > 0, x + 1.0, jnp.exp(x))
        key = jax.random.key(seed)
        k_x, k_qkv, k_proj, k_wo, k_bo = jax.random.split(key, 5)
        x = jax.random.normal(k_x, (B, N, DIM), dtype=jnp.float32)
        w_qkv = jax.random.normal(k_qkv, (DIM, 3 * DIM), dtype=jnp.float32) * (1.0 / np.sqrt(DIM))
        proj_matrix = jax.random.normal(k_proj, (HEADS, HEAD_DIM, FEAT), dtype=jnp.float32) * (1.0 / np.sqrt(HEAD_DIM))
        w_out = jax.random.normal(k_wo, (DIM, DIM), dtype=jnp.float32) * (1.0 / np.sqrt(DIM))
        b_out = jax.random.normal(k_bo, (DIM,), dtype=jnp.float32) * 0.01
        return {'x': x, 'w_qkv': w_qkv, 'proj_matrix': proj_matrix, 'w_out': w_out, 'b_out': b_out}
    _L0_attn_all = _L0_attn_setup()
    _L0_attn_in = {k: v for k, v in _L0_attn_all.items() if k in ('w_qkv', 'proj_matrix', 'w_out', 'b_out')}
    del _L0_attn_all

    def _L0_xattn_setup():
        import jax, jax.numpy as jnp
        import numpy as np
        D_MODEL = 512
        NUM_HEADS = 16
        D_K = D_MODEL // NUM_HEADS
        key = jax.random.key(seed)
        ks = jax.random.split(key, 11)
        B, S = (4, 1024)
        s = 1.0 / np.sqrt(D_MODEL)
        return {'query': jax.random.normal(ks[0], (B, S, D_MODEL), jnp.float32), 'key': jax.random.normal(ks[1], (B, S, D_MODEL), jnp.float32), 'value': jax.random.normal(ks[2], (B, S, D_MODEL), jnp.float32), 'Wq': jax.random.normal(ks[3], (D_MODEL, D_MODEL), jnp.float32) * s, 'bq': jax.random.normal(ks[4], (D_MODEL,), jnp.float32) * s, 'Wk': jax.random.normal(ks[5], (D_MODEL, D_MODEL), jnp.float32) * s, 'bk': jax.random.normal(ks[6], (D_MODEL,), jnp.float32) * s, 'Wv': jax.random.normal(ks[7], (D_MODEL, D_MODEL), jnp.float32) * s, 'bv': jax.random.normal(ks[8], (D_MODEL,), jnp.float32) * s, 'Wo': jax.random.normal(ks[9], (D_MODEL, D_MODEL), jnp.float32) * s, 'bo': jax.random.normal(ks[10], (D_MODEL,), jnp.float32) * s}
    _L0_xattn_all = _L0_xattn_setup()
    _L0_xattn_in = {k: v for k, v in _L0_xattn_all.items() if k in ('Wq', 'bq', 'Wk', 'bk', 'Wv', 'bv', 'Wo', 'bo')}
    del _L0_xattn_all

    def _L0_ffn_setup():
        import jax, jax.numpy as jnp
        import numpy as np
        TOP_K = 6

        def _glu_mlp(x, wg, wu, wd):
            return jax.nn.silu(x @ wg) * (x @ wu) @ wd
        key = jax.random.key(seed)
        ks = jax.random.split(key, 8)
        B, S, D, E, F, FS = (2, 1024, 512, 8, 256, 512)
        sc = 0.02
        return {'hidden_states': jax.random.normal(ks[0], (B, S, D), jnp.float32), 'router_w': jax.random.normal(ks[1], (D, E), jnp.float32) * sc, 'w_gate': jax.random.normal(ks[2], (E, D, F), jnp.float32) * sc, 'w_up': jax.random.normal(ks[3], (E, D, F), jnp.float32) * sc, 'w_down': jax.random.normal(ks[4], (E, F, D), jnp.float32) * sc, 'ws_gate': jax.random.normal(ks[5], (D, FS), jnp.float32) * sc, 'ws_up': jax.random.normal(ks[6], (D, FS), jnp.float32) * sc, 'ws_down': jax.random.normal(ks[7], (FS, D), jnp.float32) * sc}
    _L0_ffn_all = _L0_ffn_setup()
    _L0_ffn_in = {k: v for k, v in _L0_ffn_all.items() if k in ('router_w', 'w_gate', 'w_up', 'w_down', 'ws_gate', 'ws_up', 'ws_down')}
    del _L0_ffn_all
    return {'x': x, 'ctx_1024': ctx_1024, 'L0_attn_w_qkv': _L0_attn_in['w_qkv'], 'L0_attn_proj_matrix': _L0_attn_in['proj_matrix'], 'L0_attn_w_out': _L0_attn_in['w_out'], 'L0_attn_b_out': _L0_attn_in['b_out'], 'L0_xattn_Wq': _L0_xattn_in['Wq'], 'L0_xattn_bq': _L0_xattn_in['bq'], 'L0_xattn_Wk': _L0_xattn_in['Wk'], 'L0_xattn_bk': _L0_xattn_in['bk'], 'L0_xattn_Wv': _L0_xattn_in['Wv'], 'L0_xattn_bv': _L0_xattn_in['bv'], 'L0_xattn_Wo': _L0_xattn_in['Wo'], 'L0_xattn_bo': _L0_xattn_in['bo'], 'L0_ffn_router_w': _L0_ffn_in['router_w'], 'L0_ffn_w_gate': _L0_ffn_in['w_gate'], 'L0_ffn_w_up': _L0_ffn_in['w_up'], 'L0_ffn_w_down': _L0_ffn_in['w_down'], 'L0_ffn_ws_gate': _L0_ffn_in['ws_gate'], 'L0_ffn_ws_up': _L0_ffn_in['ws_up'], 'L0_ffn_ws_down': _L0_ffn_in['ws_down']}

def reference(x, ctx_1024, L0_attn_w_qkv, L0_attn_proj_matrix, L0_attn_w_out, L0_attn_b_out, L0_xattn_Wq, L0_xattn_bq, L0_xattn_Wk, L0_xattn_bk, L0_xattn_Wv, L0_xattn_bv, L0_xattn_Wo, L0_xattn_bo, L0_ffn_router_w, L0_ffn_w_gate, L0_ffn_w_up, L0_ffn_w_down, L0_ffn_ws_gate, L0_ffn_ws_up, L0_ffn_ws_down):
    import jax
    import jax.numpy as jnp

    def _L0_attn_ref(x, w_qkv, proj_matrix, w_out, b_out):
        import jax, jax.numpy as jnp
        import numpy as np
        DIM = 512
        HEADS = 16
        HEAD_DIM = DIM // HEADS
        FEAT = 128
        B, N = (4, 2048)

        def _elu1(x):
            return jnp.where(x > 0, x + 1.0, jnp.exp(x))
        b, n, d = x.shape
        h, hd = (HEADS, HEAD_DIM)
        qkv = x @ w_qkv
        q, k, v = jnp.split(qkv, 3, axis=-1)
        to_heads = lambda t: t.reshape(b, n, h, hd).transpose(0, 2, 1, 3)
        q, k, v = (to_heads(q), to_heads(k), to_heads(v))
        q_proj = _elu1(jnp.einsum('bhnd,hdf->bhnf', q, proj_matrix))
        k_proj = _elu1(jnp.einsum('bhnd,hdf->bhnf', k, proj_matrix))
        kv = jnp.einsum('bhnf,bhnd->bhfd', k_proj, v)
        attn = jnp.einsum('bhnf,bhfd->bhnd', q_proj, kv)
        k_sum = k_proj.sum(axis=2)
        z = 1.0 / (jnp.einsum('bhnf,bhf->bhn', q_proj, k_sum) + 1e-08)
        attn = attn * z[..., None]
        out = attn.transpose(0, 2, 1, 3).reshape(b, n, d)
        return out @ w_out + b_out

    def _L0_xattn_ref(query, key, value, Wq, bq, Wk, bk, Wv, bv, Wo, bo):
        import jax, jax.numpy as jnp
        import numpy as np
        D_MODEL = 512
        NUM_HEADS = 16
        D_K = D_MODEL // NUM_HEADS
        B, Sq, _ = query.shape

        def proj(x, W, b):
            y = x @ W.T + b
            return y.reshape(B, -1, NUM_HEADS, D_K).transpose(0, 2, 1, 3)
        q = proj(query, Wq, bq)
        k = proj(key, Wk, bk)
        v = proj(value, Wv, bv)
        scores = jnp.einsum('bhqd,bhkd->bhqk', q, k) / jnp.sqrt(jnp.float32(D_K))
        attn = jax.nn.softmax(scores, axis=-1)
        ctx = jnp.einsum('bhqk,bhkd->bhqd', attn, v)
        ctx = ctx.transpose(0, 2, 1, 3).reshape(B, Sq, D_MODEL)
        return ctx @ Wo.T + bo

    def _L0_ffn_ref(hidden_states, router_w, w_gate, w_up, w_down, ws_gate, ws_up, ws_down):
        import jax, jax.numpy as jnp
        import numpy as np
        TOP_K = 6

        def _glu_mlp(x, wg, wu, wd):
            return jax.nn.silu(x @ wg) * (x @ wu) @ wd
        B, S, D = hidden_states.shape
        x = hidden_states.reshape(-1, D)
        scores = jax.nn.softmax(x @ router_w, axis=-1)
        topk_w, topk_idx = jax.lax.top_k(scores, TOP_K)
        g = jnp.einsum('td,edf->etf', x, w_gate)
        u = jnp.einsum('td,edf->etf', x, w_up)
        f_all = jnp.einsum('etf,efd->ted', jax.nn.silu(g) * u, w_down)
        picked = jnp.take_along_axis(f_all, topk_idx[:, :, None], axis=1)
        y = jnp.sum(picked * topk_w[:, :, None], axis=1).reshape(B, S, D)
        y = y + _glu_mlp(hidden_states, ws_gate, ws_up, ws_down)
        return y
    x = x + _L0_attn_ref(_layernorm(x, axis=-1), L0_attn_w_qkv, L0_attn_proj_matrix, L0_attn_w_out, L0_attn_b_out)
    x = x + _L0_xattn_ref(_layernorm(x, axis=-1), ctx_1024, ctx_1024, L0_xattn_Wq, L0_xattn_bq, L0_xattn_Wk, L0_xattn_bk, L0_xattn_Wv, L0_xattn_bv, L0_xattn_Wo, L0_xattn_bo)
    x = x + _L0_ffn_ref(_layernorm(x, axis=-1), L0_ffn_router_w, L0_ffn_w_gate, L0_ffn_w_up, L0_ffn_w_down, L0_ffn_ws_gate, L0_ffn_ws_up, L0_ffn_ws_down)
    return x

_drawn_inputs = setup_inputs


def setup_inputs(seed=0):
    import zlib

    import numpy as np

    out = dict(_drawn_inputs(seed))
    spreads = {}
    factors = {'L0_attn_w_qkv': 2.805,
     'L0_attn_proj_matrix': 8.0,
     'L0_attn_w_out': 2.726,
     'L0_attn_b_out': 6.342,
     'L0_xattn_bq': 6.07,
     'L0_xattn_bk': 64.0,
     'L0_ffn_router_w': 8.0,
     'L0_ffn_w_gate': 5.092,
     'L0_ffn_w_up': 5.043,
     'L0_ffn_w_down': 5.017,
     'L0_ffn_ws_gate': 5.415,
     'L0_ffn_ws_up': 5.323,
     'L0_ffn_ws_down': 5.312}
    for name, (base, spread) in spreads.items():
        noise = np.random.default_rng([zlib.crc32(name.encode()), seed]).standard_normal(out[name].shape)
        drawn = base * np.exp(spread * noise) if base else spread * noise
        out[name] = jnp.asarray(drawn.astype(out[name].dtype))
    for name, factor in factors.items():
        out[name] = (out[name] * factor).astype(out[name].dtype)
    return out
```

```python
from contextlib import ExitStack

import concourse.bass as bass
import numpy as np
from concourse import mybir

F32 = mybir.dt.float32
F32R = mybir.dt.float32r
BF16 = mybir.dt.bfloat16
ALU = mybir.AluOpType
ACT = mybir.ActivationFunctionType
AX = mybir.AxisListType

P = 128
HI, LO = 0, 1
PASSES = ((HI, HI), (HI, LO), (LO, HI))

D = 512
C = D // P
H = 16
HD = D // H
HG = P // HD
G = H // HG
F = 128
TB = 512
TT = TB // P
KEYS = 154
KREM = KEYS - P
KPAD = 32
E = 8
TOP = 6
FE = 256
UNITS = E + 2
FT = FE // P
EPS = 1e-5


class Tally:

    def __init__(self, jobs, banks):
        self.pos = {key: n for n, (key, _, _) in enumerate(jobs)}
        self.jobs, self.banks, self.n = jobs, banks, len(jobs)
        self.n_act = sum(a for _, a, _ in jobs)
        self.n_dve = sum(d for _, _, d in jobs)

    def filled(self, key):
        return self.pos[key] + 1

    def act(self, key):
        return sum(a for _, a, _ in self.jobs[:self.pos[key] + 1])

    def dve(self, key):
        return sum(d for _, _, d in self.jobs[:self.pos[key] + 1])

    def bank(self, key):
        return self.pos[key] % self.banks

    def before(self, key):
        n = self.pos[key] - self.banks
        return self.jobs[n] if n >= 0 else None


def constants():
    ident = np.eye(P, dtype=np.float32)
    quad = np.arange(P) // HD
    key = np.arange(P) % HD
    mask = (quad[:, None] == np.arange(HG)).astype(np.float32)
    mask_keys = mask * (key < KREM)[:, None]
    one_col = np.zeros((P, G, HD), np.float32)
    rem_ones = np.zeros((P, G, P), np.float32)
    spread = np.zeros((P, G, P), np.float32)
    for g in range(G):
        one_col[:, g, g] = 1
        for p in range(P):
            if key[p] < KREM:
                rem_ones[p, g, 32 * quad[p] + g] = 1
            spread[32 * quad[p] + g, g, p] = 1
    minus = np.zeros((P, G, HG + 1, P), np.float32)
    for g in range(G):
        for j in range(HG):
            for r in (HG * g + j, H + HG * g + j):
                minus[r, g, j, :] = -1
                minus[r, g, HG, 32 * j:32 * j + 32] = -1
    lower = np.zeros((P, E, E), np.float32)
    for e in range(E):
        lower[:, e, :e] = 1
    small = np.concatenate([mask, mask_keys], 1)
    return {
        "ident": ident, "small": small, "one_col": one_col.reshape(P, -1), "rem_ones": rem_ones.reshape(P, -1),
        "spread": spread.reshape(P, -1), "minus": minus.reshape(P, -1), "lower": lower.reshape(P, -1),
    }


def decoder_kernel(nc, a, out):
    NB = a["x"].shape[0]
    BLK = a["x"].shape[1] // TB
    NBLK = NB * BLK
    x_blk = a["x"].rearrange("b (k t p) d -> (b k) p t d", t=TT, p=P)
    out_bat = out.rearrange("b (n p) d -> b p n d", p=P)
    x2_dram = nc.dram_tensor("x2_scratch", [NBLK, P, TT * D], F32).ap()
    q_dram = nc.dram_tensor("q_scratch", [NBLK, P, 2 * C * TB], F32).ap()
    x3_dram = nc.dram_tensor("x3_scratch", [NBLK, P, C * TB], F32).ap()

    with ExitStack() as whole:
        ident = whole.enter_context(nc.sbuf_tensor("ident", [P, P], F32))
        with ExitStack() as upto_attend:
            kv_w = upto_attend.enter_context(nc.sbuf_tensor("kv_w", [P, NB, H, HD], F32))
            ks_w = upto_attend.enter_context(nc.sbuf_tensor("ks_w", [P, NB, H, HD], F32))
            half = upto_attend.enter_context(nc.sbuf_tensor("half", [P, TT], F32))
            project(nc, a, NBLK, BLK, x_blk, q_dram, ident, kv_w, ks_w, half)
            attend(nc, a, NB, BLK, x_blk, q_dram, x2_dram, x3_dram, ident, kv_w, ks_w, half)
        experts(nc, a, NB, BLK, x2_dram, x3_dram, out_bat, ident)


def project(nc, a, NBLK, BLK, x_blk, q_dram, ident, kv_w, ks_w, half):
    T = Tally([(("T", t), 1, 1) for t in range(TT)] + [(("K", g), 1, 1) for g in range(G)]
              + [(("Q", g), 1, 1) for g in range(G)] + [(("V", t), 0, 1) for t in range(TT)]
              + [(("KP", n), 1, 1) for n in range(TT * G)], 2)
    NKP = TT * G
    LAG = 3
    with ExitStack() as ctx:
        def sb(name, shape, dt=F32):
            return ctx.enter_context(nc.sbuf_tensor("pr_" + name, shape, dt))

        def sem(name):
            return ctx.enter_context(nc.semaphore("pr_" + name))

        w_raw = sb("w_raw", [P, C, 3 * D])
        w = sb("w", [P, 2, C, 3 * D], F32R)
        f_raw = sb("f_raw", [P, G, HG * F])
        f_w = sb("f_w", [P, 2, G, HG * F], F32R)
        x = sb("x", [P, TT, D])
        xn = sb("xn", [P, TT, D])
        xt = sb("xt", [P, 2, C, TB], F32R)
        kt = sb("kt", [P, 2, C, TB], F32R)
        qs = sb("qs", [P, 2, C, TB], F32R)
        v = sb("v", [P, TT, D])
        e = sb("e", [P, 4, HG * F])
        kp = sb("kp", [P, 4, HG * F])
        stats = sb("stats", [P, TT, 6])
        mv = sb("mv", [P, TT, 2])
        rstd = sb("rstd", [P, TT])
        pause = sb("pause", [P, 1])
        ones = sb("ones", [P, HD])
        kv_sum = sb("kv_sum", [P, NBLK // BLK, G * F])
        ks_sum = sb("ks_sum", [P, NBLK // BLK, HG * F])
        pj = [ctx.enter_context(nc.psum_tensor(f"pr_pj{n}", [P, 512], F32)) for n in range(2)]
        pk = [ctx.enter_context(nc.psum_tensor(f"pr_pk{n}", [P, 512], F32)) for n in range(4)]
        p_kv = ctx.enter_context(nc.psum_tensor("pr_p_kv", [P, 512], F32))
        p_ks = ctx.enter_context(nc.psum_tensor("pr_p_ks", [P, 512], F32))

        w_in, x_in, q_out = sem("w_in"), sem("x_in"), sem("q_out")
        const_in, const_set = sem("const_in"), sem("const_set")
        w_hi, w_lo = sem("w_hi"), sem("w_lo")
        filled, act_read, dve_read = sem("filled"), sem("act_read"), sem("dve_read")
        stats_set, var_set, rstd_set, xn_set = sem("stats_set"), sem("var_set"), sem("rstd_set"), sem("xn_set")
        relu_set, kv_step, kv_taken = sem("relu_set"), sem("kv_step"), sem("kv_taken")
        turned, kv_done = sem("turned"), sem("kv_done")

        def bank_of(key):
            return pk[key[1] % 4] if key[0] == "KP" else pj[T.bank(key)]

        with nc.Block() as block:
            @block.sync
            def _(sp):
                sp.dma_start(x[:], x_blk[0]).then_inc(x_in, 16)
                sp.dma_start(ident[:], a["ident"]).then_inc(const_in, 16)
                w_src = a["w_qkv"].rearrange("(c p) n -> p c n", p=P)
                for c in range(C):
                    sp.dma_start(w_raw[:, c], w_src[:, c]).then_inc(w_in, 16)
                sp.dma_start(f_raw[:], a["features"].rearrange("p (g f) -> p g f", g=G)).then_inc(w_in, 16)

                def block_io(i, last):
                    if not last:
                        sp.wait_ge(xn_set, TT * i + TT)
                        sp.dma_start(x[:], x_blk[i + 1]).then_inc(x_in, 16)
                    sp.wait_ge(dve_read, T.n_dve * i + T.dve(("Q", G - 1)))
                    sp.dma_start(q_dram[i], qs[:].bitcast(F32).rearrange("p s c t -> p (s c t)")).then_inc(q_out, 16)

                with sp.Fori(0, NBLK - 1) as i:
                    block_io(i, False)
                block_io(NBLK - 1, True)
                sp.wait_ge(q_out, 16 * NBLK)

            @block.gpsimd
            def _(pool):
                nc.gpsimd.memset(half[:], -0.5).then_inc(const_set, 1)
                nc.gpsimd.memset(ones[:], 1.0).then_inc(const_set, 1)
                nc.gpsimd.memset(ks_w[:], 0.0).then_inc(const_set, 1)
                nc.gpsimd.memset(kv_sum[:], 0.0).then_inc(const_set, 1)
                nc.gpsimd.memset(ks_sum[:], 0.0).then_inc(const_set, 1)
                pool.wait_ge(const_set, 1)
                with pool.Fori(0, NBLK) as i:
                    pool.wait_ge(var_set, i + 1)
                    nc.gpsimd.tensor_tensor(rstd[:], mv[:, :, 1], half[:], ALU.pow).then_inc(rstd_set, 1)

            @block.scalar
            def _(act):
                for c in range(C):
                    act.wait_ge(w_in, 16 * (C + 1))
                    nc.scalar.copy(w[:, HI, c], w_raw[:, c]).then_inc(w_hi, 1)
                nc.scalar.copy(f_w[:, HI], f_raw[:]).then_inc(w_hi, 1)

                def turn(i):
                    for t in range(TT):
                        act.wait_ge(filled, T.n * i + T.filled(("T", t)))
                        nc.scalar.copy(xt[:, HI, :, t * P:(t + 1) * P],
                                       bank_of(("T", t))[:].rearrange("p (c n) -> p c n", c=C)).then_inc(act_read, 1)

                def heads(i):
                    for g in range(G):
                        act.wait_ge(filled, T.n * i + T.filled(("K", g)))
                        nc.scalar.copy(kt[:, HI, g], bank_of(("K", g))[:]).then_inc(act_read, 1)
                    act.wait_ge(q_out, 16 * i)
                    for g in range(G):
                        act.wait_ge(filled, T.n * i + T.filled(("Q", g)))
                        nc.scalar.copy(qs[:, HI, g], bank_of(("Q", g))[:]).then_inc(act_read, 1)
                    for n in range(NKP + 1):
                        if n < NKP:
                            act.wait_ge(filled, T.n * i + T.filled(("KP", n)))
                            nc.scalar.activation(e[:, n % 4], bank_of(("KP", n))[:], ACT.Relu, scale=-1.0)\
                                .then_inc(relu_set, 1)
                        if n:
                            act.wait_ge(relu_set, NKP * i + n)
                            nc.scalar.activation(e[:, (n - 1) % 4], e[:, (n - 1) % 4], ACT.Exp, scale=-1.0)\
                                .then_inc(act_read, 1)

                turn(0)
                with act.Fori(0, NBLK - 1) as i:
                    heads(i)
                    turn(i + 1)
                heads(NBLK - 1)

            @block.vector
            def _(dve):
                def norm_stats(i, t):
                    if t == 0:
                        dve.wait_ge(x_in, 16 * i + 16)
                    nc.vector.bn_stats(stats[:, t], x[:, t]).then_inc(stats_set, 1)

                def norm_var(i):
                    dve.wait_ge(stats_set, TT * i + TT)
                    nc.vector.tensor_copy(pause[:], half[:, 0:1])
                    for t in range(TT):
                        nc.vector.bn_aggr(mv[:, t], stats[:, t]).then_inc(turned, 1)
                    dve.wait_ge(turned, TT * i + TT)
                    nc.vector.tensor_scalar(mv[:, :, 1], mv[:, :, 1], EPS, None, ALU.add).then_inc(var_set, 1)

                def norm(i):
                    dve.wait_ge(rstd_set, i + 1)
                    for t in range(TT):
                        nc.vector.tensor_scalar(xn[:, t], x[:, t], mv[:, t, 0:1], rstd[:, t:t + 1],
                                                ALU.subtract, ALU.mult).then_inc(xn_set, 1)

                def turn(i):
                    for t in range(TT):
                        part = slice(t * P, (t + 1) * P)
                        dve.wait_ge(act_read, T.n_act * i + T.act(("T", t)))
                        nc.vector.tensor_tensor(xt[:, LO, :, part], bank_of(("T", t))[:].rearrange("p (c n) -> p c n", c=C),
                                                xt[:, HI, :, part].bitcast(F32), ALU.subtract).then_inc(dve_read, 1)

                def heads(i, last):
                    for g in range(G):
                        dve.wait_ge(act_read, T.n_act * i + T.act(("K", g)))
                        nc.vector.tensor_tensor(kt[:, LO, g], bank_of(("K", g))[:], kt[:, HI, g].bitcast(F32),
                                                ALU.subtract).then_inc(dve_read, 1)
                    for g in range(G):
                        dve.wait_ge(act_read, T.n_act * i + T.act(("Q", g)))
                        nc.vector.tensor_tensor(qs[:, LO, g], bank_of(("Q", g))[:], qs[:, HI, g].bitcast(F32),
                                                ALU.subtract).then_inc(dve_read, 1)
                        if not last:
                            norm_stats(i + 1, g)
                    for t in range(TT):
                        dve.wait_ge(filled, T.n * i + T.filled(("V", t)))
                        nc.vector.tensor_copy(v[:, t], bank_of(("V", t))[:]).then_inc(dve_read, 1)
                        if t == 0 and not last:
                            norm_var(i + 1)
                    if not last:
                        norm(i + 1)
                    for n in range(NKP):
                        dve.wait_ge(kv_step, NKP * i + max(n - 3, 0))
                        dve.wait_ge(act_read, T.n_act * i + T.act(("KP", n)))
                        nc.vector.scalar_tensor_tensor(kp[:, n % 4], bank_of(("KP", n))[:], 0.0, e[:, n % 4],
                                                       ALU.max, ALU.add).then_inc(dve_read, 1)

                def add_kv(i, b):
                    dve.wait_ge(kv_step, NKP * i + NKP)
                    dve.wait_ge(kv_taken, 2 * i)
                    nc.vector.tensor_tensor(kv_sum[:, b], kv_sum[:, b], p_kv[:], ALU.add).then_inc(kv_taken, 1)
                    nc.vector.tensor_tensor(ks_sum[:, b], ks_sum[:, b], p_ks[:], ALU.add).then_inc(kv_taken, 1)

                dve.wait_ge(const_set, 1)
                for t in range(TT):
                    norm_stats(0, t)
                norm_var(0)
                norm(0)
                for c in range(C):
                    dve.wait_ge(w_hi, c + 1)
                    nc.vector.tensor_tensor(w[:, LO, c], w_raw[:, c], w[:, HI, c].bitcast(F32),
                                            ALU.subtract).then_inc(w_lo, 1)
                dve.wait_ge(w_hi, C + 1)
                nc.vector.tensor_tensor(f_w[:, LO], f_raw[:], f_w[:, HI].bitcast(F32), ALU.subtract).then_inc(w_lo, 1)
                turn(0)
                dve.wait_ge(const_set, 5)
                for b in range(NBLK // BLK):
                    with dve.Fori(0, BLK - 1) as k:
                        i = k + BLK * b
                        heads(i, False)
                        turn(i + 1)
                        add_kv(i, b)
                    i = BLK * b + BLK - 1
                    heads(i, i == NBLK - 1)
                    if i < NBLK - 1:
                        turn(i + 1)
                    add_kv(i, b)
                for b in range(NBLK // BLK):
                    dve.wait_ge(kv_done, 2 * b + 1)
                    nc.vector.tensor_copy(kv_w[:, b].rearrange("p h d -> p (h d)"), pk[b][:]).then_inc(turned, 1)
                    dve.wait_ge(kv_done, 2 * b + 2)
                    flat = ks_w[:, b].rearrange("p h d -> p (h d)")
                    for j in range(HG):
                        nc.vector.tensor_copy(flat[:, j * HD:(H - HG + j) * HD + G:HG * HD + 1],
                                              pk[2 + b][:, j * P:(j + 1) * P:HD]).then_inc(turned, 1)

            @block.tensor
            def _(pe):
                def dve_has_read(i, key):
                    pe.wait_ge(dve_read, T.n_dve * i + T.dve(key))

                def turn(i, first):
                    for t in range(TT):
                        pe.wait_ge(xn_set, TT * i + t + 1)
                        if t >= 2:
                            dve_has_read(i, ("T", t - 2))
                        elif not first:
                            pe.wait_ge(dve_read, T.n_dve * (i - 1) + T.dve(("V", TT - 1)))
                        for c in range(C):
                            mm = nc.tensor.transpose(bank_of(("T", t))[:, c * P:(c + 1) * P],
                                                     xn[:, t, c * P:(c + 1) * P], ident[:])
                        mm.then_inc(filled, 1)

                def projections(i):
                    for g in range(G):
                        if g < 2:
                            dve_has_read(i, ("T", TT - 1))
                        else:
                            dve_has_read(i, ("K", g - 2))
                        matmuls(("K", g), lambda s, c, g=g: w[:, s, c, D + g * P:D + (g + 1) * P],
                                lambda s, c: xt[:, s, c])
                    for g in range(G):
                        dve_has_read(i, ("Q", g - 2) if g > 1 else ("K", g + 2))
                        matmuls(("Q", g), lambda s, c, g=g: w[:, s, c, g * P:(g + 1) * P],
                                lambda s, c: xt[:, s, c])
                    for t in range(TT):
                        dve_has_read(i, ("V", t - 2) if t > 1 else ("Q", t + 2))
                        matmuls(("V", t), lambda s, c, t=t: xt[:, s, c, t * P:(t + 1) * P],
                                lambda s, c: w[:, s, c, 2 * D:3 * D])

                def matmuls(key, stationary, moving):
                    n = 0
                    for c in range(C):
                        for s, m in PASSES:
                            mm = nc.tensor.matmul(bank_of(key)[:], stationary(s, c), moving(m, c),
                                                  start=(n == 0), stop=(n == C * 3 - 1))
                            n += 1
                    mm.then_inc(filled, 1)

                def features(i, n):
                    t, g = n // G, n % G
                    if n >= 4:
                        dve_has_read(i, ("KP", n - 4))
                    else:
                        dve_has_read(i, ("K", g))
                    for q, (s, m) in enumerate(PASSES):
                        mm = nc.tensor.matmul(pk[n % 4][:], kt[:, s, g, t * P:(t + 1) * P], f_w[:, m, g],
                                              start=(q == 0), stop=(q == 2))
                    mm.then_inc(filled, 1)

                def kv(i, n):
                    t, g = n // G, n % G
                    dve_has_read(i, ("KP", n))
                    if n == 0:
                        pe.wait_ge(kv_taken, 2 * i)
                    for j in range(HG):
                        h = g * HG + j
                        nc.tensor.matmul(p_kv[j * HD:(j + 1) * HD, g * F:(g + 1) * F], v[:, t, h * HD:(h + 1) * HD],
                                         kp[:, n % 4, j * F:(j + 1) * F], start=(t == 0 and g == 0), stop=(t == TT - 1),
                                         skip_group_check=True)
                    nc.tensor.matmul(p_ks[g * HD:(g + 1) * HD, :], ones[:], kp[:, n % 4], start=(t == 0),
                                     stop=(t == TT - 1), skip_group_check=True).then_inc(kv_step, 1)

                def block_work(i, last):
                    projections(i)
                    for n in range(NKP):
                        features(i, n)
                        if n >= LAG:
                            kv(i, n - LAG)
                    if not last:
                        turn(i + 1, False)
                    for n in range(NKP - LAG, NKP):
                        kv(i, n)

                pe.wait_ge(const_in, 16)
                pe.wait_ge(const_set, 2)
                turn(0, True)
                pe.wait_ge(w_lo, C + 1)
                with pe.Fori(0, NBLK - 1) as i:
                    block_work(i, False)
                block_work(NBLK - 1, True)
                pe.wait_ge(kv_taken, 2 * NBLK)
                for b in range(NBLK // BLK):
                    for g in range(G):
                        mm = nc.tensor.transpose(pk[b][:, g * P:(g + 1) * P], kv_sum[:, b, g * P:(g + 1) * P], ident[:])
                    mm.then_inc(kv_done, 1)
                    for j in range(HG):
                        mm = nc.tensor.transpose(pk[2 + b][:, j * P:(j + 1) * P], ks_sum[:, b, j * P:(j + 1) * P], ident[:])
                    mm.then_inc(kv_done, 1)


def attend(nc, a, NB, BLK, x_blk, q_dram, x2_dram, x3_dram, ident, kv_w, ks_w, half):
    SU = HG + 1
    jobs = [(("QP", h), 1, 1) for h in range(H)]
    jobs += [(("R1", g), 0, 1) for g in range(G)]

    def out_and_turn(o, t):
        return [((o, 0), 0, 1), ((o, 1), 0, 1), ((o, 2), 0, 1), ((t, 0), t == "T1", 1), ((o, 3), 0, 1),
                ((t, 1), t == "T1", 1), ((t, 2), t == "T1", 1), ((t, 3), t == "T1", 1)]

    jobs += out_and_turn("O1", "T1")
    jobs += [(("XQ", g), 1, 1) for g in range(G)]
    jobs += [(("MX", t, g), 0, 1) for t in range(TT) for g in range(G + 1)]
    jobs += [(("MT", 0), 1, 0)]
    jobs += [(("S", n), 1, 0) for n in range(G * SU)]
    jobs += [(("R2", g), 0, 1) for g in range(G)]
    jobs += out_and_turn("O2", "T2")
    BANKS = 5
    T = Tally(jobs, BANKS)
    SLOTS = 2 * SU
    with ExitStack() as ctx:
        def sb(name, shape, dt=F32):
            return ctx.enter_context(nc.sbuf_tensor("at_" + name, shape, dt))

        def sem(name):
            return ctx.enter_context(nc.semaphore("at_" + name))

        f_w = sb("f_w", [P, 2, G, HG * F], F32R)
        wo1 = sb("wo1", [P, 2, C, D], F32R)
        wq = sb("wq", [P, 2, C, D], F32R)
        wo2 = sb("wo2", [P, 2, C, D], F32R)
        k_w = sb("k_w", [P, 2, G, HG * P + P], F32R)
        v_w = sb("v_w", [P, D])
        v_rem = sb("v_rem", [P, G, HG, HD])
        one_col = sb("one_col", [P, G, HD])
        rem_ones = sb("rem_ones", [P, G, P])
        spread = sb("spread", [P, G, P])
        minus = sb("minus", [P, G, SU, P], BF16)
        bias1 = sb("bias1", [P, D])
        bias2 = sb("bias2", [P, D])
        bq = sb("bq", [P, C])
        bk = sb("bk", [P, C])
        small = sb("small", [P, 2 * HG])
        x = sb("x", [P, TT, D])
        qt = sb("qt", [P, 2, C, TB], F32R)
        u0 = sb("u0", [P, 2, C, TB], F32R)
        u1 = sb("u1", [P, 2, C, TB], F32R)
        xn = sb("xn", [P, 2, D])
        ring = sb("ring", [P, SLOTS, TB])
        num = sb("num", [P, G, TB])
        den = sb("den", [P, 2, TB])
        kt = sb("kt", [P, 2, P + KPAD])
        stats = sb("stats", [P, TT, 6])
        mv = sb("mv", [P, TT, 2])
        rstd = sb("rstd", [P, TT])
        pause = sb("pause", [P, 1])
        mx = sb("mx", [P, 2, TT, H])
        mxb = sb("mxb", [P, TT, P], BF16)
        mxt = sb("mxt", [P, TB], BF16)
        ident_b = sb("ident_b", [P, P], BF16)
        bank = [ctx.enter_context(nc.psum_tensor(f"at_bank{n}", [P, 512], F32)) for n in range(BANKS)]
        p_num = [ctx.enter_context(nc.psum_tensor(f"at_p_num{n}", [P, 512], F32)) for n in range(2)]
        p_den = ctx.enter_context(nc.psum_tensor("at_p_den", [P, 512], F32))

        w_in, raw_free, w_hi, w_lo = sem("w_in"), sem("raw_free"), sem("w_hi"), sem("w_lo")
        const_in, const_set = sem("const_in"), sem("const_set")
        ctx_in, ctx_mm, ctx_act, ctx_step, cast_in = (sem("ctx_in"), sem("ctx_mm"), sem("ctx_act"), sem("ctx_step"),
                                                      sem("cast_in"))
        x_in, q_in, x2_out, x3_out = sem("x_in"), sem("q_in"), sem("x2_out"), sem("x3_out")
        filled, act_read, dve_read = sem("filled"), sem("act_read"), sem("dve_read")
        relu_set, heads_used = sem("relu_set"), sem("heads_used")
        num_full, num_taken = sem("num_full"), sem("num_taken")
        den_set, rec_set = sem("den_set"), sem("rec_set")
        norm_hi, norm_lo = sem("norm_hi"), sem("norm_lo")
        xb_set, stats_set, aggr_set, var_set = sem("xb_set"), sem("stats_set"), sem("aggr_set"), sem("var_set")
        rstd_set, xn_set, mx_set = sem("rstd_set"), sem("xn_set"), sem("mx_set")

        raw = [(a["features"].rearrange("p (g f) -> p g f", g=G), f_w, ring[:, 0:4]),
               (a["w_out"].rearrange("(c p) n -> p c n", p=P), wo1, ring[:, 4:8]),
               (a["WqT"].rearrange("(c p) n -> p c n", p=P), wq, x[:]),
               (a["WoT"].rearrange("(c p) n -> p c n", p=P), wo2, num[:])]
        CTXW = P + KPAD + P
        ctx_t = num[:].rearrange("p g t -> p (g t)")[:, 0:C * CTXW].rearrange("p (c n) -> p c n", c=C)
        wk, wv, bv, tmp = ring[:, 0:4], ring[:, 4:8], ring[:, 8], ring[:, 9]
        CTX_STEPS = 6 * G + 2 + G
        CTX_IN = 64
        bk_of = lambda key: bank[T.bank(key)]

        with nc.Block() as block:
            @block.sync
            def _(sp):
                for src, _, stage in raw:
                    sp.dma_start(stage, src).then_inc(w_in, 16)
                for dst, src in ((bq, "bqT"), (bk, "bkT"), (small, "small")):
                    sp.dma_start(dst[:], a[src]).then_inc(const_in, 16)
                for dst, src in ((one_col, "one_col"), (rem_ones, "rem_ones"), (spread, "spread")):
                    sp.dma_start(dst[:].rearrange("p g n -> p (g n)"), a[src]).then_inc(const_in, 16)
                sp.dma_start(bias1[:], a["b_out"].broadcast_to([P, D])).then_inc(const_in, 16)
                sp.dma_start(bias2[:], a["bo"].broadcast_to([P, D])).then_inc(const_in, 16)
                sp.dma_start(qt[:].bitcast(F32).rearrange("p s c t -> p (s c t)"), q_dram[0]).then_inc(q_in, 16)

                def block_io(i, more):
                    sp.wait_ge(x2_out, 16 * i)
                    sp.dma_start(x[:], x_blk[i]).then_inc(x_in, 16)
                    if more:
                        sp.wait_ge(filled, T.n * i + T.filled(("QP", H - 1)))
                        sp.dma_start(qt[:].bitcast(F32).rearrange("p s c t -> p (s c t)"), q_dram[i + 1]).then_inc(q_in, 16)
                    sp.wait_ge(dve_read, T.n_dve * i + T.dve(("O2", TT - 1)))
                    sp.dma_start(x2_dram[i], x[:].rearrange("p t d -> p (t d)")).then_inc(x2_out, 16)
                    sp.wait_ge(dve_read, T.n_dve * i + T.dve(("T2", TT - 1)))
                    sp.dma_start(x3_dram[i], num[:].rearrange("p g t -> p (g t)")).then_inc(x3_out, 16)

                for b in range(NB):
                    if b == 0:
                        sp.wait_ge(w_lo, len(raw))
                        sp.wait_ge(const_set, 2)
                    else:
                        sp.wait_ge(heads_used, 2 * G * BLK * b)
                        sp.wait_ge(x3_out, 16 * BLK * b)
                    sp.dma_start(wk, a["WkT"].rearrange("(c p) n -> p c n", p=P)).then_inc(ctx_in, 16)
                    sp.dma_start(wv, a["WvT"].rearrange("(c p) n -> p c n", p=P)).then_inc(ctx_in, 16)
                    sp.dma_start(bv, a["bv"].broadcast_to([P, D])).then_inc(ctx_in, 16)
                    sp.dma_start(ctx_t, a["ctxT"][b].rearrange("(c p) n -> p c n", p=P)).then_inc(ctx_in, 16)
                    with sp.Fori(0, BLK - 1) as k:
                        block_io(k + BLK * b, True)
                    block_io(BLK * b + BLK - 1, b < NB - 1)
                sp.wait_ge(x2_out, 16 * NB * BLK)
                sp.wait_ge(x3_out, 16 * NB * BLK)

            @block.gpsimd
            def _(pool):
                nc.gpsimd.memset(mxb[:], 0.0).then_inc(const_set, 1)
                pool.dma_start(minus[:].rearrange("p g s n -> p (g s n)"), a["minus"]).then_inc(cast_in, 16)
                pool.dma_start(ident_b[:], a["ident"]).then_inc(cast_in, 16)
                pool.wait_ge(cast_in, 32)
                nc.gpsimd.memset(mx[:], 0.0).then_inc(const_set, 1)
                pool.wait_ge(const_in, 16 * 8)
                bc1 = bias1[:].rearrange("p (o d) -> p o d", o=1).broadcast_to([P, TT, D])
                bc2 = bias2[:].rearrange("p (o d) -> p o d", o=1).broadcast_to([P, TT, D])

                def rstds(i, which):
                    for t in range(TT):
                        pool.wait_ge(var_set, 2 * TT * i + which * TT + t + 1)
                        nc.gpsimd.tensor_tensor(rstd[:, t:t + 1], mv[:, t, 1:2], half[:, 0:1], ALU.pow)\
                            .then_inc(rstd_set, 1)

                with pool.Fori(0, NB * BLK) as i:
                    pool.wait_ge(x_in, 16 * i + 16)
                    nc.gpsimd.tensor_tensor(x[:], x[:], bc1, ALU.add).then_inc(xb_set, 1)
                    rstds(i, 0)
                    pool.wait_ge(xn_set, 2 * TT * i + TT)
                    nc.gpsimd.tensor_tensor(x[:], x[:], bc2, ALU.add).then_inc(xb_set, 1)
                    rstds(i, 1)

            @block.scalar
            def _(act):
                for n, (_, dst, stage) in enumerate(raw):
                    act.wait_ge(w_in, 16 * len(raw))
                    nc.scalar.copy(dst[:, HI], stage).then_inc(w_hi, 1)
                act.wait_ge(const_in, 16 * 8)

                def context(b):
                    for g in range(G):
                        act.wait_ge(ctx_mm, (G + 2) * b + g + 1)
                        if g >= 2:
                            act.wait_ge(ctx_step, CTX_STEPS * b + 6 * (g - 1))
                        nc.scalar.activation(kt[:, g % 2], bank[g % 2][:, 0:P + KPAD], ACT.Identity,
                                             bias=bk[:, g:g + 1]).then_inc(ctx_act, 1)

                def take_num(i, n):
                    act.wait_ge(num_full, 2 * G * i + n + 1)
                    nc.scalar.copy(num[:, n % G], p_num[n % 2][:]).then_inc(num_taken, 1)

                def split_norm(i, which, dst):
                    for g in range(G):
                        act.wait_ge(dve_read, T.n_dve * i + T.dve(("R%d" % (which + 1), g)))
                        nc.scalar.copy(dst[:, HI, g], num[:, g]).then_inc(norm_hi, 1)

                def block_work(i):
                    act.wait_ge(x3_out, 16 * i)
                    for h in range(H + 1):
                        if h < H:
                            act.wait_ge(filled, T.n * i + T.filled(("QP", h)))
                            if h >= 2:
                                act.wait_ge(dve_read, T.n_dve * i + T.dve(("QP", h - 2)))
                            nc.scalar.activation(ring[:, 8 + h % 2], bk_of(("QP", h))[:], ACT.Relu, scale=-1.0)\
                                .then_inc(relu_set, 1)
                        if h:
                            e = ring[:, 8 + (h - 1) % 2]
                            act.wait_ge(relu_set, H * i + h)
                            nc.scalar.activation(e, e, ACT.Exp, scale=-1.0).then_inc(act_read, 1)
                        if h % HG == HG - 1 and HG < h < H:
                            take_num(i, h // HG - 1)
                    take_num(i, G - 1)
                    split_norm(i, 0, u1)
                    for t in range(TT):
                        act.wait_ge(filled, T.n * i + T.filled(("T1", t)))
                        nc.scalar.copy(u0[:, HI, :, t * P:(t + 1) * P],
                                       bk_of(("T1", t))[:].rearrange("p (c n) -> p c n", c=C)).then_inc(act_read, 1)
                    for g in range(G):
                        act.wait_ge(filled, T.n * i + T.filled(("XQ", g)))
                        nc.scalar.activation(u1[:, HI, g], bk_of(("XQ", g))[:], ACT.Identity,
                                             bias=bq[:, g:g + 1]).then_inc(act_read, 1)
                    act.wait_ge(filled, T.n * i + T.filled(("MT", 0)))
                    nc.scalar.copy(mxt[:], bk_of(("MT", 0))[:].bitcast(BF16)[:, 0:TB]).then_inc(act_read, 1)
                    for n in range(G * SU):
                        act.wait_ge(filled, T.n * i + T.filled(("S", n)))
                        if n >= SLOTS:
                            act.wait_ge(heads_used, 2 * G * i + G + (n - SLOTS) // SU + 1)
                        nc.scalar.activation(ring[:, n % SLOTS], bk_of(("S", n))[:], ACT.Exp,
                                             scale=float(HD) ** -0.5).then_inc(act_read, 1)
                        if n % SU == SU - 1 and n > SU:
                            take_num(i, G + n // SU - 1)
                    take_num(i, 2 * G - 1)
                    split_norm(i, 1, u0)

                for b in range(NB):
                    context(b)
                    with act.Fori(0, BLK) as k:
                        block_work(k + BLK * b)

            @block.vector
            def _(dve):
                for n, (_, dst, stage) in enumerate(raw):
                    dve.wait_ge(w_hi, n + 1)
                    nc.vector.tensor_tensor(dst[:, LO], stage, dst[:, HI].bitcast(F32), ALU.subtract).then_inc(w_lo, 1)
                dve.wait_ge(const_in, 16 * 8)
                dve.wait_ge(const_set, 2)

                own = [0]

                def chain(ins):
                    own[0] += 1
                    ins.then_inc(ctx_step, 1)
                    dve.wait_ge(ctx_step, own[0])

                def context(b):
                    dve.wait_ge(ctx_in, CTX_IN * (b + 1))
                    for g in range(G):
                        dve.wait_ge(ctx_act, G * b + g + 1)
                        for lo, hi, cols in ((0, HG * P, slice(0, P)), (HG * P, HG * P + P, slice(P, P + KPAD))):
                            n = cols.stop - cols.start
                            spread_k = tmp[:, 0:HG * n].rearrange("p (j k) -> p j k", j=HG)
                            k_all = kt[:, g % 2:g % 2 + 1, cols].broadcast_to([P, HG, n])
                            rows = small[:, 0:HG].rearrange("p (j o) -> p j o", o=1).broadcast_to([P, HG, n])
                            chain(nc.vector.tensor_tensor(spread_k, k_all, rows, ALU.mult))
                            chain(nc.vector.tensor_copy(k_w[:, HI, g, lo:hi], tmp[:, 0:HG * n]))
                            chain(nc.vector.tensor_tensor(k_w[:, LO, g, lo:hi], tmp[:, 0:HG * n],
                                                          k_w[:, HI, g, lo:hi].bitcast(F32), ALU.subtract))
                    dve.wait_ge(ctx_mm, (G + 2) * b + G + 1)
                    chain(nc.vector.tensor_tensor(v_w[:], bank[2][:], bv, ALU.add))
                    dve.wait_ge(ctx_mm, (G + 2) * b + G + 2)
                    chain(nc.vector.tensor_tensor(tmp, bank[3][:], bv, ALU.add))
                    rows = small[:, HG:2 * HG].rearrange("p (j o) -> p j o", o=1)
                    for g in range(G):
                        last = nc.vector.tensor_tensor(v_rem[:, g],
                                                       tmp[:, g * P:(g + 1) * P].rearrange("p (j d) -> p j d", j=HG),
                                                       rows.broadcast_to([P, HG, HD]), ALU.mult)
                        chain(last)

                def divide(i, which):
                    dve.wait_ge(heads_used, 2 * G * i + G * (which + 1))
                    op, least = (ALU.add, 1e-8) if which == 0 else (ALU.max, 1e-30)
                    nc.vector.tensor_scalar(den[:, 0], p_den[:], least, None, op).then_inc(den_set, 1)
                    dve.wait_ge(den_set, 2 * i + which + 1)
                    nc.vector.reciprocal(den[:, 1], den[:, 0]).then_inc(rec_set, 1)

                def normalise(i, which, dst):
                    key = "R%d" % (which + 1)
                    for g in range(G + 1):
                        if g < G:
                            dve.wait_ge(num_taken, 2 * G * i + G * which + g + 1)
                            dve.wait_ge(filled, T.n * i + T.filled((key, g)))
                            nc.vector.tensor_tensor(num[:, g], num[:, g], bk_of((key, g))[:], ALU.mult)\
                                .then_inc(dve_read, 1)
                        if g:
                            dve.wait_ge(norm_hi, 2 * G * i + G * which + g)
                            nc.vector.tensor_tensor(dst[:, LO, g - 1], num[:, g - 1], dst[:, HI, g - 1].bitcast(F32),
                                                    ALU.subtract).then_inc(norm_lo, 1)

                def add_out(i, which, t):
                    o = "O%d" % (which + 1)
                    n = 2 * TT * i + TT * which + t + 1
                    if t == 0:
                        dve.wait_ge(xb_set, 2 * i + which + 1)
                    dve.wait_ge(filled, T.n * i + T.filled((o, t)))
                    nc.vector.tensor_tensor(x[:, t], x[:, t], bk_of((o, t))[:], ALU.add).then_inc(dve_read, 1)
                    dve.wait_ge(dve_read, T.n_dve * i + T.dve((o, t)))
                    nc.vector.bn_stats(stats[:, t], x[:, t]).then_inc(stats_set, 1)
                    dve.wait_ge(stats_set, n)
                    nc.vector.tensor_copy(pause[:], bq[:, 0:1])
                    nc.vector.bn_aggr(mv[:, t], stats[:, t]).then_inc(aggr_set, 1)
                    dve.wait_ge(aggr_set, n)
                    nc.vector.tensor_scalar(mv[:, t, 1:2], mv[:, t, 1:2], EPS, None, ALU.add).then_inc(var_set, 1)

                def norm(i, which, t):
                    dve.wait_ge(rstd_set, 2 * TT * i + TT * which + t + 1)
                    if t >= 2:
                        dve.wait_ge(filled, T.n * i + T.filled(("T%d" % (which + 1), t - 2)))
                    nc.vector.tensor_scalar(xn[:, t % 2], x[:, t], mv[:, t, 0:1], rstd[:, t:t + 1],
                                            ALU.subtract, ALU.mult).then_inc(xn_set, 1)

                def turned(i, which, t):
                    part = slice(t * P, (t + 1) * P)
                    key = ("T%d" % (which + 1), t)
                    src = bk_of(key)[:].rearrange("p (c n) -> p c n", c=C)
                    if which == 0:
                        dve.wait_ge(act_read, T.n_act * i + T.act(key))
                        nc.vector.tensor_tensor(u0[:, LO, :, part], src, u0[:, HI, :, part].bitcast(F32),
                                                ALU.subtract).then_inc(dve_read, 1)
                    else:
                        dve.wait_ge(filled, T.n * i + T.filled(key))
                        nc.vector.tensor_copy(num[:, :, part], src).then_inc(dve_read, 1)

                def out_and_norm(i, which):
                    add_out(i, which, 0)
                    add_out(i, which, 1)
                    norm(i, which, 0)
                    add_out(i, which, 2)
                    norm(i, which, 1)
                    turned(i, which, 0)
                    add_out(i, which, 3)
                    norm(i, which, 2)
                    turned(i, which, 1)
                    norm(i, which, 3)
                    turned(i, which, 2)
                    turned(i, which, 3)

                def block_work(i):
                    for h in range(H):
                        if h >= 8:
                            dve.wait_ge(heads_used, 2 * G * i + h // HG - 1)
                        dve.wait_ge(act_read, T.n_act * i + T.act(("QP", h)))
                        nc.vector.scalar_tensor_tensor(ring[:, h % 8], bk_of(("QP", h))[:], 0.0,
                                                       ring[:, 8 + h % 2], ALU.max, ALU.add).then_inc(dve_read, 1)
                    divide(i, 0)
                    normalise(i, 0, u1)
                    out_and_norm(i, 0)
                    for g in range(G):
                        dve.wait_ge(act_read, T.n_act * i + T.act(("XQ", g)))
                        nc.vector.scalar_tensor_tensor(u1[:, LO, g], bk_of(("XQ", g))[:], bq[:, g:g + 1],
                                                       u1[:, HI, g].bitcast(F32), ALU.add, ALU.subtract)\
                            .then_inc(dve_read, 1)
                    for t in range(TT):
                        for g in range(G + 1):
                            key = ("MX", t, g)
                            dve.wait_ge(filled, T.n * i + T.filled(key))
                            if g < G:
                                dst, src = mx[:, 0, t, g * HG:(g + 1) * HG], bk_of(key)[:].rearrange("p (h k) -> p h k", h=HG)
                            else:
                                dst, src = mx[:, 1, t], bk_of(key)[:].rearrange("p (h k) -> p h k", h=H)
                            nc.vector.tensor_reduce(dst, src, AX.X, ALU.max).then_inc(dve_read, 1)
                    dve.wait_ge(dve_read, T.n_dve * i + T.dve(("MX", TT - 1, G)))
                    nc.vector.tensor_tensor(mx[:, 0], mx[:, 0], mx[:, 1], ALU.max).then_inc(mx_set, 1)
                    dve.wait_ge(mx_set, 3 * i + 1)
                    nc.vector.tensor_copy(mxb[:, :, 0:H], mx[:, 0]).then_inc(mx_set, 1)
                    dve.wait_ge(mx_set, 3 * i + 2)
                    nc.vector.tensor_tensor(mxb[:, :, H:2 * H], mx[:, 0], mxb[:, :, 0:H], ALU.subtract)\
                        .then_inc(mx_set, 1)
                    divide(i, 1)
                    normalise(i, 1, u0)
                    out_and_norm(i, 1)

                for b in range(NB):
                    context(b)
                    with dve.Fori(0, BLK) as k:
                        block_work(k + BLK * b)

            @block.tensor
            def _(pe):
                def dve_has_read(i, key):
                    pe.wait_ge(dve_read, T.n_dve * i + T.dve(key))

                def act_has_read(i, key):
                    pe.wait_ge(act_read, T.n_act * i + T.act(key))

                def bank_free(i, key):
                    before = T.before(key)
                    if before is None:
                        if T.pos[key] == 0:
                            pe.wait_ge(act_read, T.n_act * i)
                            pe.wait_ge(dve_read, T.n_dve * i)
                    elif before[2]:
                        dve_has_read(i, before[0])
                    else:
                        act_has_read(i, before[0])

                def three(out, pairs):
                    n = 0
                    for stationary, moving in pairs:
                        for s, m in PASSES:
                            mm = nc.tensor.matmul(out, stationary(s), moving(m), start=(n == 0),
                                                  stop=(n == 3 * len(pairs) - 1))
                            n += 1
                    return mm

                def context(b):
                    pe.wait_ge(ctx_in, CTX_IN * (b + 1))
                    if b:
                        pe.wait_ge(act_read, T.n_act * BLK * b)
                        pe.wait_ge(dve_read, T.n_dve * BLK * b)
                    for g in range(G):
                        if g >= 2:
                            pe.wait_ge(ctx_act, G * b + g - 1)
                        for c in range(C):
                            mm = nc.tensor.matmul(bank[g % 2][:, 0:P + KPAD], wk[:, c, g * P:(g + 1) * P],
                                                  ctx_t[:, c, 0:P + KPAD], start=(c == 0), stop=(c == C - 1))
                        mm.then_inc(ctx_mm, 1)
                    for n, lo in ((2, 0), (3, P + KPAD)):
                        for c in range(C):
                            mm = nc.tensor.matmul(bank[n][:], ctx_t[:, c, lo:lo + P], wv[:, c], start=(c == 0),
                                                  stop=(c == C - 1))
                        mm.then_inc(ctx_mm, 1)
                    pe.wait_ge(ctx_step, CTX_STEPS * (b + 1))

                def use_heads(i, n, slots, num_w, den_w, rest):
                    if n >= 2:
                        pe.wait_ge(num_taken, 2 * G * i + n - 1)
                    else:
                        pe.wait_ge(num_taken, 2 * G * i)
                    g = n % G
                    last = rest is None
                    for j in range(HG):
                        mm = nc.tensor.matmul(p_num[n % 2][j * HD:(j + 1) * HD, :], num_w(g, j), slots[j],
                                              start=True, stop=last, skip_group_check=True)
                    if rest is not None:
                        mm = nc.tensor.matmul(p_num[n % 2][:], rest[0], slots[HG], start=False, stop=True,
                                              skip_group_check=True)
                    mm.then_inc(num_full, 1)
                    if g == 0:
                        pe.wait_ge(den_set, 2 * i + n // G)
                    for j in range(HG):
                        mm = nc.tensor.matmul(p_den[j * HD:(j + 1) * HD, :], den_w(g, j), slots[j],
                                              start=(g == 0), stop=(last and g == G - 1), skip_group_check=True)
                    if rest is not None:
                        mm = nc.tensor.matmul(p_den[:], rest[1], slots[HG], start=False, stop=(g == G - 1),
                                              skip_group_check=True)
                    mm.then_inc(heads_used, 1)

                def spread_den(i, which):
                    pe.wait_ge(rec_set, 2 * i + which + 1)
                    for g in range(G):
                        key = ("R%d" % (which + 1), g)
                        bank_free(i, key)
                        nc.tensor.matmul(bk_of(key)[:], spread[:, g], den[:, 1], start=True, stop=True)\
                            .then_inc(filled, 1)

                def out_proj(i, which, t, u, w):
                    key = ("O%d" % (which + 1), t)
                    bank_free(i, key)
                    if t == 0:
                        pe.wait_ge(norm_lo, 2 * G * i + G * (which + 1))
                    three(bk_of(key)[:], [(lambda s, g=g: u[:, s, g, t * P:(t + 1) * P], lambda m, g=g: w[:, m, g])
                                          for g in range(G)]).then_inc(filled, 1)

                def turn(i, which, t):
                    key = ("T%d" % (which + 1), t)
                    bank_free(i, key)
                    pe.wait_ge(xn_set, 2 * TT * i + TT * which + t + 1)
                    for c in range(C):
                        mm = nc.tensor.transpose(bk_of(key)[:, c * P:(c + 1) * P], xn[:, t % 2, c * P:(c + 1) * P],
                                                 ident[:])
                    mm.then_inc(filled, 1)

                def out_and_turn_work(i, which, u, w):
                    out_proj(i, which, 0, u, w)
                    out_proj(i, which, 1, u, w)
                    out_proj(i, which, 2, u, w)
                    turn(i, which, 0)
                    out_proj(i, which, 3, u, w)
                    turn(i, which, 1)
                    turn(i, which, 2)
                    turn(i, which, 3)

                def block_work(b, i):
                    def attend_group(g):
                        dve_has_read(i, ("QP", HG * g + HG - 1))
                        use_heads(i, g, [ring[:, (HG * g + j) % 8] for j in range(HG)],
                                  lambda g, j: kv_w[:, b, HG * g + j], lambda g, j: ks_w[:, b, HG * g + j], None)

                    pe.wait_ge(q_in, 16 * i + 16)
                    for h in range(H):
                        g, j = h // HG, h % HG
                        bank_free(i, ("QP", h))
                        three(bk_of(("QP", h))[:], [(lambda s: f_w[:, s, g, j * F:(j + 1) * F],
                                                     lambda m: qt[:, m, g])]).then_inc(filled, 1)
                        if j == HG - 1 and g:
                            attend_group(g - 1)
                    attend_group(G - 1)
                    spread_den(i, 0)
                    out_and_turn_work(i, 0, u1, wo1)
                    for g in range(G):
                        key = ("XQ", g)
                        bank_free(i, key)
                        if g == 0:
                            dve_has_read(i, ("T1", TT - 1))
                        three(bk_of(key)[:], [(lambda s, c=c: wq[:, s, c, g * P:(g + 1) * P],
                                               lambda m, c=c: u0[:, m, c]) for c in range(C)]).then_inc(filled, 1)
                    for t in range(TT):
                        part = slice(t * P, (t + 1) * P)
                        for g in range(G):
                            key = ("MX", t, g)
                            bank_free(i, key)
                            if t == 0:
                                act_has_read(i, ("XQ", g))
                            nc.tensor.matmul(bk_of(key)[:], u1[:, HI, g, part], k_w[:, HI, g, 0:HG * P],
                                             start=True, stop=True).then_inc(filled, 1)
                        key = ("MX", t, G)
                        bank_free(i, key)
                        for g in range(G):
                            mm = nc.tensor.matmul(bk_of(key)[:, g * P:(g + 1) * P], u1[:, HI, g, part],
                                                  k_w[:, HI, g, HG * P:HG * P + P], start=(g == 0), stop=(g == G - 1),
                                                  skip_group_check=True)
                        mm.then_inc(filled, 1)

                    def scores(n):
                        g, j = n // SU, n % SU
                        bank_free(i, ("S", n))
                        if n == 0:
                            dve_has_read(i, ("XQ", G - 1))
                        for q, (s, m) in enumerate(PASSES):
                            nc.tensor.matmul(bk_of(("S", n))[:], k_w[:, s, g, j * P:(j + 1) * P], u1[:, m, g],
                                             start=(q == 0), stop=False)

                    def shift(n):
                        nc.tensor.matmul(bk_of(("S", n))[:], minus[:, n // SU, n % SU], mxt[:], start=False,
                                         stop=True).then_inc(filled, 1)

                    def cross_group(g):
                        act_has_read(i, ("S", SU * g + SU - 1))
                        use_heads(i, G + g, [ring[:, (SU * g + j) % SLOTS] for j in range(SU)],
                                  lambda g, j: v_w[:, (HG * g + j) * HD:(HG * g + j + 1) * HD],
                                  lambda g, j: one_col[:, g],
                                  (v_rem[:, g].rearrange("p j d -> p (j d)"), rem_ones[:, g]))

                    EARLY = 3
                    for n in range(EARLY):
                        scores(n)
                    bank_free(i, ("MT", 0))
                    pe.wait_ge(mx_set, 3 * i + 3)
                    for t in range(TT):
                        mm = nc.tensor.transpose(bk_of(("MT", 0))[:].bitcast(BF16)[:, t * P:(t + 1) * P], mxb[:, t],
                                                 ident_b[:])
                    mm.then_inc(filled, 1)
                    act_has_read(i, ("MT", 0))
                    for n in range(G * SU):
                        if n >= EARLY:
                            scores(n)
                        shift(n)
                        if n % SU == SU - 1 and n > SU:
                            cross_group(n // SU - 1)
                    cross_group(G - 1)
                    spread_den(i, 1)
                    out_and_turn_work(i, 1, u0, wo2)

                pe.wait_ge(const_in, 16 * 8)
                pe.wait_ge(const_set, 2)
                for b in range(NB):
                    context(b)
                    with pe.Fori(0, BLK) as k:
                        block_work(b, k + BLK * b)


def experts(nc, a, NB, BLK, x2_dram, x3_dram, out_bat, ident):
    NT = BLK * TT
    WG, WU, WD = 0, C * FE, 2 * C * FE
    WN = 2 * C * FE + FT * D
    with ExitStack() as ctx:
        def sb(name, shape, dt=F32):
            return ctx.enter_context(nc.sbuf_tensor("ex_" + name, shape, dt))

        def sem(name):
            return ctx.enter_context(nc.semaphore("ex_" + name))

        x3 = sb("x3", [P, 2, BLK, C * TB], F32R)
        acc = sb("acc", [P, NT, D])
        w_raw = sb("w_raw", [P, WN])
        w = sb("w", [P, 2, 2, WN], F32R)
        s_g = sb("s_g", [P, FT, TB])
        h = sb("h", [P, FT, TB])
        ht = sb("ht", [P, 2, 2, FT, TB], F32R)
        r_raw = sb("r_raw", [P, C, P])
        r_w = sb("r_w", [P, 2, C, P], F32R)
        lt = sb("lt", [P, NT, E])
        total = sb("total", [P, NT])
        top = sb("top", [P, NT])
        ex = sb("ex", [P, NT, E])
        gt = sb("gt", [P, NT, E, E])
        lower = sb("lower", [P, E * E])
        rank = sb("rank", [P, NT, E])
        rank2 = sb("rank2", [P, NT, E])
        share = sb("share", [P, NT, UNITS])
        pg = [ctx.enter_context(nc.psum_tensor(f"ex_pg{n}", [P, 512], F32)) for n in range(2 * FT)]
        pd = [ctx.enter_context(nc.psum_tensor(f"ex_pd{n}", [P, 512], F32)) for n in range(4)]

        x3_in, x3_hi, x3_lo = [sem("x3_in0"), sem("x3_in1")], sem("x3_hi"), sem("x3_lo")
        acc_in, const_in, out_done = sem("acc_in"), sem("const_in"), sem("out_done")
        w_in, w_hi, w_lo = sem("w_in"), sem("w_hi"), sem("w_lo")
        r_hi, r_lo = sem("r_hi"), sem("r_lo")
        lg_full, lg_taken, lt_full, lt_taken = sem("lg_full"), sem("lg_taken"), sem("lt_full"), sem("lt_taken")
        own, exp_set, share_set = sem("own"), sem("exp_set"), sem("share_set")
        OWN = 13
        gu_full, silu_set, h_set, ht_hi, ht_lo = (sem("gu_full"), sem("silu_set"), sem("h_set"), sem("ht_hi"),
                                                  sem("ht_lo"))
        d_full, d_taken = sem("d_full"), sem("d_taken")

        PAIRS = UNITS // 2
        STEPS = 2 * BLK
        stage = (s_g[:].rearrange("p f t -> p (f t)"), h[:].rearrange("p f t -> p (f t)"))
        HALF = FT * TB
        NX = BLK * C * TB // HALF
        lg = [stage[k // 2][0:E, (k % 2) * TB:(k % 2 + 1) * TB] for k in range(BLK)]

        with nc.Block() as block:
            @block.sync
            def _(sp):
                sp.dma_start(r_raw[:], a["router"].rearrange("(c p) n -> p c n", p=P)).then_inc(const_in, 16)
                sp.dma_start(lower[:], a["lower"]).then_inc(const_in, 16)
                for b in range(NB):
                    if b:
                        sp.wait_ge(d_taken, PAIRS * STEPS * TT * b)
                    for n in range(NX):
                        k, part = n // 2, n % 2
                        if n >= 2:
                            sp.wait_ge(x3_lo, NX * b + n - 1)
                        sp.dma_start(stage[n % 2], x3_dram[b * BLK + k][:, part * HALF:(part + 1) * HALF])\
                            .then_inc(x3_in[n % 2], 16)
                    if b == 0:
                        sp.dma_start(w_raw[:], a["units"][0]).then_inc(w_in, 16)
                    else:
                        sp.wait_ge(out_done, 16 * b)
                    sp.dma_start(acc[:].rearrange("p (k t) d -> p k (t d)", k=BLK),
                                 x2_dram[b * BLK:(b + 1) * BLK].rearrange("k p n -> p k n")).then_inc(acc_in, 16)
                    with sp.Fori(0, UNITS) as e:
                        sp.wait_ge(w_lo, e + (b * UNITS + 1))
                        sp.dma_start(w_raw[:], a["units"][e + 1]).then_inc(w_in, 16)
                    sp.wait_ge(d_taken, PAIRS * STEPS * TT * (b + 1))
                    sp.dma_start(out_bat[b], acc[:]).then_inc(out_done, 16)
                sp.wait_ge(out_done, 16 * NB)

            @block.gpsimd
            def _(pool):
                nc.gpsimd.memset(share[:], 1.0).then_inc(share_set, 1)

            @block.scalar
            def _(act):
                act.wait_ge(const_in, 32)
                nc.scalar.copy(r_w[:, HI], r_raw[:]).then_inc(r_hi, 1)
                for b in range(NB):
                    if b:
                        act.wait_ge(gu_full, 2 * FT * STEPS * PAIRS * b)
                    for n in range(NX):
                        k, part = n // 2, n % 2
                        act.wait_ge(x3_in[n % 2], 16 * (NX // 2 * b + n // 2 + 1))
                        nc.scalar.copy(x3[:, HI, k, part * HALF:(part + 1) * HALF], stage[n % 2]).then_inc(x3_hi, 1)
                    if b == 0:
                        act.wait_ge(w_in, 16)
                        nc.scalar.copy(w[:, 0, HI], w_raw[:]).then_inc(w_hi, 1)
                    act.wait_ge(own, OWN * b + 2)
                    nc.scalar.activation(ex[:], ex[:], ACT.Exp).then_inc(exp_set, 1)
                    with act.Fori(0, PAIRS) as p:
                        q = p + b * PAIRS
                        for s in range(STEPS):
                            step = q * STEPS + s
                            for f in range(FT):
                                act.wait_ge(gu_full, step * (2 * FT) + 2 * f + 1)
                                act.wait_ge(h_set, step * FT + (f + 1 - FT if s else 0))
                                nc.scalar.activation(s_g[:, f], pg[2 * f][:], ACT.Silu).then_inc(silu_set, 1)
                            for f in range(FT):
                                act.wait_ge(h_set, step * FT + f + 1)
                                nc.scalar.copy(ht[:, s % 2, HI, f], h[:, f]).then_inc(ht_hi, 1)
                            if s == 1:
                                act.wait_ge(w_in, q * 32 + 32)
                                nc.scalar.copy(w[:, 1, HI], w_raw[:]).then_inc(w_hi, 1)
                            if s == BLK + 1:
                                act.wait_ge(w_in, q * 32 + 48)
                                nc.scalar.copy(w[:, 0, HI], w_raw[:]).then_inc(w_hi, 1)

            @block.vector
            def _(dve):
                dve.wait_ge(r_hi, 1)
                nc.vector.tensor_tensor(r_w[:, LO], r_raw[:], r_w[:, HI].bitcast(F32), ALU.subtract).then_inc(r_lo, 1)

                def split_w(slot, n):
                    dve.wait_ge(w_hi, n)
                    nc.vector.tensor_tensor(w[:, slot, LO], w_raw[:], w[:, slot, HI].bitcast(F32),
                                            ALU.subtract).then_inc(w_lo, 1)

                def router(b):
                    dve.wait_ge(x3_lo, NX * (b + 1))
                    for k in range(BLK):
                        dve.wait_ge(lg_full, BLK * b + k + 1)
                        nc.vector.tensor_copy(lg[k], pg[k][0:E, :]).then_inc(lg_taken, 1)
                    dve.wait_ge(lt_full, b + 1)
                    nc.vector.tensor_copy(lt[:].rearrange("p n e -> p (n e)"), pd[0][:, 0:NT * E]).then_inc(lt_taken, 1)
                    dve.wait_ge(lt_taken, b + 1)
                    count = [OWN * b]

                    def chain(ins):
                        count[0] += 1
                        ins.then_inc(own, 1)
                        dve.wait_ge(own, count[0])

                    per_e = lt[:].rearrange("p n (e o) -> p n e o", o=1).broadcast_to([P, NT, E, E])
                    per_f = lt[:].rearrange("p n (o e) -> p n o e", o=1).broadcast_to([P, NT, E, E])
                    low = lower[:].rearrange("p (o n) -> p o n", o=1).broadcast_to([P, NT, E * E])
                    gt_flat = gt[:].rearrange("p n e f -> p n (e f)")
                    per_n = lambda t: t[:].rearrange("p (n o) -> p n o", o=1).broadcast_to([P, NT, E])
                    chain(nc.vector.tensor_reduce(top[:], lt[:], AX.X, ALU.max))
                    chain(nc.vector.tensor_tensor(ex[:], lt[:], per_n(top), ALU.subtract))
                    chain(nc.vector.tensor_tensor(gt[:], per_f, per_e, ALU.is_gt))
                    chain(nc.vector.tensor_reduce(rank[:], gt[:], AX.X, ALU.add))
                    chain(nc.vector.tensor_tensor(gt[:], per_f, per_e, ALU.is_equal))
                    chain(nc.vector.tensor_tensor(gt_flat, gt_flat, low, ALU.mult))
                    chain(nc.vector.tensor_reduce(rank2[:], gt[:], AX.X, ALU.add))
                    chain(nc.vector.tensor_tensor(rank[:], rank[:], rank2[:], ALU.add))
                    chain(nc.vector.tensor_scalar(rank[:], rank[:], TOP - 0.5, None, ALU.is_lt))
                    dve.wait_ge(exp_set, b + 1)
                    chain(nc.vector.tensor_reduce(top[:], ex[:], AX.X, ALU.add))
                    chain(nc.vector.reciprocal(total[:], top[:]))
                    chain(nc.vector.tensor_tensor(ex[:], ex[:], per_n(total), ALU.mult))
                    chain(nc.vector.tensor_tensor(share[:, :, 0:E], ex[:], rank[:], ALU.mult))
                    assert count[0] == OWN * (b + 1)

                def add_down(e, step, s):
                    k = s % BLK
                    for t in range(TT):
                        n = k * TT + t
                        dve.wait_ge(d_full, step * TT + t + 1)
                        nc.vector.scalar_tensor_tensor(acc[:, n], pd[t][:], share[:, n, bass.ds(e + s // BLK, 1)],
                                                       acc[:, n], ALU.mult, ALU.add).then_inc(d_taken, 1)

                for b in range(NB):
                    for n in range(NX):
                        k, part = n // 2, slice((n % 2) * HALF, (n % 2 + 1) * HALF)
                        dve.wait_ge(x3_hi, NX * b + n + 1)
                        nc.vector.tensor_tensor(x3[:, LO, k, part], stage[n % 2], x3[:, HI, k, part].bitcast(F32),
                                                ALU.subtract).then_inc(x3_lo, 1)
                    if b == 0:
                        split_w(0, 1)
                        dve.wait_ge(share_set, 1)
                    router(b)
                    dve.wait_ge(acc_in, 16 * (b + 1))
                    with dve.Fori(0, PAIRS) as p:
                        q = p + b * PAIRS
                        for s in range(STEPS):
                            step = q * STEPS + s
                            for f in range(FT):
                                dve.wait_ge(ht_lo, step * FT + (f + 1 - FT if s else 0))
                                dve.wait_ge(silu_set, step * FT + f + 1)
                                dve.wait_ge(gu_full, step * (2 * FT) + 2 * f + 2)
                                nc.vector.tensor_tensor(h[:, f], s_g[:, f], pg[2 * f + 1][:], ALU.mult).then_inc(h_set, 1)
                            for f in range(FT):
                                dve.wait_ge(ht_hi, step * FT + f + 1)
                                nc.vector.tensor_tensor(ht[:, s % 2, LO, f], h[:, f], ht[:, s % 2, HI, f].bitcast(F32),
                                                        ALU.subtract).then_inc(ht_lo, 1)
                            if s == 1:
                                split_w(1, q * 2 + 2)
                            if s == BLK + 1:
                                split_w(0, q * 2 + 3)
                            if s:
                                add_down(p * 2, step - 1, s - 1)
                        add_down(p * 2, q * STEPS + (STEPS - 1), STEPS - 1)

            @block.tensor
            def _(pe):
                pe.wait_ge(r_lo, 1)

                def router(b):
                    for k in range(BLK):
                        pe.wait_ge(x3_lo, NX * b + 2 * k + 2)
                        if b:
                            pe.wait_ge(h_set, FT * STEPS * PAIRS * b)
                        n = 0
                        for c in range(C):
                            for s, m in PASSES:
                                mm = nc.tensor.matmul(pg[k][:], r_w[:, s, c], x3[:, m, k, c * TB:(c + 1) * TB],
                                                      start=(n == 0), stop=(n == 3 * C - 1))
                                n += 1
                        mm.then_inc(lg_full, 1)
                    pe.wait_ge(lg_taken, BLK * (b + 1))
                    if b:
                        pe.wait_ge(d_taken, PAIRS * STEPS * TT * b)
                    for k in range(BLK):
                        for t in range(TT):
                            n = k * TT + t
                            mm = nc.tensor.transpose(pd[0][:, n * E:(n + 1) * E], lg[k][:, t * P:(t + 1) * P],
                                                     ident[0:E, 0:E])
                    mm.then_inc(lt_full, 1)

                def gate_up(s, step):
                    k, slot = s % BLK, s // BLK
                    for f in range(FT):
                        for which, start in ((0, WG), (1, WU)):
                            pe.wait_ge((silu_set, h_set)[which], step * FT + (f + 1 - FT if s else 0))
                            n = 0
                            for c in range(C):
                                col = start + c * FE + f * P
                                for sp_, m in PASSES:
                                    mm = nc.tensor.matmul(pg[2 * f + which][:], w[:, slot, sp_, col:col + P],
                                                          x3[:, m, k, c * TB:(c + 1) * TB],
                                                          start=(n == 0), stop=(n == 3 * C - 1))
                                    n += 1
                            mm.then_inc(gu_full, 1)

                def down(s, step):
                    slot = s // BLK
                    pe.wait_ge(ht_lo, step * FT + FT)
                    for t in range(TT):
                        pe.wait_ge(d_taken, step * TT + (t + 1 - TT if s else 0))
                        n = 0
                        for f in range(FT):
                            for sp_, m in PASSES:
                                mm = nc.tensor.matmul(pd[t][:], ht[:, s % 2, sp_, f, t * P:(t + 1) * P],
                                                      w[:, slot, m, WD + f * D:WD + (f + 1) * D],
                                                      start=(n == 0), stop=(n == 3 * FT - 1))
                                n += 1
                        mm.then_inc(d_full, 1)

                for b in range(NB):
                    router(b)
                    pe.wait_ge(lt_taken, b + 1)
                    with pe.Fori(0, PAIRS) as p:
                        q = p + b * PAIRS
                        for s in range(STEPS):
                            if s % BLK == 0:
                                pe.wait_ge(w_lo, q * 2 + (s // BLK + 1))
                            gate_up(s, q * STEPS + s)
                            if s:
                                down(s - 1, q * STEPS + (s - 1))
                        down(STEPS - 1, q * STEPS + (STEPS - 1))


def kernel(**inputs):
    import concourse.bacc as bacc
    from concourse.bass_utils import run_bass_kernel_spmd

    f = {k.removeprefix("L0_"): np.asarray(v) for k, v in inputs.items()}
    proj = f["attn_proj_matrix"]
    features = np.zeros((P, G, HG, F), np.float32)
    for h in range(H):
        g, j = h // HG, h % HG
        features[j * HD:(j + 1) * HD, g, j] = proj[h]
    ctx = f["ctx_1024"].transpose(0, 2, 1)
    rest = np.concatenate([ctx[:, :, P:], np.repeat(ctx[:, :, -1:], KPAD - KREM, 2)], 2)
    ctx_t = np.concatenate([ctx[:, :, :P], rest, rest, rest, rest, rest], 2)

    def chunks(w):
        return w.reshape(-1, P, w.shape[1]).transpose(1, 0, 2).reshape(P, -1)

    gates = list(f["ffn_w_gate"]) + np.split(f["ffn_ws_gate"], 2, axis=1)
    ups = list(f["ffn_w_up"]) + np.split(f["ffn_ws_up"], 2, axis=1)
    downs = list(f["ffn_w_down"]) + np.split(f["ffn_ws_down"], 2, axis=0)
    units = [np.concatenate([chunks(g), chunks(u), chunks(d)], 1) for g, u, d in zip(gates, ups, downs)]
    router = np.zeros((D, P), np.float32)
    router[:, :E] = f["ffn_router_w"]
    arrays = {
        "x": f["x"], "w_qkv": f["attn_w_qkv"], "features": features.reshape(P, -1), "w_out": f["attn_w_out"],
        "b_out": f["attn_b_out"].reshape(1, D), "ctxT": ctx_t,
        "WqT": f["xattn_Wq"].T, "WkT": f["xattn_Wk"].T, "WvT": f["xattn_Wv"].T, "WoT": f["xattn_Wo"].T,
        "bqT": f["xattn_bq"].reshape(C, P).T, "bkT": f["xattn_bk"].reshape(C, P).T,
        "bv": f["xattn_bv"].reshape(1, D), "bo": f["xattn_bo"].reshape(1, D),
        "router": router, "units": np.stack(units + units[:1]),
    }
    arrays.update(constants())
    arrays = {"in_" + k: np.ascontiguousarray(v) for k, v in arrays.items()}

    nc = bacc.Bacc("TRN2", target_bir_lowering=False, num_devices=1)
    aps = {k[3:]: nc.dram_tensor(k, v.shape, mybir.dt.from_np(v.dtype), kind="ExternalInput").ap()
           for k, v in arrays.items()}
    out = nc.dram_tensor("out", f["x"].shape, F32, kind="ExternalOutput").ap()
    decoder_kernel(nc, aps, out)
    got = run_bass_kernel_spmd(nc, [arrays], core_ids=[0])
    return got.results[0]["out"]
```

```python
from contextlib import ExitStack

import concourse.bass as bass
import numpy as np
from concourse import mybir

F32 = mybir.dt.float32
F32R = mybir.dt.float32r
BF16 = mybir.dt.bfloat16
ALU = mybir.AluOpType
ACT = mybir.ActivationFunctionType
AX = mybir.AxisListType

P = 128
HI, LO = 0, 1
PASSES = ((HI, HI), (HI, LO), (LO, HI))

D = 512
C = D // P
H = 16
HD = D // H
HG = P // HD
G = H // HG
F = 128
TB = 512
TT = TB // P
KEYS = 154
KREM = KEYS - P
KPAD = 32
E = 8
TOP = 6
FE = 256
UNITS = E + 2
FT = FE // P
EPS = 1e-5


def primed(ctx, nc, sems, name):
    sems.append(ctx.enter_context(nc.semaphore(name)))
    return sems[-1]


def prime(nc, pause, sems):
    with nc.Block() as block:
        @block.gpsimd
        def _(pool):
            for s in sems:
                pool.sem_inc(s, 1)


class Tally:

    def __init__(self, jobs, banks):
        self.pos = {key: n for n, (key, _, _) in enumerate(jobs)}
        self.jobs, self.banks, self.n = jobs, banks, len(jobs)
        self.n_act = sum(a for _, a, _ in jobs)
        self.n_dve = sum(d for _, _, d in jobs)

    def filled(self, key):
        return self.pos[key] + 1

    def act(self, key):
        return sum(a for _, a, _ in self.jobs[:self.pos[key] + 1])

    def dve(self, key):
        return sum(d for _, _, d in self.jobs[:self.pos[key] + 1])

    def bank(self, key):
        return self.pos[key] % self.banks

    def before(self, key):
        n = self.pos[key] - self.banks
        return self.jobs[n] if n >= 0 else None


def constants():
    ident = np.eye(P, dtype=np.float32)
    quad = np.arange(P) // HD
    key = np.arange(P) % HD
    mask = (quad[:, None] == np.arange(HG)).astype(np.float32)
    mask_keys = mask * (key < KREM)[:, None]
    one_col = np.zeros((P, G, HD), np.float32)
    rem_ones = np.zeros((P, G, P), np.float32)
    spread = np.zeros((P, G, P), np.float32)
    for g in range(G):
        one_col[:, g, g] = 1
        for p in range(P):
            if key[p] < KREM:
                rem_ones[p, g, 32 * quad[p] + g] = 1
            spread[32 * quad[p] + g, g, p] = 1
    minus = np.zeros((P, G, HG + 1, P), np.float32)
    for g in range(G):
        for j in range(HG):
            for r in (HG * g + j, H + HG * g + j):
                minus[r, g, j, :] = -1
                minus[r, g, HG, 32 * j:32 * j + 32] = -1
    lower = np.zeros((P, E, E), np.float32)
    for e in range(E):
        lower[:, e, :e] = 1
    small = np.concatenate([mask, mask_keys], 1)
    return {
        "ident": ident, "small": small, "one_col": one_col.reshape(P, -1), "rem_ones": rem_ones.reshape(P, -1),
        "spread": spread.reshape(P, -1), "minus": minus.reshape(P, -1), "lower": lower.reshape(P, -1),
    }


def decoder_kernel(nc, a, out):
    NB = a["x"].shape[0]
    BLK = a["x"].shape[1] // TB
    NBLK = NB * BLK
    x_blk = a["x"].rearrange("b (k t p) d -> (b k) p t d", t=TT, p=P)
    out_bat = out.rearrange("b (n p) d -> b p n d", p=P)
    x2_dram = nc.dram_tensor("x2_scratch", [NBLK, P, TT * D], F32).ap()
    q_dram = nc.dram_tensor("q_scratch", [NBLK, 2, HD, H * TB], F32).ap()
    x1_dram = nc.dram_tensor("x1_scratch", [NBLK, P, TT * D], F32).ap()
    xq_dram = nc.dram_tensor("xq_scratch", [NBLK, P, C * TB], F32).ap()
    x3_dram = nc.dram_tensor("x3_scratch", [NBLK, P, C * TB], F32).ap()

    with ExitStack() as whole:
        ident = whole.enter_context(nc.sbuf_tensor("ident", [P, P], F32))
        half = whole.enter_context(nc.sbuf_tensor("half", [P, TT], F32))
        with ExitStack() as linear:
            kv_w = linear.enter_context(nc.sbuf_tensor("kv_w", [P, NB, H, HD], F32))
            ks_w = linear.enter_context(nc.sbuf_tensor("ks_w", [P, NB, H, HD], F32))
            project(nc, a, NBLK, BLK, x_blk, q_dram, ident, kv_w, ks_w, half)
            attend_linear(nc, a, NBLK, BLK, x_blk, q_dram, x1_dram, xq_dram, ident, kv_w, ks_w, half)
        attend_cross(nc, a, NB, BLK, x1_dram, xq_dram, x2_dram, x3_dram, ident, half)
        experts(nc, a, NB, BLK, x2_dram, x3_dram, out_bat, ident)


def project(nc, a, NBLK, BLK, x_blk, q_dram, ident, kv_w, ks_w, half):
    T = Tally([(("T", t), 1, 1) for t in range(TT)] + [(("K", g), 1, 1) for g in range(G)]
              + [(("Q", g), 1, 1) for g in range(G)] + [(("V", t), 0, 1) for t in range(TT)]
              + [(("KP", n), 1, 1) for n in range(TT * G)], 2)
    NKP = TT * G
    LAG = 3
    with ExitStack() as ctx:
        def sb(name, shape, dt=F32):
            return ctx.enter_context(nc.sbuf_tensor("pr_" + name, shape, dt))

        def sem(name):
            return primed(ctx, nc, sems, "pr_" + name)

        sems = []

        w_raw = sb("w_raw", [P, C, 3 * D])
        w = sb("w", [P, 2, C, 3 * D], F32R)
        f_raw = sb("f_raw", [P, G, HG * F])
        f_w = sb("f_w", [P, 2, G, HG * F], F32R)
        x = sb("x", [P, TT, D])
        xn = sb("xn", [P, TT, D])
        xt = sb("xt", [P, 2, C, TB], F32R)
        kt = sb("kt", [P, 2, C, TB], F32R)
        qs = sb("qs", [P, 2, C, TB], F32R)
        v = sb("v", [P, TT, D])
        e = sb("e", [P, 4, HG * F])
        kp = sb("kp", [P, 4, HG * F])
        stats = sb("stats", [P, TT, 6])
        mv = sb("mv", [P, TT, 2])
        rstd = sb("rstd", [P, TT])
        pause = sb("pause", [P, 1])
        ones = sb("ones", [P, HD])
        kv_sum = sb("kv_sum", [P, NBLK // BLK, G * F])
        ks_sum = sb("ks_sum", [P, NBLK // BLK, HG * F])
        pj = [ctx.enter_context(nc.psum_tensor(f"pr_pj{n}", [P, 512], F32)) for n in range(2)]
        pk = [ctx.enter_context(nc.psum_tensor(f"pr_pk{n}", [P, 512], F32)) for n in range(4)]
        p_kv = ctx.enter_context(nc.psum_tensor("pr_p_kv", [P, 512], F32))
        p_ks = ctx.enter_context(nc.psum_tensor("pr_p_ks", [P, 512], F32))

        w_in, x_in, q_out = sem("w_in"), sem("x_in"), sem("q_out")
        const_in, const_set = sem("const_in"), sem("const_set")
        w_hi, w_lo = sem("w_hi"), sem("w_lo")
        filled, act_read, dve_read = sem("filled"), sem("act_read"), sem("dve_read")
        stats_set, var_set, rstd_set, xn_set = sem("stats_set"), sem("var_set"), sem("rstd_set"), sem("xn_set")
        relu_set, kv_step, kv_taken = sem("relu_set"), sem("kv_step"), sem("kv_taken")
        turned, kv_done = sem("turned"), sem("kv_done")

        prime(nc, pause, sems)

        def bank_of(key):
            return pk[key[1] % 4] if key[0] == "KP" else pj[T.bank(key)]

        with nc.Block() as block:
            @block.sync
            def _(sp):
                sp.dma_start(x[:], x_blk[0]).then_inc(x_in, 16)
                sp.dma_start(ident[:], a["ident"]).then_inc(const_in, 16)
                w_src = a["w_qkv"].rearrange("(c p) n -> p c n", p=P)
                for c in range(C):
                    sp.dma_start(w_raw[:, c], w_src[:, c]).then_inc(w_in, 16)
                sp.dma_start(f_raw[:], a["features"].rearrange("p (g f) -> p g f", g=G)).then_inc(w_in, 16)

                def block_io(i, last):
                    if not last:
                        sp.wait_ge(xn_set, 1 + TT * i + TT)
                        sp.dma_start(x[:], x_blk[i + 1]).then_inc(x_in, 16)
                    sp.wait_ge(dve_read, 1 + T.n_dve * i + T.dve(("Q", G - 1)))
                    for s in (HI, LO):
                        for j in range(HG):
                            sp.dma_start(q_dram[i, s].rearrange("d (g j t) -> d g j t", g=G, j=HG)[:, :, j],
                                         qs[j * HD:(j + 1) * HD, s].bitcast(F32)).then_inc(q_out, 16)

                with sp.Fori(0, NBLK - 1) as i:
                    block_io(i, False)
                block_io(NBLK - 1, True)
                sp.wait_ge(q_out, 1 + 16 * 2 * HG * NBLK)

            @block.gpsimd
            def _(pool):
                nc.gpsimd.memset(half[:], -0.5).then_inc(const_set, 1)
                nc.gpsimd.memset(ones[:], 1.0).then_inc(const_set, 1)
                nc.gpsimd.memset(ks_w[:], 0.0).then_inc(const_set, 1)
                nc.gpsimd.memset(kv_sum[:], 0.0).then_inc(const_set, 1)
                nc.gpsimd.memset(ks_sum[:], 0.0).then_inc(const_set, 1)
                pool.wait_ge(const_set, 2)
                with pool.Fori(0, NBLK) as i:
                    pool.wait_ge(var_set, 1 + i + 1)
                    nc.gpsimd.tensor_tensor(rstd[:], mv[:, :, 1], half[:], ALU.pow).then_inc(rstd_set, 1)

            @block.scalar
            def _(act):
                for c in range(C):
                    act.wait_ge(w_in, 1 + 16 * (C + 1))
                    nc.scalar.copy(w[:, HI, c], w_raw[:, c]).then_inc(w_hi, 1)
                nc.scalar.copy(f_w[:, HI], f_raw[:]).then_inc(w_hi, 1)

                def turn(i):
                    for t in range(TT):
                        act.wait_ge(filled, 1 + T.n * i + T.filled(("T", t)))
                        nc.scalar.copy(xt[:, HI, :, t * P:(t + 1) * P],
                                       bank_of(("T", t))[:].rearrange("p (c n) -> p c n", c=C)).then_inc(act_read, 1)

                def heads(i):
                    for g in range(G):
                        act.wait_ge(filled, 1 + T.n * i + T.filled(("K", g)))
                        nc.scalar.copy(kt[:, HI, g], bank_of(("K", g))[:]).then_inc(act_read, 1)
                    act.wait_ge(q_out, 1 + 16 * 2 * HG * i)
                    for g in range(G):
                        act.wait_ge(filled, 1 + T.n * i + T.filled(("Q", g)))
                        nc.scalar.copy(qs[:, HI, g], bank_of(("Q", g))[:]).then_inc(act_read, 1)
                    for n in range(NKP + 1):
                        if n < NKP:
                            act.wait_ge(filled, 1 + T.n * i + T.filled(("KP", n)))
                            nc.scalar.activation(e[:, n % 4], bank_of(("KP", n))[:], ACT.Relu, scale=-1.0)\
                                .then_inc(relu_set, 1)
                        if n:
                            act.wait_ge(relu_set, 1 + NKP * i + n)
                            nc.scalar.activation(e[:, (n - 1) % 4], e[:, (n - 1) % 4], ACT.Exp, scale=-1.0)\
                                .then_inc(act_read, 1)

                turn(0)
                with act.Fori(0, NBLK - 1) as i:
                    heads(i)
                    turn(i + 1)
                heads(NBLK - 1)

            @block.vector
            def _(dve):
                def norm_stats(i, t):
                    if t == 0:
                        dve.wait_ge(x_in, 1 + 16 * i + 16)
                    nc.vector.bn_stats(stats[:, t], x[:, t]).then_inc(stats_set, 1)

                def norm_var(i):
                    dve.wait_ge(stats_set, 1 + TT * i + TT)
                    nc.vector.tensor_copy(pause[:], half[:, 0:1])
                    for t in range(TT):
                        nc.vector.bn_aggr(mv[:, t], stats[:, t]).then_inc(turned, 1)
                    dve.wait_ge(turned, 1 + TT * i + TT)
                    nc.vector.tensor_scalar(mv[:, :, 1], mv[:, :, 1], EPS, None, ALU.add).then_inc(var_set, 1)

                def norm(i):
                    dve.wait_ge(rstd_set, 1 + i + 1)
                    for t in range(TT):
                        nc.vector.tensor_scalar(xn[:, t], x[:, t], mv[:, t, 0:1], rstd[:, t:t + 1],
                                                ALU.subtract, ALU.mult).then_inc(xn_set, 1)

                def turn(i):
                    for t in range(TT):
                        part = slice(t * P, (t + 1) * P)
                        dve.wait_ge(act_read, 1 + T.n_act * i + T.act(("T", t)))
                        nc.vector.tensor_tensor(xt[:, LO, :, part], bank_of(("T", t))[:].rearrange("p (c n) -> p c n", c=C),
                                                xt[:, HI, :, part].bitcast(F32), ALU.subtract).then_inc(dve_read, 1)

                def heads(i, last):
                    for g in range(G):
                        dve.wait_ge(act_read, 1 + T.n_act * i + T.act(("K", g)))
                        nc.vector.tensor_tensor(kt[:, LO, g], bank_of(("K", g))[:], kt[:, HI, g].bitcast(F32),
                                                ALU.subtract).then_inc(dve_read, 1)
                    for g in range(G):
                        dve.wait_ge(act_read, 1 + T.n_act * i + T.act(("Q", g)))
                        nc.vector.tensor_tensor(qs[:, LO, g], bank_of(("Q", g))[:], qs[:, HI, g].bitcast(F32),
                                                ALU.subtract).then_inc(dve_read, 1)
                        if not last:
                            norm_stats(i + 1, g)
                    for t in range(TT):
                        dve.wait_ge(filled, 1 + T.n * i + T.filled(("V", t)))
                        nc.vector.tensor_copy(v[:, t], bank_of(("V", t))[:]).then_inc(dve_read, 1)
                        if t == 0 and not last:
                            norm_var(i + 1)
                    if not last:
                        norm(i + 1)
                    for n in range(NKP):
                        dve.wait_ge(kv_step, 1 + NKP * i + max(n - 3, 0))
                        dve.wait_ge(act_read, 1 + T.n_act * i + T.act(("KP", n)))
                        nc.vector.scalar_tensor_tensor(kp[:, n % 4], bank_of(("KP", n))[:], 0.0, e[:, n % 4],
                                                       ALU.max, ALU.add).then_inc(dve_read, 1)

                def add_kv(i, b):
                    dve.wait_ge(kv_step, 1 + NKP * i + NKP)
                    dve.wait_ge(kv_taken, 1 + 2 * i)
                    nc.vector.tensor_tensor(kv_sum[:, b], kv_sum[:, b], p_kv[:], ALU.add).then_inc(kv_taken, 1)
                    nc.vector.tensor_tensor(ks_sum[:, b], ks_sum[:, b], p_ks[:], ALU.add).then_inc(kv_taken, 1)

                dve.wait_ge(const_set, 2)
                for t in range(TT):
                    norm_stats(0, t)
                norm_var(0)
                norm(0)
                for c in range(C):
                    dve.wait_ge(w_hi, 1 + c + 1)
                    nc.vector.tensor_tensor(w[:, LO, c], w_raw[:, c], w[:, HI, c].bitcast(F32),
                                            ALU.subtract).then_inc(w_lo, 1)
                dve.wait_ge(w_hi, 1 + C + 1)
                nc.vector.tensor_tensor(f_w[:, LO], f_raw[:], f_w[:, HI].bitcast(F32), ALU.subtract).then_inc(w_lo, 1)
                turn(0)
                dve.wait_ge(const_set, 6)
                for b in range(NBLK // BLK):
                    with dve.Fori(0, BLK - 1) as k:
                        i = k + BLK * b
                        heads(i, False)
                        turn(i + 1)
                        add_kv(i, b)
                    i = BLK * b + BLK - 1
                    heads(i, i == NBLK - 1)
                    if i < NBLK - 1:
                        turn(i + 1)
                    add_kv(i, b)
                for b in range(NBLK // BLK):
                    dve.wait_ge(kv_done, 1 + 2 * b + 1)
                    nc.vector.tensor_copy(kv_w[:, b].rearrange("p h d -> p (h d)"), pk[b][:]).then_inc(turned, 1)
                    dve.wait_ge(kv_done, 1 + 2 * b + 2)
                    flat = ks_w[:, b].rearrange("p h d -> p (h d)")
                    for j in range(HG):
                        nc.vector.tensor_copy(flat[:, j * HD:(H - HG + j) * HD + G:HG * HD + 1],
                                              pk[2 + b][:, j * P:(j + 1) * P:HD]).then_inc(turned, 1)

            @block.tensor
            def _(pe):
                def dve_has_read(i, key):
                    pe.wait_ge(dve_read, 1 + T.n_dve * i + T.dve(key))

                def turn(i, first):
                    for t in range(TT):
                        pe.wait_ge(xn_set, 1 + TT * i + t + 1)
                        if t >= 2:
                            dve_has_read(i, ("T", t - 2))
                        elif not first:
                            pe.wait_ge(dve_read, 1 + T.n_dve * (i - 1) + T.dve(("V", TT - 1)))
                        for c in range(C):
                            mm = nc.tensor.transpose(bank_of(("T", t))[:, c * P:(c + 1) * P],
                                                     xn[:, t, c * P:(c + 1) * P], ident[:])
                        mm.then_inc(filled, 1)

                def projections(i):
                    for g in range(G):
                        if g < 2:
                            dve_has_read(i, ("T", TT - 1))
                        else:
                            dve_has_read(i, ("K", g - 2))
                        matmuls(("K", g), lambda s, c, g=g: w[:, s, c, D + g * P:D + (g + 1) * P],
                                lambda s, c: xt[:, s, c])
                    for g in range(G):
                        dve_has_read(i, ("Q", g - 2) if g > 1 else ("K", g + 2))
                        matmuls(("Q", g), lambda s, c, g=g: w[:, s, c, g * P:(g + 1) * P],
                                lambda s, c: xt[:, s, c])
                    for t in range(TT):
                        dve_has_read(i, ("V", t - 2) if t > 1 else ("Q", t + 2))
                        matmuls(("V", t), lambda s, c, t=t: xt[:, s, c, t * P:(t + 1) * P],
                                lambda s, c: w[:, s, c, 2 * D:3 * D])

                def matmuls(key, stationary, moving):
                    n = 0
                    for c in range(C):
                        for s, m in PASSES:
                            mm = nc.tensor.matmul(bank_of(key)[:], stationary(s, c), moving(m, c),
                                                  start=(n == 0), stop=(n == C * 3 - 1))
                            n += 1
                    mm.then_inc(filled, 1)

                def features(i, n):
                    t, g = n // G, n % G
                    if n >= 4:
                        dve_has_read(i, ("KP", n - 4))
                    else:
                        dve_has_read(i, ("K", g))
                    for q, (s, m) in enumerate(PASSES):
                        mm = nc.tensor.matmul(pk[n % 4][:], kt[:, s, g, t * P:(t + 1) * P], f_w[:, m, g],
                                              start=(q == 0), stop=(q == 2))
                    mm.then_inc(filled, 1)

                def kv(i, n):
                    t, g = n // G, n % G
                    dve_has_read(i, ("KP", n))
                    if n == 0:
                        pe.wait_ge(kv_taken, 1 + 2 * i)
                    for j in range(HG):
                        h = g * HG + j
                        nc.tensor.matmul(p_kv[j * HD:(j + 1) * HD, g * F:(g + 1) * F], v[:, t, h * HD:(h + 1) * HD],
                                         kp[:, n % 4, j * F:(j + 1) * F], start=(t == 0 and g == 0), stop=(t == TT - 1),
                                         skip_group_check=True)
                    nc.tensor.matmul(p_ks[g * HD:(g + 1) * HD, :], ones[:], kp[:, n % 4], start=(t == 0),
                                     stop=(t == TT - 1), skip_group_check=True).then_inc(kv_step, 1)

                def block_work(i, last):
                    projections(i)
                    for n in range(NKP):
                        features(i, n)
                        if n >= LAG:
                            kv(i, n - LAG)
                    if not last:
                        turn(i + 1, False)
                    for n in range(NKP - LAG, NKP):
                        kv(i, n)

                pe.wait_ge(const_in, 17)
                pe.wait_ge(const_set, 3)
                turn(0, True)
                pe.wait_ge(w_lo, 1 + C + 1)
                with pe.Fori(0, NBLK - 1) as i:
                    block_work(i, False)
                block_work(NBLK - 1, True)
                pe.wait_ge(kv_taken, 1 + 2 * NBLK)
                for b in range(NBLK // BLK):
                    for g in range(G):
                        mm = nc.tensor.transpose(pk[b][:, g * P:(g + 1) * P], kv_sum[:, b, g * P:(g + 1) * P], ident[:])
                    mm.then_inc(kv_done, 1)
                    for j in range(HG):
                        mm = nc.tensor.transpose(pk[2 + b][:, j * P:(j + 1) * P], ks_sum[:, b, j * P:(j + 1) * P], ident[:])
                    mm.then_inc(kv_done, 1)


def attend_linear(nc, a, NBLK, BLK, x_blk, q_dram, x1_dram, xq_dram, ident, kv_w, ks_w, half):
    qp_pair = lambda n: [("QP", 2 * n), ("QP", 2 * n + 1)]
    JOBS = ([("R", g) for g in range(G)] + qp_pair(0) + [("O", 0)] + qp_pair(1) + [("O", 1)] + qp_pair(2)
            + [("O", 2)] + qp_pair(3) + [("T", 0), ("O", 3)] + qp_pair(4) + [("T", 1)] + qp_pair(5) + [("T", 2)]
            + qp_pair(6) + [("T", 3)] + qp_pair(7) + [("XQ", g) for g in range(G)])
    POS = {key: n for n, key in enumerate(JOBS)}
    LAST_POS = {key: n for n, key in enumerate(j for j in JOBS if j[0] != "QP")}
    NJ, BANKS, QSLOTS, ESLOTS = len(JOBS), 4, 8, 4
    assert NJ % BANKS == 0 and H % BANKS == 0
    with ExitStack() as ctx:
        def sb(name, shape, dt=F32):
            return ctx.enter_context(nc.sbuf_tensor("li_" + name, shape, dt))

        def sem(name):
            return primed(ctx, nc, sems, "li_" + name)

        sems = []
        f_w = sb("f_w", [3 * HD, H, F], F32R)
        wo = sb("wo", [P, 2, C, D], F32R)
        wq = sb("wq", [P, 2, C, D], F32R)
        spread = sb("spread", [P, G, P])
        bias = sb("bias", [P, D])
        bq = sb("bq", [P, C])
        x = sb("x", [P, TT, D])
        q3 = sb("q3", [3 * HD, H, TB], F32R)
        u_att = sb("u_att", [P, 2, C, TB], F32R)
        u_ln = sb("u_ln", [P, 2, C, TB], F32R)
        xn = sb("xn", [P, 2, D])
        qp = sb("qp", [P, QSLOTS, TB])
        e = sb("e", [P, ESLOTS, TB])
        num = sb("num", [P, G, TB])
        den = sb("den", [P, 2, TB])
        xq = sb("xq", [P, G, TB])
        stats = sb("stats", [P, TT, 6])
        mv = sb("mv", [P, TT, 2])
        rstd = sb("rstd", [P, TT])
        pause = sb("pause", [P, 1])
        bank = [ctx.enter_context(nc.psum_tensor(f"li_bank{n}", [P, 512], F32)) for n in range(BANKS)]
        p_num = [ctx.enter_context(nc.psum_tensor(f"li_p_num{n}", [P, 512], F32)) for n in range(2)]
        p_den = ctx.enter_context(nc.psum_tensor("li_p_den", [P, 512], F32))

        w_in, w_hi, w_lo, const_in = [sem(f"w_in{n}") for n in range(3)], sem("w_hi"), sem("w_lo"), sem("const_in")
        x_in, q_in, x1_out, xq_out = sem("x_in"), sem("q_in"), sem("x1_out"), sem("xq_out")
        filled, dve_read = sem("filled"), sem("dve_read")
        relu_set, exp_set, heads_used = sem("relu_set"), sem("exp_set"), sem("heads_used")
        num_full, num_taken, den_set, rec_set = sem("num_full"), sem("num_taken"), sem("den_set"), sem("rec_set")
        norm_hi, norm_lo, turn_hi = sem("norm_hi"), sem("norm_lo"), sem("turn_hi")
        xb_set, stats_set, aggr_set, var_set = sem("xb_set"), sem("stats_set"), sem("aggr_set"), sem("var_set")
        rstd_set, xn_set = sem("rstd_set"), sem("xn_set")
        prime(nc, pause, sems)

        raw = [(a["features3"].rearrange("p (h f) -> p h f", h=H), f_w, qp[0:3 * HD].rearrange("p s t -> p (s t)")
                [:, 0:H * F].rearrange("p (h f) -> p h f", h=H)),
               (a["w_out"].rearrange("(c p) n -> p c n", p=P), wo, num[:]),
               (a["WqT"].rearrange("(c p) n -> p c n", p=P), wq, xq[:])]

        def job(turn, key):
            return H + NJ * turn + pos(turn)[key]

        def pos(turn):
            return LAST_POS if isinstance(turn, int) and turn == NBLK - 1 else POS

        def head_job(block, h):
            return h if isinstance(block, int) and block == 0 else job(block - 1, ("QP", h))

        def bank_of(turn, key):
            return bank[pos(turn)[key] % BANKS]

        def head_bank(block, h):
            return bank[h % BANKS] if isinstance(block, int) and block == 0 else bank_of(block - 1, ("QP", h))

        def turns(engine, body):
            for b in range(NBLK // BLK):
                with engine.Fori(0, BLK - 1) as k:
                    body(k + BLK * b, b, True)
                body(BLK * b + BLK - 1, b + 1, b + 1 < NBLK // BLK)

        with nc.Block() as block:
            @block.sync
            def _(sp):
                def load_q(i):
                    for r, part in enumerate((HI, LO, HI)):
                        sp.dma_start(q3[r * HD:(r + 1) * HD].bitcast(F32).rearrange("p h t -> p (h t)"),
                                     q_dram[i, part]).then_inc(q_in, 16)

                sp.dma_start(raw[0][2], raw[0][0]).then_inc(w_in[0], 16)
                load_q(0)
                for n in (1, 2):
                    sp.dma_start(raw[n][2], raw[n][0]).then_inc(w_in[n], 16)
                sp.dma_start(bq[:], a["bqT"]).then_inc(const_in, 16)
                sp.dma_start(spread[:].rearrange("p g n -> p (g n)"), a["spread"]).then_inc(const_in, 16)
                sp.dma_start(bias[:], a["b_out"].broadcast_to([P, D])).then_inc(const_in, 16)
                sp.dma_start(x[:], x_blk[0]).then_inc(x_in, 16)
                sp.wait_ge(filled, 1 + H)
                load_q(1)

                def turn(i, left):
                    sp.wait_ge(dve_read, 2 + job(i, ("O", TT - 1)))
                    sp.dma_start(x1_dram[i], x[:].rearrange("p t d -> p (t d)")).then_inc(x1_out, 16)
                    if left:
                        sp.wait_ge(x1_out, 17 + 16 * i)
                        sp.wait_ge(xn_set, 1 + TT * i + TT)
                        sp.dma_start(x[:], x_blk[i + 1]).then_inc(x_in, 16)
                    if left > 1:
                        sp.wait_ge(filled, 2 + job(i, ("QP", H - 1)))
                        load_q(i + 2)
                    sp.wait_ge(dve_read, 2 + job(i, ("XQ", G - 1)))
                    sp.dma_start(xq_dram[i], xq[:].rearrange("p g t -> p (g t)")).then_inc(xq_out, 16)

                with sp.Fori(0, NBLK - 2) as i:
                    turn(i, 2)
                turn(NBLK - 2, 1)
                turn(NBLK - 1, 0)
                sp.wait_ge(x1_out, 1 + 16 * NBLK)
                sp.wait_ge(xq_out, 1 + 16 * NBLK)

            @block.gpsimd
            def _(pool):
                pool.wait_ge(const_in, 1 + 48)
                rows = bias[:].rearrange("p (o d) -> p o d", o=1).broadcast_to([P, TT, D])
                with pool.Fori(0, NBLK) as i:
                    pool.wait_ge(x_in, 17 + 16 * i)
                    nc.gpsimd.tensor_tensor(x[:], x[:], rows, ALU.add).then_inc(xb_set, 1)
                    for t in range(TT):
                        pool.wait_ge(var_set, 2 + TT * i + t)
                        nc.gpsimd.tensor_tensor(rstd[:, t:t + 1], mv[:, t, 1:2], half[:, 0:1], ALU.pow)\
                            .then_inc(rstd_set, 1)

            @block.scalar
            def _(act):
                def heads(i, lo, hi):
                    for h in range(lo, hi + 1):
                        if h < hi:
                            act.wait_ge(filled, 2 + head_job(i, h))
                            nc.scalar.activation(e[:, h % ESLOTS], head_bank(i, h)[:], ACT.Relu, scale=-1.0)\
                                .then_inc(relu_set, 1)
                        if h > lo:
                            s = e[:, (h - 1) % ESLOTS]
                            act.wait_ge(relu_set, 1 + H * i + h)
                            nc.scalar.activation(s, s, ACT.Exp, scale=-1.0).then_inc(exp_set, 1)

                def take_num(i, g):
                    act.wait_ge(num_full, 2 + G * i + g)
                    if not (isinstance(i, int) and i == 0):
                        act.wait_ge(norm_lo, 2 + G * (i - 1) + g)
                    nc.scalar.copy(num[:, g], p_num[g % 2][:]).then_inc(num_taken, 1)

                def turned(i, t):
                    act.wait_ge(filled, 2 + job(i, ("T", t)))
                    nc.scalar.copy(u_ln[:, HI, :, t * P:(t + 1) * P],
                                   bank_of(i, ("T", t))[:].rearrange("p (c n) -> p c n", c=C)).then_inc(turn_hi, 1)

                def turn(i, b, more):
                    def next_heads(pair):
                        if more:
                            heads(i + 1, 2 * pair, 2 * pair + 2)

                    def next_num(g):
                        if more:
                            take_num(i + 1, g)

                    for g in range(G):
                        act.wait_ge(dve_read, 2 + job(i, ("R", g)))
                        nc.scalar.copy(u_att[:, HI, g], num[:, g]).then_inc(norm_hi, 1)
                    next_heads(0)
                    next_heads(1)
                    next_heads(2)
                    next_num(0)
                    next_heads(3)
                    turned(i, 0)
                    next_heads(4)
                    next_num(1)
                    turned(i, 1)
                    next_heads(5)
                    turned(i, 2)
                    next_heads(6)
                    next_num(2)
                    turned(i, 3)
                    next_heads(7)
                    next_num(3)

                act.wait_ge(w_in[0], 17)
                nc.scalar.copy(f_w[:], raw[0][2]).then_inc(w_hi, 1)
                heads(0, 0, H // 2)
                act.wait_ge(w_lo, 3)
                take_num(0, 0)
                heads(0, H // 2, H)
                for g in range(1, G):
                    take_num(0, g)
                turns(act, turn)

            @block.vector
            def _(dve):
                def heads(i, b, lo, hi):
                    for h in range(lo, hi):
                        if not (isinstance(i, int) and i == 0 and h < QSLOTS):
                            dve.wait_ge(heads_used, 2 + G * i + (h - QSLOTS) // HG)
                        dve.wait_ge(exp_set, 2 + H * i + h)
                        nc.vector.scalar_tensor_tensor(qp[:, h % QSLOTS], head_bank(i, h)[:], 0.0, e[:, h % ESLOTS],
                                                       ALU.max, ALU.add).then_inc(dve_read, 1)

                def divide(i):
                    dve.wait_ge(heads_used, 1 + G * i + G)
                    nc.vector.tensor_scalar(den[:, 0], p_den[:], 1e-8, None, ALU.add).then_inc(den_set, 1)
                    dve.wait_ge(den_set, 2 + i)
                    nc.vector.reciprocal(den[:, 1], den[:, 0]).then_inc(rec_set, 1)

                def normalise(i):
                    for g in range(G + 1):
                        if g < G:
                            dve.wait_ge(num_taken, 2 + G * i + g)
                            dve.wait_ge(filled, 2 + job(i, ("R", g)))
                            nc.vector.tensor_tensor(num[:, g], num[:, g], bank_of(i, ("R", g))[:], ALU.mult)\
                                .then_inc(dve_read, 1)
                        if g:
                            dve.wait_ge(norm_hi, 1 + G * i + g)
                            nc.vector.tensor_tensor(u_att[:, LO, g - 1], num[:, g - 1], u_att[:, HI, g - 1].bitcast(F32),
                                                    ALU.subtract).then_inc(norm_lo, 1)

                def add_out(i, t):
                    if t == 0:
                        dve.wait_ge(xb_set, 2 + i)
                    dve.wait_ge(filled, 2 + job(i, ("O", t)))
                    nc.vector.tensor_tensor(x[:, t], x[:, t], bank_of(i, ("O", t))[:], ALU.add).then_inc(dve_read, 1)
                    dve.wait_ge(dve_read, 2 + job(i, ("O", t)))
                    nc.vector.bn_stats(stats[:, t], x[:, t]).then_inc(stats_set, 1)
                    dve.wait_ge(stats_set, 2 + TT * i + t)
                    nc.vector.tensor_copy(pause[:], half[:, 0:1])
                    nc.vector.bn_aggr(mv[:, t], stats[:, t]).then_inc(aggr_set, 1)
                    dve.wait_ge(aggr_set, 2 + TT * i + t)
                    nc.vector.tensor_scalar(mv[:, t, 1:2], mv[:, t, 1:2], EPS, None, ALU.add).then_inc(var_set, 1)

                def norm(i, t):
                    dve.wait_ge(rstd_set, 2 + TT * i + t)
                    if t >= 2:
                        dve.wait_ge(filled, 2 + job(i, ("T", t - 2)))
                    nc.vector.tensor_scalar(xn[:, t % 2], x[:, t], mv[:, t, 0:1], rstd[:, t:t + 1],
                                            ALU.subtract, ALU.mult).then_inc(xn_set, 1)

                def turned(i, t):
                    part = slice(t * P, (t + 1) * P)
                    dve.wait_ge(turn_hi, 2 + TT * i + t)
                    nc.vector.tensor_tensor(u_ln[:, LO, :, part], bank_of(i, ("T", t))[:].rearrange("p (c n) -> p c n", c=C),
                                            u_ln[:, HI, :, part].bitcast(F32), ALU.subtract).then_inc(dve_read, 1)

                def turn(i, b, more):
                    def next_heads(pair):
                        if more:
                            heads(i + 1, b, 2 * pair, 2 * pair + 2)

                    normalise(i)
                    next_heads(0)
                    add_out(i, 0)
                    next_heads(1)
                    add_out(i, 1)
                    norm(i, 0)
                    next_heads(2)
                    add_out(i, 2)
                    norm(i, 1)
                    next_heads(3)
                    turned(i, 0)
                    add_out(i, 3)
                    norm(i, 2)
                    next_heads(4)
                    turned(i, 1)
                    norm(i, 3)
                    next_heads(5)
                    turned(i, 2)
                    next_heads(6)
                    turned(i, 3)
                    next_heads(7)
                    dve.wait_ge(xq_out, 1 + 16 * i)
                    for g in range(G):
                        dve.wait_ge(filled, 2 + job(i, ("XQ", g)))
                        nc.vector.tensor_scalar(xq[:, g], bank_of(i, ("XQ", g))[:], bq[:, g:g + 1], None, ALU.add)\
                            .then_inc(dve_read, 1)
                        if g == 0 and more:
                            divide(i + 1)

                dve.wait_ge(w_hi, 2)
                lo_rows = slice(2 * HD, 3 * HD)
                nc.vector.tensor_tensor(f_w[lo_rows], raw[0][2][lo_rows], f_w[lo_rows].bitcast(F32), ALU.subtract)\
                    .then_inc(w_lo, 1)
                for n in (1, 2):
                    _, dst, stage = raw[n]
                    dve.wait_ge(w_in[n], 17)
                    nc.vector.tensor_copy(dst[:, HI], stage).then_inc(w_hi, 1)
                    dve.wait_ge(w_hi, 2 + n)
                    nc.vector.tensor_tensor(dst[:, LO], stage, dst[:, HI].bitcast(F32), ALU.subtract).then_inc(w_lo, 1)
                dve.wait_ge(const_in, 49)
                heads(0, 0, 0, H)
                divide(0)
                turns(dve, turn)

            @block.tensor
            def _(pe):
                def bank_free(n):
                    if not (isinstance(n, int) and n < BANKS):
                        pe.wait_ge(dve_read, 2 + n - BANKS)

                def three(out, stationary, moving, c):
                    for n, (s, m) in enumerate(PASSES):
                        mm = nc.tensor.matmul(out, stationary(s), moving(m), start=(c == 0 and n == 0),
                                              stop=(c == C - 1 and n == 2))
                    return mm

                def heads(i, lo, hi):
                    if lo == 0:
                        pe.wait_ge(q_in, 49 + 48 * i)
                    for h in range(lo, hi):
                        bank_free(head_job(i, h))
                        nc.tensor.matmul(head_bank(i, h)[:], f_w[:, h], q3[:, h], start=True, stop=True)\
                            .then_inc(filled, 1)

                def attend_group(i, b, g):
                    pe.wait_ge(dve_read, 2 + head_job(i, HG * g + HG - 1))
                    if not (isinstance(i, int) and i == 0 and g < 2):
                        pe.wait_ge(num_taken, G * i + g)
                    if g == 0 and not (isinstance(i, int) and i == 0):
                        pe.wait_ge(den_set, 1 + i)
                    slot = lambda j: qp[:, (HG * g + j) % QSLOTS]

                    def dens():
                        for j in range(HG):
                            mm = nc.tensor.matmul(p_den[j * HD:(j + 1) * HD, :], ks_w[:, b, HG * g + j], slot(j),
                                                  start=(g == 0), stop=(g == G - 1), skip_group_check=True)
                        mm.then_inc(heads_used, 1)

                    def nums():
                        for j in range(HG):
                            mm = nc.tensor.matmul(p_num[g % 2][j * HD:(j + 1) * HD, :], kv_w[:, b, HG * g + j], slot(j),
                                                  start=True, stop=True, skip_group_check=True)
                        mm.then_inc(num_full, 1)

                    nums()
                    dens()

                def out_proj(i, t):
                    bank_free(job(i, ("O", t)))
                    for g in range(G):
                        if t == 0:
                            pe.wait_ge(norm_lo, 2 + G * i + g)
                        mm = three(bank_of(i, ("O", t))[:], lambda s: u_att[:, s, g, t * P:(t + 1) * P],
                                   lambda m: wo[:, m, g], g)
                    mm.then_inc(filled, 1)

                def transposes(i, t):
                    bank_free(job(i, ("T", t)))
                    pe.wait_ge(xn_set, 2 + TT * i + t)
                    for c in range(C):
                        mm = nc.tensor.transpose(bank_of(i, ("T", t))[:, c * P:(c + 1) * P], xn[:, t % 2, c * P:(c + 1) * P],
                                                 ident[:])
                    mm.then_inc(filled, 1)

                def turn(i, b, more):
                    def next_heads(pair):
                        if more:
                            heads(i + 1, 2 * pair, 2 * pair + 2)

                    def next_group(g):
                        if more:
                            attend_group(i + 1, b, g)

                    pe.wait_ge(rec_set, 2 + i)
                    for g in range(G):
                        bank_free(job(i, ("R", g)))
                        nc.tensor.matmul(bank_of(i, ("R", g))[:], spread[:, g], den[:, 1], start=True, stop=True)\
                            .then_inc(filled, 1)
                    next_heads(0)
                    out_proj(i, 0)
                    next_heads(1)
                    out_proj(i, 1)
                    next_heads(2)
                    next_group(0)
                    out_proj(i, 2)
                    next_heads(3)
                    transposes(i, 0)
                    out_proj(i, 3)
                    next_heads(4)
                    next_group(1)
                    transposes(i, 1)
                    next_heads(5)
                    transposes(i, 2)
                    next_heads(6)
                    next_group(2)
                    transposes(i, 3)
                    next_heads(7)
                    pe.wait_ge(dve_read, 2 + job(i, ("T", TT - 1)))
                    for g in range(G):
                        bank_free(job(i, ("XQ", g)))
                        for c in range(C):
                            mm = three(bank_of(i, ("XQ", g))[:], lambda s: wq[:, s, c, g * P:(g + 1) * P],
                                       lambda m: u_ln[:, m, c], c)
                        mm.then_inc(filled, 1)
                        if g == 0:
                            next_group(3)

                pe.wait_ge(w_lo, 2)
                heads(0, 0, H // 2)
                attend_group(0, 0, 0)
                heads(0, H // 2, H)
                pe.wait_ge(w_lo, 4)
                for g in range(1, G):
                    attend_group(0, 0, g)
                turns(pe, turn)


def attend_cross(nc, a, NB, BLK, x1_dram, xq_dram, x2_dram, x3_dram, ident, half):
    SU = HG + 1
    NS = G * SU
    SLOTS = 2 * SU
    mx_jobs = lambda k: [(k, "MX", n // SU, n % SU) for n in range(TT * SU)]
    JOBS = mx_jobs(0) + [(0, "MT")]
    for k in range(BLK):
        more = k + 1 < BLK
        JOBS += ((mx_jobs(k + 1) if more else []) + [(k, "R", g) for g in range(G)] + [(k, "O", 0)]
                 + [(k + 1, "MT")] * more + [(k, "O", 1), (k, "O", 2), (k, "T", 0), (k, "O", 3)]
                 + [(k, "T", t) for t in range(1, TT)])
    POS = {key: n for n, key in enumerate(JOBS)}
    NJ, BANKS, SBANKS = len(JOBS), 3, 2
    assert NJ % BANKS == 0 and BLK * NS % SBANKS == 0
    with ExitStack() as ctx:
        def sb(name, shape, dt=F32):
            return ctx.enter_context(nc.sbuf_tensor("cr_" + name, shape, dt))

        def sem(name):
            return primed(ctx, nc, sems, "cr_" + name)

        sems = []
        wo = sb("wo", [P, 2, C, D], F32R)
        k_w = sb("k_w", [P, 2, G, HG * P + P], F32R)
        v_w = sb("v_w", [P, D])
        v_rem = sb("v_rem", [P, G, HG, HD])
        one_col = sb("one_col", [P, G, HD])
        rem_ones = sb("rem_ones", [P, G, P])
        spread = sb("spread", [P, G, P])
        minus = sb("minus", [P, G, SU, P], BF16)
        bias = sb("bias", [P, D])
        bk = sb("bk", [P, C])
        small = sb("small", [P, 2 * HG])
        x = sb("x", [P, TT, D])
        xq_raw = sb("xq_raw", [P, C * TB])
        xq = [sb(f"xq{n}", [P, 2, C * TB], F32R) for n in range(2)]
        u = sb("u", [P, 2, C, TB], F32R)
        xn = sb("xn", [P, 2, D])
        ring = sb("ring", [P, SLOTS, TB])
        num = sb("num", [P, G, TB])
        x3 = sb("x3", [P, C, TB])
        den = sb("den", [P, 2, TB])
        kt = sb("kt", [P, 2, P + KPAD])
        stats = sb("stats", [P, TT, 6])
        mv = sb("mv", [P, TT, 2])
        rstd = sb("rstd", [P, TT])
        pause = sb("pause", [P, 1])
        mx = sb("mx", [P, 2, TT, H])
        mxb = sb("mxb", [P, TT, P], BF16)
        mxt = sb("mxt", [P, TB], BF16)
        ident_b = sb("ident_b", [P, P], BF16)
        bank = [ctx.enter_context(nc.psum_tensor(f"cr_bank{n}", [P, 512], F32)) for n in range(BANKS)]
        s_bank = [ctx.enter_context(nc.psum_tensor(f"cr_s_bank{n}", [P, 512], F32)) for n in range(SBANKS)]
        p_num = [ctx.enter_context(nc.psum_tensor(f"cr_p_num{n}", [P, 512], F32)) for n in range(2)]
        p_den = ctx.enter_context(nc.psum_tensor("cr_p_den", [P, 512], F32))

        w_in, w_hi, w_lo, const_in, zero_set = sem("w_in"), sem("w_hi"), sem("w_lo"), sem("const_in"), sem("zero_set")
        cast_in = ctx.enter_context(nc.semaphore("cr_cast_in"))
        ctx_in, ctx_mm, ctx_act, ctx_step = sem("ctx_in"), sem("ctx_mm"), sem("ctx_act"), sem("ctx_step")
        x_in, xq_in, xq_hi, xq_lo, x2_out, x3_out = (sem("x_in"), sem("xq_in"), sem("xq_hi"), sem("xq_lo"),
                                                     sem("x2_out"), sem("x3_out"))
        filled, dve_read, s_full, s_read = sem("filled"), sem("dve_read"), sem("s_full"), sem("s_read")
        heads_used, num_full, num_taken = sem("heads_used"), sem("num_full"), sem("num_taken")
        den_full, den_set, rec_set = sem("den_full"), sem("den_set"), sem("rec_set")
        norm_hi, norm_lo, mx_set = sem("norm_hi"), sem("norm_lo"), sem("mx_set")
        xb_set, stats_set, aggr_set, var_set = sem("xb_set"), sem("stats_set"), sem("aggr_set"), sem("var_set")
        rstd_set, xn_set = sem("rstd_set"), sem("xn_set")
        prime(nc, pause, sems)

        CTXW = P + KPAD + P
        ctx_t = num[:].rearrange("p g t -> p (g t)")[:, 0:C * CTXW].rearrange("p (c n) -> p c n", c=C)
        wk, wv, bv, tmp = ring[:, 0:4], ring[:, 4:8], ring[:, 8], ring[:, 9]
        CTX_STEPS = 6 * G + 2 + G

        def job(b, k, *what):
            return NJ * b + POS[(k, *what)]

        def bank_of(k, *what):
            return bank[POS[(k, *what)] % BANKS]

        with nc.Block() as block:
            @block.sync
            def _(sp):
                def load_context(b):
                    sp.dma_start(wk, a["WkT"].rearrange("(c p) n -> p c n", p=P)).then_inc(ctx_in, 16)
                    sp.dma_start(ctx_t, a["ctxT"][b].rearrange("(c p) n -> p c n", p=P)).then_inc(ctx_in, 16)
                    sp.dma_start(wv, a["WvT"].rearrange("(c p) n -> p c n", p=P)).then_inc(ctx_in, 16)
                    sp.dma_start(bv, a["bv"].broadcast_to([P, D])).then_inc(ctx_in, 16)

                def batch(b, more):
                    def load_xq(k):
                        sp.wait_ge(xq_lo, 1 + (b * BLK + k))
                        sp.dma_start(xq_raw[:], xq_dram[b * BLK + k]).then_inc(xq_in, 16)

                    load_xq(0)
                    load_xq(1)
                    for k in range(BLK):
                        i = b * BLK + k
                        sp.wait_ge(x2_out, 1 + 16 * i)
                        sp.dma_start(x[:].rearrange("p t d -> p (t d)"), x1_dram[i]).then_inc(x_in, 16)
                        if k + 2 < BLK:
                            load_xq(k + 2)
                        if k == BLK - 1 and more:
                            sp.wait_ge(num_full, 1 + G * BLK * (b + 1))
                            sp.wait_ge(norm_lo, 1 + G * BLK * (b + 1))
                            load_context(b + 1)
                        sp.wait_ge(dve_read, 2 + job(b, k, "O", TT - 1))
                        sp.dma_start(x2_dram[i], x[:].rearrange("p t d -> p (t d)")).then_inc(x2_out, 16)
                        sp.wait_ge(dve_read, 2 + job(b, k, "T", TT - 1))
                        sp.dma_start(x3_dram[i], x3[:].rearrange("p g t -> p (g t)")).then_inc(x3_out, 16)

                sp.dma_start(bk[:], a["bkT"]).then_inc(const_in, 16)
                sp.dma_start(small[:], a["small"]).then_inc(const_in, 16)
                load_context(0)
                for dst, src in ((one_col, "one_col"), (rem_ones, "rem_ones"), (spread, "spread")):
                    sp.dma_start(dst[:].rearrange("p g n -> p (g n)"), a[src]).then_inc(const_in, 16)
                sp.dma_start(bias[:], a["bo"].broadcast_to([P, D])).then_inc(const_in, 16)
                sp.dma_start(x[:], a["WoT"].rearrange("(c p) n -> p c n", p=P)).then_inc(w_in, 16)
                sp.wait_ge(w_lo, 2)
                with sp.Fori(0, NB - 1) as b:
                    batch(b, True)
                batch(NB - 1, False)
                sp.wait_ge(x2_out, 1 + 16 * NB * BLK)
                sp.wait_ge(x3_out, 1 + 16 * NB * BLK)

            @block.gpsimd
            def _(pool):
                nc.gpsimd.memset(mxb[:], 0.0).then_inc(zero_set, 1)
                pool.dma_start(minus[:].rearrange("p g s n -> p (g s n)"), a["minus"]).then_inc(cast_in, 16)
                pool.dma_start(ident_b[:], a["ident"]).then_inc(cast_in, 16)
                pool.wait_ge(const_in, 1 + 96)
                rows = bias[:].rearrange("p (o d) -> p o d", o=1).broadcast_to([P, TT, D])
                with pool.Fori(0, NB * BLK) as i:
                    pool.wait_ge(x_in, 17 + 16 * i)
                    nc.gpsimd.tensor_tensor(x[:], x[:], rows, ALU.add).then_inc(xb_set, 1)
                    for t in range(TT):
                        pool.wait_ge(var_set, 2 + TT * i + t)
                        nc.gpsimd.tensor_tensor(rstd[:, t:t + 1], mv[:, t, 1:2], half[:, 0:1], ALU.pow)\
                            .then_inc(rstd_set, 1)

            @block.scalar
            def _(act):
                act.wait_ge(w_in, 17)
                nc.scalar.copy(wo[:, HI], x[:]).then_inc(w_hi, 1)
                act.wait_ge(const_in, 1 + 96)
                with act.Fori(0, NB) as b:
                    for g in range(G):
                        act.wait_ge(ctx_mm, 2 + ((G + 2) * b + g))
                        if g >= 2:
                            act.wait_ge(ctx_step, 1 + (CTX_STEPS * b + 6 * (g - 1)))
                        nc.scalar.activation(kt[:, g % 2], bank[g % 2][:, 0:P + KPAD], ACT.Identity,
                                             bias=bk[:, g:g + 1]).then_inc(ctx_act, 1)

                    def split_xq(k):
                        act.wait_ge(xq_in, 17 + 16 * (b * BLK + k))
                        nc.scalar.copy(xq[k % 2][:, HI], xq_raw[:]).then_inc(xq_hi, 1)

                    def take_num(k, g):
                        act.wait_ge(num_full, 2 + (G * BLK * b + G * k + g))
                        nc.scalar.copy(num[:, g], p_num[g % 2][:]).then_inc(num_taken, 1)

                    split_xq(0)
                    split_xq(1)
                    for k in range(BLK):
                        for n in range(NS):
                            act.wait_ge(s_full, 2 + (NS * BLK * b + NS * k + n))
                            if n >= SLOTS:
                                act.wait_ge(heads_used, 2 + ((G - 1) * (BLK * b + k) + (n - SLOTS) // SU))
                            nc.scalar.activation(ring[:, n % SLOTS], s_bank[n % SBANKS][:], ACT.Exp,
                                                 scale=float(HD) ** -0.5).then_inc(s_read, 1)
                            if n % SU == SU - 1 and n > SU:
                                take_num(k, n // SU - 1)
                        take_num(k, G - 1)
                        for g in range(G):
                            act.wait_ge(dve_read, 2 + job(b, k, "R", g))
                            nc.scalar.copy(u[:, HI, g], num[:, g]).then_inc(norm_hi, 1)
                        if k + 2 < BLK:
                            split_xq(k + 2)

            @block.vector
            def _(dve):
                dve.wait_ge(w_hi, 2)
                nc.vector.tensor_tensor(wo[:, LO], x[:], wo[:, HI].bitcast(F32), ALU.subtract).then_inc(w_lo, 1)
                nc.vector.memset(mx[:], 0.0).then_inc(zero_set, 1)
                dve.wait_ge(const_in, 1 + 96)
                dve.wait_ge(zero_set, 3)
                with dve.Fori(0, NB) as b:
                    step = [0]

                    def chain(ins):
                        step[0] += 1
                        ins.then_inc(ctx_step, 1)
                        dve.wait_ge(ctx_step, 1 + step[0] + CTX_STEPS * b)

                    dve.wait_ge(ctx_in, 65 + 64 * b)
                    for g in range(G):
                        dve.wait_ge(ctx_act, 2 + (G * b + g))
                        for lo, cols in ((0, slice(0, P)), (HG * P, slice(P, P + KPAD))):
                            n = cols.stop - cols.start
                            out = slice(lo, lo + HG * n)
                            k_all = kt[:, g % 2:g % 2 + 1, cols].broadcast_to([P, HG, n])
                            rows = small[:, 0:HG].rearrange("p (j o) -> p j o", o=1).broadcast_to([P, HG, n])
                            chain(nc.vector.tensor_tensor(tmp[:, 0:HG * n].rearrange("p (j k) -> p j k", j=HG), k_all,
                                                          rows, ALU.mult))
                            chain(nc.vector.tensor_copy(k_w[:, HI, g, out], tmp[:, 0:HG * n]))
                            chain(nc.vector.tensor_tensor(k_w[:, LO, g, out], tmp[:, 0:HG * n],
                                                          k_w[:, HI, g, out].bitcast(F32), ALU.subtract))
                    dve.wait_ge(ctx_mm, 2 + ((G + 2) * b + G))
                    chain(nc.vector.tensor_tensor(v_w[:], bank[2][:], bv, ALU.add))
                    dve.wait_ge(ctx_mm, 2 + ((G + 2) * b + G + 1))
                    chain(nc.vector.tensor_tensor(tmp, s_bank[0][:], bv, ALU.add))
                    rows = small[:, HG:2 * HG].rearrange("p (j o) -> p j o", o=1).broadcast_to([P, HG, HD])
                    for g in range(G):
                        chain(nc.vector.tensor_tensor(v_rem[:, g], tmp[:, g * P:(g + 1) * P].rearrange(
                            "p (j d) -> p j d", j=HG), rows, ALU.mult))

                    def split_xq(k):
                        dve.wait_ge(xq_hi, 2 + (b * BLK + k))
                        nc.vector.tensor_tensor(xq[k % 2][:, LO], xq_raw[:], xq[k % 2][:, HI].bitcast(F32),
                                                ALU.subtract).then_inc(xq_lo, 1)

                    def maxima(k, t):
                        if t == 0:
                            dve.wait_ge(mx_set, 1 + 3 * (BLK * b + k))
                        for g in range(G + 1):
                            dve.wait_ge(filled, 2 + job(b, k, "MX", t, g))
                            src = bank_of(k, "MX", t, g)[:].rearrange("p (h n) -> p h n", h=HG if g < G else H)
                            dst = mx[:, 0, t, g * HG:(g + 1) * HG] if g < G else mx[:, 1, t]
                            nc.vector.tensor_reduce(dst, src, AX.X, ALU.max).then_inc(dve_read, 1)
                        if t < TT - 1:
                            return
                        dve.wait_ge(dve_read, 2 + job(b, k, "MX", t, G))
                        nc.vector.tensor_tensor(mx[:, 0], mx[:, 0], mx[:, 1], ALU.max).then_inc(mx_set, 1)
                        dve.wait_ge(mx_set, 2 + (3 * BLK * b + 3 * k))
                        nc.vector.tensor_copy(mxb[:, :, 0:H], mx[:, 0]).then_inc(mx_set, 1)
                        dve.wait_ge(mx_set, 3 + (3 * BLK * b + 3 * k))
                        nc.vector.tensor_tensor(mxb[:, :, H:2 * H], mx[:, 0], mxb[:, :, 0:H], ALU.subtract)\
                            .then_inc(mx_set, 1)

                    def add_out(k, t):
                        n = TT * BLK * b + TT * k + t
                        if t == 0:
                            dve.wait_ge(xb_set, 2 + (BLK * b + k))
                        dve.wait_ge(filled, 2 + job(b, k, "O", t))
                        nc.vector.tensor_tensor(x[:, t], x[:, t], bank_of(k, "O", t)[:], ALU.add).then_inc(dve_read, 1)
                        dve.wait_ge(dve_read, 2 + job(b, k, "O", t))
                        nc.vector.bn_stats(stats[:, t], x[:, t]).then_inc(stats_set, 1)
                        dve.wait_ge(stats_set, 2 + n)
                        nc.vector.tensor_copy(pause[:], half[:, 0:1])
                        nc.vector.bn_aggr(mv[:, t], stats[:, t]).then_inc(aggr_set, 1)
                        dve.wait_ge(aggr_set, 2 + n)
                        nc.vector.tensor_scalar(mv[:, t, 1:2], mv[:, t, 1:2], EPS, None, ALU.add).then_inc(var_set, 1)

                    def norm(k, t):
                        dve.wait_ge(rstd_set, 2 + (TT * BLK * b + TT * k + t))
                        if t >= 2:
                            dve.wait_ge(filled, 2 + job(b, k, "T", t - 2))
                        nc.vector.tensor_scalar(xn[:, t % 2], x[:, t], mv[:, t, 0:1], rstd[:, t:t + 1],
                                                ALU.subtract, ALU.mult).then_inc(xn_set, 1)

                    def turned(k, t):
                        if t == 0:
                            dve.wait_ge(x3_out, 1 + 16 * (b * BLK + k))
                        dve.wait_ge(filled, 2 + job(b, k, "T", t))
                        nc.vector.tensor_copy(x3[:, :, t * P:(t + 1) * P],
                                              bank_of(k, "T", t)[:].rearrange("p (c n) -> p c n", c=C))\
                            .then_inc(dve_read, 1)

                    def turned_maxima(k):
                        dve.wait_ge(filled, 2 + job(b, k, "MT"))
                        nc.vector.tensor_copy(mxt[:], bank_of(k, "MT")[:].bitcast(BF16)[:, 0:TB]).then_inc(dve_read, 1)

                    split_xq(0)
                    for t in range(TT):
                        maxima(0, t)
                    turned_maxima(0)
                    split_xq(1)
                    for k in range(BLK):
                        i = b * BLK + k
                        if k + 1 < BLK:
                            for t in range(TT):
                                maxima(k + 1, t)
                        dve.wait_ge(den_full, 2 + i)
                        nc.vector.tensor_scalar(den[:, 0], p_den[:], 1e-30, None, ALU.max).then_inc(den_set, 1)
                        dve.wait_ge(den_set, 2 + i)
                        nc.vector.reciprocal(den[:, 1], den[:, 0]).then_inc(rec_set, 1)
                        for g in range(G + 1):
                            if g < G:
                                dve.wait_ge(num_taken, 2 + (G * i + g))
                                dve.wait_ge(filled, 2 + job(b, k, "R", g))
                                nc.vector.tensor_tensor(num[:, g], num[:, g], bank_of(k, "R", g)[:], ALU.mult)\
                                    .then_inc(dve_read, 1)
                            if g:
                                dve.wait_ge(norm_hi, 1 + (G * i + g))
                                nc.vector.tensor_tensor(u[:, LO, g - 1], num[:, g - 1], u[:, HI, g - 1].bitcast(F32),
                                                        ALU.subtract).then_inc(norm_lo, 1)
                        add_out(k, 0)
                        if k + 1 < BLK:
                            turned_maxima(k + 1)
                        add_out(k, 1)
                        norm(k, 0)
                        add_out(k, 2)
                        norm(k, 1)
                        turned(k, 0)
                        add_out(k, 3)
                        norm(k, 2)
                        turned(k, 1)
                        norm(k, 3)
                        turned(k, 2)
                        turned(k, 3)
                        if k + 2 < BLK:
                            split_xq(k + 2)

            @block.tensor
            def _(pe):
                pe.wait_ge(const_in, 1 + 96)
                pe.wait_ge(cast_in, 32)
                pe.wait_ge(zero_set, 3)
                with pe.Fori(0, NB) as b:
                    pe.wait_ge(ctx_in, 65 + 64 * b)
                    pe.wait_ge(dve_read, 1 + NJ * b)
                    pe.wait_ge(s_read, 1 + NS * BLK * b)
                    for g in range(G):
                        if g >= 2:
                            pe.wait_ge(ctx_act, 1 + (G * b + g - 1))
                        for c in range(C):
                            mm = nc.tensor.matmul(bank[g % 2][:, 0:P + KPAD], wk[:, c, g * P:(g + 1) * P],
                                                  ctx_t[:, c, 0:P + KPAD], start=(c == 0), stop=(c == C - 1))
                        mm.then_inc(ctx_mm, 1)
                    for out, lo in ((bank[2], 0), (s_bank[0], P + KPAD)):
                        for c in range(C):
                            mm = nc.tensor.matmul(out[:], ctx_t[:, c, lo:lo + P], wv[:, c], start=(c == 0),
                                                  stop=(c == C - 1))
                        mm.then_inc(ctx_mm, 1)
                    pe.wait_ge(ctx_step, 1 + CTX_STEPS * (b + 1))

                    def bank_free(k, *what):
                        n = POS[(k, *what)]
                        if n >= BANKS:
                            pe.wait_ge(dve_read, 2 + (NJ * b + n - BANKS))

                    def maxima(k, n):
                        q = xq[k % 2][:].rearrange("p s (g n) -> p s g n", g=G)
                        t, unit = n // SU, n % SU
                        part = slice(t * P, (t + 1) * P)
                        bank_free(k, "MX", t, unit)
                        if n == 0:
                            pe.wait_ge(xq_hi, 2 + (b * BLK + k))
                        if unit < G:
                            mm = nc.tensor.matmul(bank_of(k, "MX", t, unit)[:], q[:, HI, unit, part],
                                                  k_w[:, HI, unit, 0:HG * P], start=True, stop=True)
                        else:
                            for g in range(G):
                                mm = nc.tensor.matmul(bank_of(k, "MX", t, G)[:, g * P:(g + 1) * P], q[:, HI, g, part],
                                                      k_w[:, HI, g, HG * P:HG * P + P], start=(g == 0),
                                                      stop=(g == G - 1), skip_group_check=True)
                        mm.then_inc(filled, 1)

                    def turn_maxima(k):
                        bank_free(k, "MT")
                        pe.wait_ge(mx_set, 4 + 3 * (b * BLK + k))
                        for t in range(TT):
                            mm = nc.tensor.transpose(bank_of(k, "MT")[:].bitcast(BF16)[:, t * P:(t + 1) * P], mxb[:, t],
                                                     ident_b[:])
                        mm.then_inc(filled, 1)

                    def scores(k, n):
                        g, j = n // SU, n % SU
                        q = xq[k % 2][:].rearrange("p s (g n) -> p s g n", g=G)
                        if n == 0:
                            pe.wait_ge(xq_lo, 2 + (b * BLK + k))
                        if NS * k + n >= SBANKS:
                            pe.wait_ge(s_read, 2 + (NS * BLK * b + NS * k + n - SBANKS))
                        for c, (s, m) in enumerate(PASSES):
                            nc.tensor.matmul(s_bank[n % SBANKS][:], k_w[:, s, g, j * P:(j + 1) * P], q[:, m, g],
                                             start=(c == 0), stop=False)

                    def shift(k, n):
                        nc.tensor.matmul(s_bank[n % SBANKS][:], minus[:, n // SU, n % SU], mxt[:], start=False,
                                         stop=True).then_inc(s_full, 1)

                    def attend_group(k, g):
                        n = G * BLK * b + G * k + g
                        pe.wait_ge(s_read, 2 + (NS * BLK * b + NS * k + SU * g + SU - 1))
                        slot = [ring[:, (SU * g + j) % SLOTS] for j in range(SU)]

                        def dens():
                            if g == 0:
                                pe.wait_ge(den_set, 1 + (b * BLK + k))
                            for j in range(HG):
                                nc.tensor.matmul(p_den[j * HD:(j + 1) * HD, :], one_col[:, g], slot[j], start=(g == 0),
                                                 stop=False, skip_group_check=True)
                            return nc.tensor.matmul(p_den[:], rem_ones[:, g], slot[HG], start=False, stop=(g == G - 1),
                                                    skip_group_check=True)

                        def nums():
                            pe.wait_ge(num_taken, n if k or g >= 2 else 1 + G * BLK * b)
                            for j in range(HG):
                                h = HG * g + j
                                nc.tensor.matmul(p_num[g % 2][j * HD:(j + 1) * HD, :], v_w[:, h * HD:(h + 1) * HD],
                                                 slot[j], start=True, stop=False, skip_group_check=True)
                            return nc.tensor.matmul(p_num[g % 2][:], v_rem[:, g].rearrange("p j d -> p (j d)"), slot[HG],
                                                    start=False, stop=True, skip_group_check=True)

                        if g < G - 1:
                            nums().then_inc(num_full, 1)
                            dens().then_inc(heads_used, 1)
                        else:
                            dens().then_inc(den_full, 1)
                            nums().then_inc(num_full, 1)

                    def out_proj(k, t):
                        bank_free(k, "O", t)
                        n = 0
                        for g in range(G):
                            if t == 0:
                                pe.wait_ge(norm_lo, 2 + (G * (BLK * b + k) + g))
                            for s, m in PASSES:
                                mm = nc.tensor.matmul(bank_of(k, "O", t)[:], u[:, s, g, t * P:(t + 1) * P], wo[:, m, g],
                                                      start=(n == 0), stop=(n == 3 * G - 1))
                                n += 1
                        mm.then_inc(filled, 1)

                    def transposes(k, t):
                        bank_free(k, "T", t)
                        pe.wait_ge(xn_set, 2 + (TT * BLK * b + TT * k + t))
                        for c in range(C):
                            mm = nc.tensor.transpose(bank_of(k, "T", t)[:, c * P:(c + 1) * P],
                                                     xn[:, t % 2, c * P:(c + 1) * P], ident[:])
                        mm.then_inc(filled, 1)

                    for n in range(NS):
                        maxima(0, n)
                    turn_maxima(0)
                    for k in range(BLK):
                        i = b * BLK + k
                        more = k + 1 < BLK
                        scores(k, 0)
                        scores(k, 1)
                        pe.wait_ge(dve_read, 2 + job(b, k, "MT"))
                        for n in range(NS):
                            if n >= 2:
                                scores(k, n)
                            shift(k, n)
                            if more:
                                maxima(k + 1, n)
                            if n % SU == SU - 1 and n > SU:
                                attend_group(k, n // SU - 1)
                        attend_group(k, G - 1)
                        pe.wait_ge(rec_set, 2 + i)
                        for g in range(G):
                            bank_free(k, "R", g)
                            nc.tensor.matmul(bank_of(k, "R", g)[:], spread[:, g], den[:, 1], start=True, stop=True)\
                                .then_inc(filled, 1)
                        out_proj(k, 0)
                        if more:
                            turn_maxima(k + 1)
                        out_proj(k, 1)
                        out_proj(k, 2)
                        transposes(k, 0)
                        out_proj(k, 3)
                        transposes(k, 1)
                        transposes(k, 2)
                        transposes(k, 3)


def experts(nc, a, NB, BLK, x2_dram, x3_dram, out_bat, ident):
    NT = BLK * TT
    WG, WU, WD = 0, C * FE, 2 * C * FE
    WN = 2 * C * FE + FT * D
    with ExitStack() as ctx:
        def sb(name, shape, dt=F32):
            return ctx.enter_context(nc.sbuf_tensor("ex_" + name, shape, dt))

        def sem(name):
            return primed(ctx, nc, sems, "ex_" + name)

        sems = []

        x3 = sb("x3", [P, 2, BLK, C * TB], F32R)
        acc = sb("acc", [P, NT, D])
        w_raw = sb("w_raw", [P, WN])
        w = sb("w", [P, 2, 2, WN], F32R)
        s_g = sb("s_g", [P, FT, TB])
        h = sb("h", [P, FT, TB])
        ht = sb("ht", [P, 2, 2, FT, TB], F32R)
        r_raw = sb("r_raw", [P, C, P])
        r_w = sb("r_w", [P, 2, C, P], F32R)
        lt = sb("lt", [P, NT, E])
        total = sb("total", [P, NT])
        top = sb("top", [P, NT])
        ex = sb("ex", [P, NT, E])
        gt = sb("gt", [P, NT, E, E])
        lower = sb("lower", [P, E * E])
        rank = sb("rank", [P, NT, E])
        rank2 = sb("rank2", [P, NT, E])
        share = sb("share", [P, NT, UNITS])
        pg = [ctx.enter_context(nc.psum_tensor(f"ex_pg{n}", [P, 512], F32)) for n in range(2 * FT)]
        pd = [ctx.enter_context(nc.psum_tensor(f"ex_pd{n}", [P, 512], F32)) for n in range(4)]

        x3_in, x3_hi, x3_lo = [sem("x3_in0"), sem("x3_in1")], sem("x3_hi"), sem("x3_lo")
        acc_in, const_in, out_done = sem("acc_in"), sem("const_in"), sem("out_done")
        w_in, w_hi, w_lo = sem("w_in"), sem("w_hi"), sem("w_lo")
        r_hi, r_lo = sem("r_hi"), sem("r_lo")
        lg_full, lg_taken, lt_full, lt_taken = sem("lg_full"), sem("lg_taken"), sem("lt_full"), sem("lt_taken")
        own, exp_set, share_set = sem("own"), sem("exp_set"), sem("share_set")
        OWN = 13
        gu_full, silu_set, h_set, ht_hi, ht_lo = (sem("gu_full"), sem("silu_set"), sem("h_set"), sem("ht_hi"),
                                                  sem("ht_lo"))
        d_full, d_taken = sem("d_full"), sem("d_taken")
        prime(nc, total, sems)

        PAIRS = UNITS // 2
        STEPS = 2 * BLK
        stage = (s_g[:].rearrange("p f t -> p (f t)"), h[:].rearrange("p f t -> p (f t)"))
        HALF = FT * TB
        NX = BLK * C * TB // HALF
        lg = [stage[k // 2][0:E, (k % 2) * TB:(k % 2 + 1) * TB] for k in range(BLK)]

        with nc.Block() as block:
            @block.sync
            def _(sp):
                sp.dma_start(r_raw[:], a["router"].rearrange("(c p) n -> p c n", p=P)).then_inc(const_in, 16)
                sp.dma_start(lower[:], a["lower"]).then_inc(const_in, 16)
                for b in range(NB):
                    if b:
                        sp.wait_ge(d_taken, 1 + PAIRS * STEPS * TT * b)
                    for n in range(NX):
                        k, part = n // 2, n % 2
                        if n >= 2:
                            sp.wait_ge(x3_lo, 1 + NX * b + n - 1)
                        sp.dma_start(stage[n % 2], x3_dram[b * BLK + k][:, part * HALF:(part + 1) * HALF])\
                            .then_inc(x3_in[n % 2], 16)
                    if b == 0:
                        sp.dma_start(w_raw[:], a["units"][0]).then_inc(w_in, 16)
                    else:
                        sp.wait_ge(out_done, 1 + 16 * b)
                    sp.dma_start(acc[:].rearrange("p (k t) d -> p k (t d)", k=BLK),
                                 x2_dram[b * BLK:(b + 1) * BLK].rearrange("k p n -> p k n")).then_inc(acc_in, 16)
                    with sp.Fori(0, UNITS) as e:
                        sp.wait_ge(w_lo, 1 + e + (b * UNITS + 1))
                        sp.dma_start(w_raw[:], a["units"][e + 1]).then_inc(w_in, 16)
                    sp.wait_ge(d_taken, 1 + PAIRS * STEPS * TT * (b + 1))
                    sp.dma_start(out_bat[b], acc[:]).then_inc(out_done, 16)
                sp.wait_ge(out_done, 1 + 16 * NB)

            @block.gpsimd
            def _(pool):
                nc.gpsimd.memset(share[:], 1.0).then_inc(share_set, 1)

            @block.scalar
            def _(act):
                act.wait_ge(const_in, 33)
                nc.scalar.copy(r_w[:, HI], r_raw[:]).then_inc(r_hi, 1)
                for b in range(NB):
                    if b:
                        act.wait_ge(gu_full, 1 + 2 * FT * STEPS * PAIRS * b)
                    for n in range(NX):
                        k, part = n // 2, n % 2
                        act.wait_ge(x3_in[n % 2], 1 + 16 * (NX // 2 * b + n // 2 + 1))
                        nc.scalar.copy(x3[:, HI, k, part * HALF:(part + 1) * HALF], stage[n % 2]).then_inc(x3_hi, 1)
                    if b == 0:
                        act.wait_ge(w_in, 17)
                        nc.scalar.copy(w[:, 0, HI], w_raw[:]).then_inc(w_hi, 1)
                    act.wait_ge(own, 1 + OWN * b + 2)
                    nc.scalar.activation(ex[:], ex[:], ACT.Exp).then_inc(exp_set, 1)
                    with act.Fori(0, PAIRS) as p:
                        q = p + b * PAIRS
                        for s in range(STEPS):
                            step = q * STEPS + s
                            for f in range(FT):
                                act.wait_ge(gu_full, 1 + step * (2 * FT) + 2 * f + 1)
                                act.wait_ge(h_set, 1 + step * FT + (f + 1 - FT if s else 0))
                                nc.scalar.activation(s_g[:, f], pg[2 * f][:], ACT.Silu).then_inc(silu_set, 1)
                            for f in range(FT):
                                act.wait_ge(h_set, 1 + step * FT + f + 1)
                                nc.scalar.copy(ht[:, s % 2, HI, f], h[:, f]).then_inc(ht_hi, 1)
                            if s == 1:
                                act.wait_ge(w_in, 1 + q * 32 + 32)
                                nc.scalar.copy(w[:, 1, HI], w_raw[:]).then_inc(w_hi, 1)
                            if s == BLK + 1:
                                act.wait_ge(w_in, 1 + q * 32 + 48)
                                nc.scalar.copy(w[:, 0, HI], w_raw[:]).then_inc(w_hi, 1)

            @block.vector
            def _(dve):
                dve.wait_ge(r_hi, 2)
                nc.vector.tensor_tensor(r_w[:, LO], r_raw[:], r_w[:, HI].bitcast(F32), ALU.subtract).then_inc(r_lo, 1)

                def split_w(slot, n):
                    dve.wait_ge(w_hi, 1 + n)
                    nc.vector.tensor_tensor(w[:, slot, LO], w_raw[:], w[:, slot, HI].bitcast(F32),
                                            ALU.subtract).then_inc(w_lo, 1)

                def router(b):
                    dve.wait_ge(x3_lo, 1 + NX * (b + 1))
                    for k in range(BLK):
                        dve.wait_ge(lg_full, 1 + BLK * b + k + 1)
                        nc.vector.tensor_copy(lg[k], pg[k][0:E, :]).then_inc(lg_taken, 1)
                    dve.wait_ge(lt_full, 1 + b + 1)
                    nc.vector.tensor_copy(lt[:].rearrange("p n e -> p (n e)"), pd[0][:, 0:NT * E]).then_inc(lt_taken, 1)
                    dve.wait_ge(lt_taken, 1 + b + 1)
                    count = [OWN * b]

                    def chain(ins):
                        count[0] += 1
                        ins.then_inc(own, 1)
                        dve.wait_ge(own, 1 + count[0])

                    per_e = lt[:].rearrange("p n (e o) -> p n e o", o=1).broadcast_to([P, NT, E, E])
                    per_f = lt[:].rearrange("p n (o e) -> p n o e", o=1).broadcast_to([P, NT, E, E])
                    low = lower[:].rearrange("p (o n) -> p o n", o=1).broadcast_to([P, NT, E * E])
                    gt_flat = gt[:].rearrange("p n e f -> p n (e f)")
                    per_n = lambda t: t[:].rearrange("p (n o) -> p n o", o=1).broadcast_to([P, NT, E])
                    chain(nc.vector.tensor_reduce(top[:], lt[:], AX.X, ALU.max))
                    chain(nc.vector.tensor_tensor(ex[:], lt[:], per_n(top), ALU.subtract))
                    chain(nc.vector.tensor_tensor(gt[:], per_f, per_e, ALU.is_gt))
                    chain(nc.vector.tensor_reduce(rank[:], gt[:], AX.X, ALU.add))
                    chain(nc.vector.tensor_tensor(gt[:], per_f, per_e, ALU.is_equal))
                    chain(nc.vector.tensor_tensor(gt_flat, gt_flat, low, ALU.mult))
                    chain(nc.vector.tensor_reduce(rank2[:], gt[:], AX.X, ALU.add))
                    chain(nc.vector.tensor_tensor(rank[:], rank[:], rank2[:], ALU.add))
                    chain(nc.vector.tensor_scalar(rank[:], rank[:], TOP - 0.5, None, ALU.is_lt))
                    dve.wait_ge(exp_set, 1 + b + 1)
                    chain(nc.vector.tensor_reduce(top[:], ex[:], AX.X, ALU.add))
                    chain(nc.vector.reciprocal(total[:], top[:]))
                    chain(nc.vector.tensor_tensor(ex[:], ex[:], per_n(total), ALU.mult))
                    chain(nc.vector.tensor_tensor(share[:, :, 0:E], ex[:], rank[:], ALU.mult))
                    assert count[0] == OWN * (b + 1)

                def add_down(e, step, s):
                    k = s % BLK
                    for t in range(TT):
                        n = k * TT + t
                        dve.wait_ge(d_full, 1 + step * TT + t + 1)
                        nc.vector.scalar_tensor_tensor(acc[:, n], pd[t][:], share[:, n, bass.ds(e + s // BLK, 1)],
                                                       acc[:, n], ALU.mult, ALU.add).then_inc(d_taken, 1)

                for b in range(NB):
                    for n in range(NX):
                        k, part = n // 2, slice((n % 2) * HALF, (n % 2 + 1) * HALF)
                        dve.wait_ge(x3_hi, 1 + NX * b + n + 1)
                        nc.vector.tensor_tensor(x3[:, LO, k, part], stage[n % 2], x3[:, HI, k, part].bitcast(F32),
                                                ALU.subtract).then_inc(x3_lo, 1)
                    if b == 0:
                        split_w(0, 1)
                        dve.wait_ge(share_set, 2)
                    router(b)
                    dve.wait_ge(acc_in, 1 + 16 * (b + 1))
                    with dve.Fori(0, PAIRS) as p:
                        q = p + b * PAIRS
                        for s in range(STEPS):
                            step = q * STEPS + s
                            for f in range(FT):
                                dve.wait_ge(ht_lo, 1 + step * FT + (f + 1 - FT if s else 0))
                                dve.wait_ge(silu_set, 1 + step * FT + f + 1)
                                dve.wait_ge(gu_full, 1 + step * (2 * FT) + 2 * f + 2)
                                nc.vector.tensor_tensor(h[:, f], s_g[:, f], pg[2 * f + 1][:], ALU.mult).then_inc(h_set, 1)
                            for f in range(FT):
                                dve.wait_ge(ht_hi, 1 + step * FT + f + 1)
                                nc.vector.tensor_tensor(ht[:, s % 2, LO, f], h[:, f], ht[:, s % 2, HI, f].bitcast(F32),
                                                        ALU.subtract).then_inc(ht_lo, 1)
                            if s == 1:
                                split_w(1, q * 2 + 2)
                            if s == BLK + 1:
                                split_w(0, q * 2 + 3)
                            if s:
                                add_down(p * 2, step - 1, s - 1)
                        add_down(p * 2, q * STEPS + (STEPS - 1), STEPS - 1)

            @block.tensor
            def _(pe):
                pe.wait_ge(r_lo, 2)

                def router(b):
                    for k in range(BLK):
                        pe.wait_ge(x3_lo, 1 + NX * b + 2 * k + 2)
                        if b:
                            pe.wait_ge(h_set, 1 + FT * STEPS * PAIRS * b)
                        n = 0
                        for c in range(C):
                            for s, m in PASSES:
                                mm = nc.tensor.matmul(pg[k][:], r_w[:, s, c], x3[:, m, k, c * TB:(c + 1) * TB],
                                                      start=(n == 0), stop=(n == 3 * C - 1))
                                n += 1
                        mm.then_inc(lg_full, 1)
                    pe.wait_ge(lg_taken, 1 + BLK * (b + 1))
                    if b:
                        pe.wait_ge(d_taken, 1 + PAIRS * STEPS * TT * b)
                    for k in range(BLK):
                        for t in range(TT):
                            n = k * TT + t
                            mm = nc.tensor.transpose(pd[0][:, n * E:(n + 1) * E], lg[k][:, t * P:(t + 1) * P],
                                                     ident[0:E, 0:E])
                    mm.then_inc(lt_full, 1)

                def gate_up(s, step):
                    k, slot = s % BLK, s // BLK
                    for f in range(FT):
                        for which, start in ((0, WG), (1, WU)):
                            pe.wait_ge((silu_set, h_set)[which], 1 + step * FT + (f + 1 - FT if s else 0))
                            n = 0
                            for c in range(C):
                                col = start + c * FE + f * P
                                for sp_, m in PASSES:
                                    mm = nc.tensor.matmul(pg[2 * f + which][:], w[:, slot, sp_, col:col + P],
                                                          x3[:, m, k, c * TB:(c + 1) * TB],
                                                          start=(n == 0), stop=(n == 3 * C - 1))
                                    n += 1
                            mm.then_inc(gu_full, 1)

                def down(s, step):
                    slot = s // BLK
                    pe.wait_ge(ht_lo, 1 + step * FT + FT)
                    for t in range(TT):
                        pe.wait_ge(d_taken, 1 + step * TT + (t + 1 - TT if s else 0))
                        n = 0
                        for f in range(FT):
                            for sp_, m in PASSES:
                                mm = nc.tensor.matmul(pd[t][:], ht[:, s % 2, sp_, f, t * P:(t + 1) * P],
                                                      w[:, slot, m, WD + f * D:WD + (f + 1) * D],
                                                      start=(n == 0), stop=(n == 3 * FT - 1))
                                n += 1
                        mm.then_inc(d_full, 1)

                for b in range(NB):
                    router(b)
                    pe.wait_ge(lt_taken, 1 + b + 1)
                    with pe.Fori(0, PAIRS) as p:
                        q = p + b * PAIRS
                        for s in range(STEPS):
                            if s % BLK == 0:
                                pe.wait_ge(w_lo, 1 + q * 2 + (s // BLK + 1))
                            gate_up(s, q * STEPS + s)
                            if s:
                                down(s - 1, q * STEPS + (s - 1))
                        down(STEPS - 1, q * STEPS + (STEPS - 1))


def kernel(**inputs):
    import concourse.bacc as bacc
    from concourse.bass_utils import run_bass_kernel_spmd

    f = {k.removeprefix("L0_"): np.asarray(v) for k, v in inputs.items()}
    proj = f["attn_proj_matrix"]
    features = np.zeros((P, G, HG, F), np.float32)
    for h in range(H):
        g, j = h // HG, h % HG
        features[j * HD:(j + 1) * HD, g, j] = proj[h]
    ctx = f["ctx_1024"].transpose(0, 2, 1)
    rest = np.concatenate([ctx[:, :, P:], np.repeat(ctx[:, :, -1:], KPAD - KREM, 2)], 2)
    ctx_t = np.concatenate([ctx[:, :, :P], rest, rest, rest, rest, rest], 2)

    def chunks(w):
        return w.reshape(-1, P, w.shape[1]).transpose(1, 0, 2).reshape(P, -1)

    gates = list(f["ffn_w_gate"]) + np.split(f["ffn_ws_gate"], 2, axis=1)
    ups = list(f["ffn_w_up"]) + np.split(f["ffn_ws_up"], 2, axis=1)
    downs = list(f["ffn_w_down"]) + np.split(f["ffn_ws_down"], 2, axis=0)
    units = [np.concatenate([chunks(g), chunks(u), chunks(d)], 1) for g, u, d in zip(gates, ups, downs)]
    router = np.zeros((D, P), np.float32)
    router[:, :E] = f["ffn_router_w"]
    arrays = {
        "x": f["x"], "w_qkv": f["attn_w_qkv"], "features": features.reshape(P, -1),
        "features3": np.concatenate([proj.transpose(1, 0, 2).reshape(HD, -1)] * 3, 0), "w_out": f["attn_w_out"],
        "b_out": f["attn_b_out"].reshape(1, D), "ctxT": ctx_t,
        "WqT": f["xattn_Wq"].T, "WkT": f["xattn_Wk"].T, "WvT": f["xattn_Wv"].T, "WoT": f["xattn_Wo"].T,
        "bqT": f["xattn_bq"].reshape(C, P).T, "bkT": f["xattn_bk"].reshape(C, P).T,
        "bv": f["xattn_bv"].reshape(1, D), "bo": f["xattn_bo"].reshape(1, D),
        "router": router, "units": np.stack(units + units[:1]),
    }
    arrays.update(constants())
    arrays = {"in_" + k: np.ascontiguousarray(v) for k, v in arrays.items()}

    nc = bacc.Bacc("TRN2", target_bir_lowering=False, num_devices=1)
    aps = {k[3:]: nc.dram_tensor(k, v.shape, mybir.dt.from_np(v.dtype), kind="ExternalInput").ap()
           for k, v in arrays.items()}
    out = nc.dram_tensor("out", f["x"].shape, F32, kind="ExternalOutput").ap()
    decoder_kernel(nc, aps, out)
    got = run_bass_kernel_spmd(nc, [arrays], core_ids=[0])
    return got.results[0]["out"]
```

```python
from contextlib import ExitStack

import concourse.bass as bass
import numpy as np
from concourse import mybir

F32 = mybir.dt.float32
F32R = mybir.dt.float32r
BF16 = mybir.dt.bfloat16
ALU = mybir.AluOpType
ACT = mybir.ActivationFunctionType
AX = mybir.AxisListType

P = 128
HI, LO = 0, 1
PASSES = ((HI, HI), (HI, LO), (LO, HI))

D = 512
C = D // P
H = 16
HD = D // H
HG = P // HD
G = H // HG
F = 128
TB = 512
TT = TB // P
KEYS = 154
KREM = KEYS - P
KPAD = 32
E = 8
TOP = 6
FE = 256
UNITS = E + 2
FT = FE // P
UNIT = 2 * C * FE + FT * D
X3_SLOTS = 3
X3_PART = FT * TB
EPS = 1e-5


def primed(ctx, nc, sems, name):
    sems.append(ctx.enter_context(nc.semaphore(name)))
    return sems[-1]


def prime(nc, pause, sems):
    with nc.Block() as block:
        @block.gpsimd
        def _(pool):
            for s in sems:
                pool.sem_inc(s, 1)


def staged(stage, n):
    return stage[:, n * C * D:(n + 1) * C * D].rearrange("p (c n) -> p c n", c=C)


def x3_slot(stage, n):
    first = UNIT + n % X3_SLOTS * X3_PART
    return stage[:, first:first + X3_PART]


def x3_part(x3_dram, n):
    per = C * TB // X3_PART
    return x3_dram[n // per][:, n % per * X3_PART:(n % per + 1) * X3_PART]


class Tally:

    def __init__(self, jobs, banks):
        self.pos = {key: n for n, (key, _, _) in enumerate(jobs)}
        self.jobs, self.banks, self.n = jobs, banks, len(jobs)
        self.n_act = sum(a for _, a, _ in jobs)
        self.n_dve = sum(d for _, _, d in jobs)

    def filled(self, key):
        return self.pos[key] + 1

    def act(self, key):
        return sum(a for _, a, _ in self.jobs[:self.pos[key] + 1])

    def dve(self, key):
        return sum(d for _, _, d in self.jobs[:self.pos[key] + 1])

    def bank(self, key):
        return self.pos[key] % self.banks


def constants():
    ident = np.eye(P, dtype=np.float32)
    quad = np.arange(P) // HD
    key = np.arange(P) % HD
    mask = (quad[:, None] == np.arange(HG)).astype(np.float32)
    mask_keys = mask * (key < KREM)[:, None]
    one_col = np.zeros((P, G, HD), np.float32)
    rem_ones = np.zeros((P, G, P), np.float32)
    spread = np.zeros((P, G, P), np.float32)
    for g in range(G):
        one_col[:, g, g] = 1
        for p in range(P):
            if key[p] < KREM:
                rem_ones[p, g, 32 * quad[p] + g] = 1
            spread[32 * quad[p] + g, g, p] = 1
    minus = np.zeros((P, G, HG + 1, P), np.float32)
    for g in range(G):
        for j in range(HG):
            for r in (HG * g + j, H + HG * g + j):
                minus[r, g, j, :] = -1
                minus[r, g, HG, 32 * j:32 * j + 32] = -1
    lower = np.zeros((P, E, E), np.float32)
    for e in range(E):
        lower[:, e, :e] = 1
    small = np.concatenate([mask, mask_keys], 1)
    return {
        "ident": ident, "small": small, "one_col": one_col.reshape(P, -1), "rem_ones": rem_ones.reshape(P, -1),
        "spread": spread.reshape(P, -1), "minus": minus.reshape(P, -1), "lower": lower.reshape(P, -1),
    }


def decoder_kernel(nc, a, out):
    NB = a["x"].shape[0]
    BLK = a["x"].shape[1] // TB
    NBLK = NB * BLK
    x_blk = a["x"].rearrange("b (k t p) d -> (b k) p t d", t=TT, p=P)
    out_bat = out.rearrange("b (n p) d -> b p n d", p=P)
    x2_dram = nc.dram_tensor("x2_scratch", [NBLK, P, TT * D], F32).ap()
    q_dram = nc.dram_tensor("q_scratch", [NBLK, 2, HD, H * TB], F32).ap()
    x1_dram = nc.dram_tensor("x1_scratch", [NBLK, P, TT * D], F32).ap()
    xq_dram = nc.dram_tensor("xq_scratch", [NBLK, P, C * TB], F32).ap()
    x3_dram = nc.dram_tensor("x3_scratch", [NBLK, P, C * TB], F32).ap()

    with ExitStack() as whole:
        ident = whole.enter_context(nc.sbuf_tensor("ident", [P, P], F32))
        half = whole.enter_context(nc.sbuf_tensor("half", [P, TT], F32))
        stage = whole.enter_context(nc.sbuf_tensor("stage", [P, 3 * C * D], F32))
        with ExitStack() as linear:
            kv_w = linear.enter_context(nc.sbuf_tensor("kv_w", [P, NB, H, HD], F32))
            ks_w = linear.enter_context(nc.sbuf_tensor("ks_w", [P, NB, H, HD], F32))
            project(nc, a, NBLK, BLK, x_blk, q_dram, ident, kv_w, ks_w, half, stage)
            attend_linear(nc, a, NBLK, BLK, x_blk, q_dram, x1_dram, xq_dram, ident, kv_w, ks_w, half, stage)
        attend_cross(nc, a, NB, BLK, x1_dram, xq_dram, x2_dram, x3_dram, ident, half, stage)
        experts(nc, a, NB, BLK, x2_dram, x3_dram, out_bat, ident, stage)


def project(nc, a, NBLK, BLK, x_blk, q_dram, ident, kv_w, ks_w, half, stage):
    T = Tally([(("T", t), 1, 1) for t in range(TT)] + [(("K", g), 1, 1) for g in range(G)]
              + [(("Q", g), 1, 1) for g in range(G)] + [(("V", t), 0, 1) for t in range(TT)]
              + [(("KP", n), 1, 1) for n in range(TT * G)], 2)
    NKP = TT * G
    LAG = 3
    with ExitStack() as ctx:
        def sb(name, shape, dt=F32):
            return ctx.enter_context(nc.sbuf_tensor("pr_" + name, shape, dt))

        def sem(name):
            return primed(ctx, nc, sems, "pr_" + name)

        sems = []

        w = sb("w", [P, 2, 3, C, D], F32R)
        f_raw = sb("f_raw", [P, G, HG * F])
        f_w = sb("f_w", [P, 2, G, HG * F], F32R)
        x = sb("x", [P, TT, D])
        xn = sb("xn", [P, TT, D])
        xt = sb("xt", [P, 2, C, TB], F32R)
        kt = sb("kt", [P, 2, C, TB], F32R)
        qs = sb("qs", [P, 2, C, TB], F32R)
        v = sb("v", [P, TT, D])
        e = sb("e", [P, 4, HG * F])
        kp = sb("kp", [P, 4, HG * F])
        stats = sb("stats", [P, TT, 6])
        mv = sb("mv", [P, TT, 2])
        rstd = sb("rstd", [P, TT])
        pause = sb("pause", [P, 1])
        ones = sb("ones", [P, HD])
        kv_sum = sb("kv_sum", [P, NBLK // BLK, G * F])
        ks_sum = sb("ks_sum", [P, NBLK // BLK, HG * F])
        pj = [ctx.enter_context(nc.psum_tensor(f"pr_pj{n}", [P, 512], F32)) for n in range(2)]
        pk = [ctx.enter_context(nc.psum_tensor(f"pr_pk{n}", [P, 512], F32)) for n in range(4)]
        p_kv = ctx.enter_context(nc.psum_tensor("pr_p_kv", [P, 512], F32))
        p_ks = ctx.enter_context(nc.psum_tensor("pr_p_ks", [P, 512], F32))

        w_in, x_in, q_out = [sem(f"w_in{n}") for n in range(3)], sem("x_in"), sem("q_out")
        f_in, next_in = sem("f_in"), sem("next_in")
        const_in, const_set = sem("const_in"), sem("const_set")
        w_hi, w_lo = sem("w_hi"), sem("w_lo")
        filled, act_read, dve_read = sem("filled"), sem("act_read"), sem("dve_read")
        stats_set, var_set, rstd_set, xn_set = sem("stats_set"), sem("var_set"), sem("rstd_set"), sem("xn_set")
        relu_set, kv_step, kv_taken = sem("relu_set"), sem("kv_step"), sem("kv_taken")
        turned, kv_done = sem("turned"), sem("kv_done")

        prime(nc, pause, sems)

        def bank_of(key):
            return pk[key[1] % 4] if key[0] == "KP" else pj[T.bank(key)]

        with nc.Block() as block:
            @block.sync
            def _(sp):
                sp.dma_start(x[:], x_blk[0]).then_inc(x_in, 16)
                sp.dma_start(ident[:], a["ident"]).then_inc(const_in, 16)
                w_src = a["w_qkv"].rearrange("(c p) (n d) -> p c n d", p=P, n=3)
                for n in (1, 0, 2):
                    sp.dma_start(staged(stage, n), w_src[:, :, n]).then_inc(w_in[n], 16)
                sp.dma_start(f_raw[:], a["features"].rearrange("p (g f) -> p g f", g=G)).then_inc(f_in, 16)
                sp.wait_ge(w_lo, 1 + 4)
                sp.dma_start(stage[0:3 * HD, 0:H * F], a["features3"]).then_inc(next_in, 16)
                sp.dma_start(staged(stage, 1), a["w_out"].rearrange("(c p) n -> p c n", p=P)).then_inc(next_in, 16)
                sp.dma_start(staged(stage, 2), a["WqT"].rearrange("(c p) n -> p c n", p=P)).then_inc(next_in, 16)

                def block_io(i, last):
                    if not last:
                        sp.wait_ge(xn_set, 1 + TT * i + TT)
                        sp.dma_start(x[:], x_blk[i + 1]).then_inc(x_in, 16)
                    sp.wait_ge(dve_read, 1 + T.n_dve * i + T.dve(("Q", G - 1)))
                    for s in (HI, LO):
                        for j in range(HG):
                            sp.dma_start(q_dram[i, s].rearrange("d (g j t) -> d g j t", g=G, j=HG)[:, :, j],
                                         qs[j * HD:(j + 1) * HD, s].bitcast(F32)).then_inc(q_out, 16)

                with sp.Fori(0, NBLK - 1) as i:
                    block_io(i, False)
                block_io(NBLK - 1, True)
                sp.wait_ge(q_out, 1 + 16 * 2 * HG * NBLK)
                sp.wait_ge(next_in, 1 + 48)

            @block.gpsimd
            def _(pool):
                nc.gpsimd.memset(half[:], -0.5).then_inc(const_set, 1)
                nc.gpsimd.memset(ones[:], 1.0).then_inc(const_set, 1)
                nc.gpsimd.memset(ks_w[:], 0.0).then_inc(const_set, 1)
                nc.gpsimd.memset(kv_sum[:], 0.0).then_inc(const_set, 1)
                nc.gpsimd.memset(ks_sum[:], 0.0).then_inc(const_set, 1)
                pool.wait_ge(const_set, 2)
                with pool.Fori(0, NBLK) as i:
                    pool.wait_ge(var_set, 1 + i + 1)
                    nc.gpsimd.tensor_tensor(rstd[:], mv[:, :, 1], half[:], ALU.pow).then_inc(rstd_set, 1)

            @block.scalar
            def _(act):
                def split_w(n):
                    act.wait_ge(w_in[n], 1 + 16)
                    nc.scalar.copy(w[:, HI, n], staged(stage, n)).then_inc(w_hi, 1)

                def turn(i):
                    for t in range(TT):
                        act.wait_ge(filled, 1 + T.n * i + T.filled(("T", t)))
                        nc.scalar.copy(xt[:, HI, :, t * P:(t + 1) * P],
                                       bank_of(("T", t))[:].rearrange("p (c n) -> p c n", c=C)).then_inc(act_read, 1)

                def heads(i):
                    for g in range(G):
                        act.wait_ge(filled, 1 + T.n * i + T.filled(("K", g)))
                        nc.scalar.copy(kt[:, HI, g], bank_of(("K", g))[:]).then_inc(act_read, 1)
                    act.wait_ge(q_out, 1 + 16 * 2 * HG * i)
                    for g in range(G):
                        act.wait_ge(filled, 1 + T.n * i + T.filled(("Q", g)))
                        nc.scalar.copy(qs[:, HI, g], bank_of(("Q", g))[:]).then_inc(act_read, 1)
                    for n in range(NKP + 1):
                        if n < NKP:
                            act.wait_ge(filled, 1 + T.n * i + T.filled(("KP", n)))
                            nc.scalar.activation(e[:, n % 4], bank_of(("KP", n))[:], ACT.Relu, scale=-1.0)\
                                .then_inc(relu_set, 1)
                        if n:
                            act.wait_ge(relu_set, 1 + NKP * i + n)
                            nc.scalar.activation(e[:, (n - 1) % 4], e[:, (n - 1) % 4], ACT.Exp, scale=-1.0)\
                                .then_inc(act_read, 1)

                split_w(1)
                turn(0)
                split_w(0)
                split_w(2)
                act.wait_ge(f_in, 1 + 16)
                nc.scalar.copy(f_w[:, HI], f_raw[:]).then_inc(w_hi, 1)
                with act.Fori(0, NBLK - 1) as i:
                    heads(i)
                    turn(i + 1)
                heads(NBLK - 1)

            @block.vector
            def _(dve):
                def norm_stats(i, t):
                    if t == 0:
                        dve.wait_ge(x_in, 1 + 16 * i + 16)
                    nc.vector.bn_stats(stats[:, t], x[:, t]).then_inc(stats_set, 1)

                def norm_var(i):
                    dve.wait_ge(stats_set, 1 + TT * i + TT)
                    nc.vector.tensor_copy(pause[:], half[:, 0:1])
                    for t in range(TT):
                        nc.vector.bn_aggr(mv[:, t], stats[:, t]).then_inc(turned, 1)
                    dve.wait_ge(turned, 1 + TT * i + TT)
                    nc.vector.tensor_scalar(mv[:, :, 1], mv[:, :, 1], EPS, None, ALU.add).then_inc(var_set, 1)

                def norm(i):
                    dve.wait_ge(rstd_set, 1 + i + 1)
                    for t in range(TT):
                        nc.vector.tensor_scalar(xn[:, t], x[:, t], mv[:, t, 0:1], rstd[:, t:t + 1],
                                                ALU.subtract, ALU.mult).then_inc(xn_set, 1)

                def turn(i):
                    for t in range(TT):
                        part = slice(t * P, (t + 1) * P)
                        dve.wait_ge(act_read, 1 + T.n_act * i + T.act(("T", t)))
                        nc.vector.tensor_tensor(xt[:, LO, :, part], bank_of(("T", t))[:].rearrange("p (c n) -> p c n", c=C),
                                                xt[:, HI, :, part].bitcast(F32), ALU.subtract).then_inc(dve_read, 1)

                def heads(i, last):
                    for g in range(G):
                        dve.wait_ge(act_read, 1 + T.n_act * i + T.act(("K", g)))
                        nc.vector.tensor_tensor(kt[:, LO, g], bank_of(("K", g))[:], kt[:, HI, g].bitcast(F32),
                                                ALU.subtract).then_inc(dve_read, 1)
                    for g in range(G):
                        dve.wait_ge(act_read, 1 + T.n_act * i + T.act(("Q", g)))
                        nc.vector.tensor_tensor(qs[:, LO, g], bank_of(("Q", g))[:], qs[:, HI, g].bitcast(F32),
                                                ALU.subtract).then_inc(dve_read, 1)
                        if not last:
                            norm_stats(i + 1, g)
                    for t in range(TT):
                        dve.wait_ge(filled, 1 + T.n * i + T.filled(("V", t)))
                        nc.vector.tensor_copy(v[:, t], bank_of(("V", t))[:]).then_inc(dve_read, 1)
                        if t == 0 and not last:
                            norm_var(i + 1)
                    if not last:
                        norm(i + 1)
                    for n in range(NKP):
                        dve.wait_ge(kv_step, 1 + NKP * i + max(n - 3, 0))
                        dve.wait_ge(act_read, 1 + T.n_act * i + T.act(("KP", n)))
                        nc.vector.scalar_tensor_tensor(kp[:, n % 4], bank_of(("KP", n))[:], 0.0, e[:, n % 4],
                                                       ALU.max, ALU.add).then_inc(dve_read, 1)

                def add_kv(i, b):
                    dve.wait_ge(kv_step, 1 + NKP * i + NKP)
                    dve.wait_ge(kv_taken, 1 + 2 * i)
                    nc.vector.tensor_tensor(kv_sum[:, b], kv_sum[:, b], p_kv[:], ALU.add).then_inc(kv_taken, 1)
                    nc.vector.tensor_tensor(ks_sum[:, b], ks_sum[:, b], p_ks[:], ALU.add).then_inc(kv_taken, 1)

                dve.wait_ge(const_set, 2)
                for t in range(TT):
                    norm_stats(0, t)
                norm_var(0)
                norm(0)
                for count, n in enumerate((1, 0, 2)):
                    dve.wait_ge(w_hi, 1 + count + 1)
                    nc.vector.tensor_tensor(w[:, LO, n], staged(stage, n), w[:, HI, n].bitcast(F32),
                                            ALU.subtract).then_inc(w_lo, 1)
                    if n == 1:
                        turn(0)
                dve.wait_ge(w_hi, 1 + 4)
                nc.vector.tensor_tensor(f_w[:, LO], f_raw[:], f_w[:, HI].bitcast(F32), ALU.subtract).then_inc(w_lo, 1)
                dve.wait_ge(const_set, 6)
                for b in range(NBLK // BLK):
                    with dve.Fori(0, BLK - 1) as k:
                        i = k + BLK * b
                        heads(i, False)
                        turn(i + 1)
                        add_kv(i, b)
                    i = BLK * b + BLK - 1
                    heads(i, i == NBLK - 1)
                    if i < NBLK - 1:
                        turn(i + 1)
                    add_kv(i, b)
                for b in range(NBLK // BLK):
                    dve.wait_ge(kv_done, 1 + 2 * b + 1)
                    nc.vector.tensor_copy(kv_w[:, b].rearrange("p h d -> p (h d)"), pk[b][:]).then_inc(turned, 1)
                    dve.wait_ge(kv_done, 1 + 2 * b + 2)
                    flat = ks_w[:, b].rearrange("p h d -> p (h d)")
                    for j in range(HG):
                        nc.vector.tensor_copy(flat[:, j * HD:(H - HG + j) * HD + G:HG * HD + 1],
                                              pk[2 + b][:, j * P:(j + 1) * P:HD]).then_inc(turned, 1)

            @block.tensor
            def _(pe):
                def dve_has_read(i, key):
                    pe.wait_ge(dve_read, 1 + T.n_dve * i + T.dve(key))

                def turn(i, first):
                    for t in range(TT):
                        pe.wait_ge(xn_set, 1 + TT * i + t + 1)
                        if t >= 2:
                            dve_has_read(i, ("T", t - 2))
                        elif not first:
                            pe.wait_ge(dve_read, 1 + T.n_dve * (i - 1) + T.dve(("V", TT - 1)))
                        for c in range(C):
                            mm = nc.tensor.transpose(bank_of(("T", t))[:, c * P:(c + 1) * P],
                                                     xn[:, t, c * P:(c + 1) * P], ident[:])
                        mm.then_inc(filled, 1)

                def projections(i):
                    pe.wait_ge(w_lo, 1 + 1)
                    for g in range(G):
                        if g < 2:
                            dve_has_read(i, ("T", TT - 1))
                        else:
                            dve_has_read(i, ("K", g - 2))
                        matmuls(("K", g), lambda s, c, g=g: w[:, s, 1, c, g * P:(g + 1) * P],
                                lambda s, c: xt[:, s, c])
                    pe.wait_ge(w_lo, 1 + 2)
                    for g in range(G):
                        dve_has_read(i, ("Q", g - 2) if g > 1 else ("K", g + 2))
                        matmuls(("Q", g), lambda s, c, g=g: w[:, s, 0, c, g * P:(g + 1) * P],
                                lambda s, c: xt[:, s, c])
                    pe.wait_ge(w_lo, 1 + 4)
                    for t in range(TT):
                        dve_has_read(i, ("V", t - 2) if t > 1 else ("Q", t + 2))
                        matmuls(("V", t), lambda s, c, t=t: xt[:, s, c, t * P:(t + 1) * P],
                                lambda s, c: w[:, s, 2, c])

                def matmuls(key, stationary, moving):
                    n = 0
                    for c in range(C):
                        for s, m in PASSES:
                            mm = nc.tensor.matmul(bank_of(key)[:], stationary(s, c), moving(m, c),
                                                  start=(n == 0), stop=(n == C * 3 - 1))
                            n += 1
                    mm.then_inc(filled, 1)

                def features(i, n):
                    t, g = n // G, n % G
                    if n >= 4:
                        dve_has_read(i, ("KP", n - 4))
                    else:
                        dve_has_read(i, ("K", g))
                    for q, (s, m) in enumerate(PASSES):
                        mm = nc.tensor.matmul(pk[n % 4][:], kt[:, s, g, t * P:(t + 1) * P], f_w[:, m, g],
                                              start=(q == 0), stop=(q == 2))
                    mm.then_inc(filled, 1)

                def kv(i, n):
                    t, g = n // G, n % G
                    dve_has_read(i, ("KP", n))
                    if n == 0:
                        pe.wait_ge(kv_taken, 1 + 2 * i)
                    for j in range(HG):
                        h = g * HG + j
                        nc.tensor.matmul(p_kv[j * HD:(j + 1) * HD, g * F:(g + 1) * F], v[:, t, h * HD:(h + 1) * HD],
                                         kp[:, n % 4, j * F:(j + 1) * F], start=(t == 0 and g == 0), stop=(t == TT - 1),
                                         skip_group_check=True)
                    nc.tensor.matmul(p_ks[g * HD:(g + 1) * HD, :], ones[:], kp[:, n % 4], start=(t == 0),
                                     stop=(t == TT - 1), skip_group_check=True).then_inc(kv_step, 1)

                def block_work(i, last):
                    projections(i)
                    for n in range(NKP):
                        features(i, n)
                        if n >= LAG:
                            kv(i, n - LAG)
                    if not last:
                        turn(i + 1, False)
                    for n in range(NKP - LAG, NKP):
                        kv(i, n)

                pe.wait_ge(const_in, 17)
                pe.wait_ge(const_set, 3)
                turn(0, True)
                with pe.Fori(0, NBLK - 1) as i:
                    block_work(i, False)
                block_work(NBLK - 1, True)
                pe.wait_ge(kv_taken, 1 + 2 * NBLK)
                for b in range(NBLK // BLK):
                    for g in range(G):
                        mm = nc.tensor.transpose(pk[b][:, g * P:(g + 1) * P], kv_sum[:, b, g * P:(g + 1) * P], ident[:])
                    mm.then_inc(kv_done, 1)
                    for j in range(HG):
                        mm = nc.tensor.transpose(pk[2 + b][:, j * P:(j + 1) * P], ks_sum[:, b, j * P:(j + 1) * P], ident[:])
                    mm.then_inc(kv_done, 1)


def attend_linear(nc, a, NBLK, BLK, x_blk, q_dram, x1_dram, xq_dram, ident, kv_w, ks_w, half, stage):
    qp_pair = lambda n: [("QP", 2 * n), ("QP", 2 * n + 1)]
    JOBS = (qp_pair(0) + [("O", 0)] + qp_pair(1) + [("O", 1)] + qp_pair(2)
            + [("O", 2)] + qp_pair(3) + [("T", 0), ("O", 3)] + qp_pair(4) + [("T", 1)] + qp_pair(5) + [("T", 2)]
            + qp_pair(6) + [("T", 3)] + qp_pair(7) + [("XQ", 0), ("XQ", 1), ("XQ", 2)]
            + [("R", g) for g in range(G)] + [("XQ", 3)])
    POS = {key: n for n, key in enumerate(JOBS)}
    LAST_POS = {key: n for n, key in enumerate(j for j in JOBS if j[0] not in ("QP", "R"))}
    NJ, BANKS, QSLOTS, ESLOTS = len(JOBS), 4, 8, 4
    FIRST = H + G
    assert NJ % BANKS == 0 and FIRST % BANKS == 0
    with ExitStack() as ctx:
        def sb(name, shape, dt=F32):
            return ctx.enter_context(nc.sbuf_tensor("li_" + name, shape, dt))

        def sem(name):
            return primed(ctx, nc, sems, "li_" + name)

        sems = []
        f_w = sb("f_w", [3 * HD, H, F], F32R)
        wo = sb("wo", [P, 2, C, D], F32R)
        wq = sb("wq", [P, 2, C, D], F32R)
        spread_raw = sb("spread_raw", [P, G, P])
        spread = sb("spread", [P, G, P], F32R)
        rec = sb("rec", [P, 2, TB], F32R)
        bias = sb("bias", [P, D])
        bq = sb("bq", [P, C])
        x = sb("x", [P, TT, D])
        q3 = sb("q3", [3 * HD, H, TB], F32R)
        u_att = sb("u_att", [P, 2, C, TB], F32R)
        u_ln = sb("u_ln", [P, 2, C, TB], F32R)
        xn = sb("xn", [P, 2, D])
        qp = sb("qp", [P, QSLOTS, TB])
        e = sb("e", [P, ESLOTS, TB])
        num = sb("num", [P, G, TB])
        den = sb("den", [P, 2, TB])
        xq = sb("xq", [P, G, TB])
        stats = sb("stats", [P, TT, 6])
        mv = sb("mv", [P, TT, 2])
        rstd = sb("rstd", [P, TT])
        pause = sb("pause", [P, 1])
        bank = [ctx.enter_context(nc.psum_tensor(f"li_bank{n}", [P, 512], F32)) for n in range(BANKS)]
        p_num = [ctx.enter_context(nc.psum_tensor(f"li_p_num{n}", [P, 512], F32)) for n in range(2)]
        p_den = ctx.enter_context(nc.psum_tensor("li_p_den", [P, 512], F32))

        w_hi, w_lo, const_in, next_in = sem("w_hi"), sem("w_lo"), sem("const_in"), sem("next_in")
        x_in, q_in, x1_out, xq_out = sem("x_in"), sem("q_in"), sem("x1_out"), sem("xq_out")
        q0_in = [sem(f"q0_in{g}") for g in range(G)]
        filled, dve_read = sem("filled"), sem("dve_read")
        relu_set, exp_set, heads_used = sem("relu_set"), sem("exp_set"), sem("heads_used")
        num_full, num_taken, den_set, rec_set = sem("num_full"), sem("num_taken"), sem("den_set"), sem("rec_set")
        norm_hi, norm_lo, turn_hi = sem("norm_hi"), sem("norm_lo"), sem("turn_hi")
        xb_set, stats_set, aggr_set, var_set = sem("xb_set"), sem("stats_set"), sem("aggr_set"), sem("var_set")
        rstd_set, xn_set = sem("rstd_set"), sem("xn_set")
        prime(nc, pause, sems)

        f_raw = stage[0:3 * HD, 0:H * F].rearrange("p (h f) -> p h f", h=H)

        def pos(turn):
            return LAST_POS if isinstance(turn, int) and turn == NBLK - 1 else POS

        def job(turn, key):
            return FIRST + NJ * turn + pos(turn)[key]

        def bank_of(turn, key):
            return bank[pos(turn)[key] % BANKS]

        def is_first(block):
            return isinstance(block, int) and block == 0

        def ahead(block, key):
            return key[1] + H * (key[0] == "R") if is_first(block) else job(block - 1, key)

        def bank_ahead(block, key):
            return bank[key[1] % BANKS] if is_first(block) else bank_of(block - 1, key)

        def turns(engine, body):
            for b in range(NBLK // BLK):
                with engine.Fori(0, BLK - 1) as k:
                    body(k + BLK * b, b, True)
                body(BLK * b + BLK - 1, b + 1, b + 1 < NBLK // BLK)

        with nc.Block() as block:
            @block.sync
            def _(sp):
                def load_q(i):
                    for r, part in enumerate((HI, LO, HI)):
                        sp.dma_start(q3[r * HD:(r + 1) * HD].bitcast(F32).rearrange("p h t -> p (h t)"),
                                     q_dram[i, part]).then_inc(q_in, 16)

                for g in range(G):
                    for r, part in enumerate((HI, LO, HI)):
                        cols = slice(g * HG * TB, (g + 1) * HG * TB)
                        sp.dma_start(q3[r * HD:(r + 1) * HD].bitcast(F32).rearrange("p h t -> p (h t)")[:, cols],
                                     q_dram[0, part][:, cols]).then_inc(q0_in[g], 16)
                sp.dma_start(bq[:], a["bqT"]).then_inc(const_in, 16)
                sp.dma_start(spread_raw[:].rearrange("p g n -> p (g n)"), a["spread"]).then_inc(const_in, 16)
                sp.dma_start(bias[:], a["b_out"].broadcast_to([P, D])).then_inc(const_in, 16)
                sp.dma_start(x[:], x_blk[0]).then_inc(x_in, 16)
                sp.wait_ge(filled, 1 + H)
                load_q(1)
                sp.wait_ge(w_lo, 1 + 4)
                for n, name in enumerate(("WkT", "WvT", "WoT")):
                    sp.dma_start(staged(stage, n), a[name].rearrange("(c p) n -> p c n", p=P)).then_inc(next_in, 16)

                def turn(i, left):
                    sp.wait_ge(dve_read, 2 + job(i, ("O", TT - 1)))
                    sp.dma_start(x1_dram[i], x[:].rearrange("p t d -> p (t d)")).then_inc(x1_out, 16)
                    if left:
                        sp.wait_ge(x1_out, 17 + 16 * i)
                        sp.wait_ge(xn_set, 1 + TT * i + TT)
                        sp.dma_start(x[:], x_blk[i + 1]).then_inc(x_in, 16)
                    if left > 1:
                        sp.wait_ge(filled, 2 + job(i, ("QP", H - 1)))
                        load_q(i + 2)
                    sp.wait_ge(dve_read, 2 + job(i, ("XQ", G - 1)))
                    sp.dma_start(xq_dram[i], xq[:].rearrange("p g t -> p (g t)")).then_inc(xq_out, 16)

                with sp.Fori(0, NBLK - 2) as i:
                    turn(i, 2)
                turn(NBLK - 2, 1)
                turn(NBLK - 1, 0)
                sp.wait_ge(next_in, 1 + 48)
                sp.wait_ge(x1_out, 1 + 16 * NBLK)
                sp.wait_ge(xq_out, 1 + 16 * NBLK)

            @block.gpsimd
            def _(pool):
                pool.wait_ge(const_in, 1 + 48)
                rows = bias[:].rearrange("p (o d) -> p o d", o=1).broadcast_to([P, TT, D])
                with pool.Fori(0, NBLK) as i:
                    pool.wait_ge(x_in, 17 + 16 * i)
                    nc.gpsimd.tensor_tensor(x[:], x[:], rows, ALU.add).then_inc(xb_set, 1)
                    for t in range(TT):
                        pool.wait_ge(var_set, 2 + TT * i + t)
                        nc.gpsimd.tensor_tensor(rstd[:, t:t + 1], mv[:, t, 1:2], half[:, 0:1], ALU.pow)\
                            .then_inc(rstd_set, 1)

            @block.scalar
            def _(act):
                def heads(i, lo, hi):
                    for h in range(lo, hi + 1):
                        if h < hi:
                            act.wait_ge(filled, 2 + ahead(i, ("QP", h)))
                            nc.scalar.activation(e[:, h % ESLOTS], bank_ahead(i, ("QP", h))[:], ACT.Relu, scale=-1.0)\
                                .then_inc(relu_set, 1)
                        if h > lo:
                            s = e[:, (h - 1) % ESLOTS]
                            act.wait_ge(relu_set, 1 + H * i + h)
                            nc.scalar.activation(s, s, ACT.Exp, scale=-1.0).then_inc(exp_set, 1)

                def take_num(i, g):
                    act.wait_ge(num_full, 2 + G * i + g)
                    if not is_first(i):
                        act.wait_ge(norm_lo, 2 + G * (i - 1) + g)
                    nc.scalar.copy(num[:, g], p_num[g % 2][:]).then_inc(num_taken, 1)

                def normalised(i):
                    for g in range(G):
                        act.wait_ge(dve_read, 2 + ahead(i, ("R", g)))
                        nc.scalar.copy(u_att[:, HI, g], num[:, g]).then_inc(norm_hi, 1)

                def turned(i, t):
                    act.wait_ge(filled, 2 + job(i, ("T", t)))
                    nc.scalar.copy(u_ln[:, HI, :, t * P:(t + 1) * P],
                                   bank_of(i, ("T", t))[:].rearrange("p (c n) -> p c n", c=C)).then_inc(turn_hi, 1)

                def turn(i, b, more):
                    def next_heads(pair):
                        if more:
                            heads(i + 1, 2 * pair, 2 * pair + 2)

                    def next_num(g):
                        if more:
                            take_num(i + 1, g)

                    next_heads(0)
                    next_heads(1)
                    next_heads(2)
                    next_num(0)
                    next_heads(3)
                    turned(i, 0)
                    next_heads(4)
                    next_num(1)
                    turned(i, 1)
                    next_heads(5)
                    turned(i, 2)
                    next_heads(6)
                    next_num(2)
                    turned(i, 3)
                    next_heads(7)
                    next_num(3)
                    if more:
                        normalised(i + 1)

                nc.scalar.copy(f_w[:], f_raw).then_inc(w_hi, 1)
                heads(0, 0, H // 2)
                nc.scalar.copy(wo[:, HI], staged(stage, 1)).then_inc(w_hi, 1)
                take_num(0, 0)
                heads(0, H // 2, H)
                nc.scalar.copy(wq[:, HI], staged(stage, 2)).then_inc(w_hi, 1)
                for g in range(1, G):
                    take_num(0, g)
                normalised(0)
                turns(act, turn)

            @block.vector
            def _(dve):
                def heads(i, b, lo, hi):
                    for h in range(lo, hi):
                        if not (is_first(i) and h < QSLOTS):
                            dve.wait_ge(heads_used, 2 + G * i + (h - QSLOTS) // HG)
                        dve.wait_ge(exp_set, 2 + H * i + h)
                        nc.vector.scalar_tensor_tensor(qp[:, h % QSLOTS], bank_ahead(i, ("QP", h))[:], 0.0, e[:, h % ESLOTS],
                                                       ALU.max, ALU.add).then_inc(dve_read, 1)

                def divide(i):
                    dve.wait_ge(heads_used, 1 + G * i + G)
                    nc.vector.tensor_scalar(den[:, 0], p_den[:], 1e-8, None, ALU.add).then_inc(den_set, 1)
                    dve.wait_ge(den_set, 2 + i)
                    nc.vector.reciprocal(den[:, 1], den[:, 0]).then_inc(rec_set, 1)
                    dve.wait_ge(rec_set, 2 + 3 * i)
                    nc.vector.tensor_copy(rec[:, HI], den[:, 1]).then_inc(rec_set, 1)
                    dve.wait_ge(rec_set, 3 + 3 * i)
                    nc.vector.tensor_tensor(rec[:, LO], den[:, 1], rec[:, HI].bitcast(F32), ALU.subtract)\
                        .then_inc(rec_set, 1)

                def normalise(i):
                    for g in range(G + 1):
                        if g < G:
                            dve.wait_ge(num_taken, 2 + G * i + g)
                            dve.wait_ge(filled, 2 + ahead(i, ("R", g)))
                            nc.vector.tensor_tensor(num[:, g], num[:, g], bank_ahead(i, ("R", g))[:], ALU.mult)\
                                .then_inc(dve_read, 1)
                        if g:
                            dve.wait_ge(norm_hi, 1 + G * i + g)
                            nc.vector.tensor_tensor(u_att[:, LO, g - 1], num[:, g - 1], u_att[:, HI, g - 1].bitcast(F32),
                                                    ALU.subtract).then_inc(norm_lo, 1)

                def add_out(i, t):
                    if t == 0:
                        dve.wait_ge(xb_set, 2 + i)
                    dve.wait_ge(filled, 2 + job(i, ("O", t)))
                    nc.vector.tensor_tensor(x[:, t], x[:, t], bank_of(i, ("O", t))[:], ALU.add).then_inc(dve_read, 1)
                    dve.wait_ge(dve_read, 2 + job(i, ("O", t)))
                    nc.vector.bn_stats(stats[:, t], x[:, t]).then_inc(stats_set, 1)
                    dve.wait_ge(stats_set, 2 + TT * i + t)
                    nc.vector.tensor_copy(pause[:], half[:, 0:1])
                    nc.vector.bn_aggr(mv[:, t], stats[:, t]).then_inc(aggr_set, 1)
                    dve.wait_ge(aggr_set, 2 + TT * i + t)
                    nc.vector.tensor_scalar(mv[:, t, 1:2], mv[:, t, 1:2], EPS, None, ALU.add).then_inc(var_set, 1)

                def norm(i, t):
                    dve.wait_ge(rstd_set, 2 + TT * i + t)
                    if t >= 2:
                        dve.wait_ge(filled, 2 + job(i, ("T", t - 2)))
                    nc.vector.tensor_scalar(xn[:, t % 2], x[:, t], mv[:, t, 0:1], rstd[:, t:t + 1],
                                            ALU.subtract, ALU.mult).then_inc(xn_set, 1)

                def turned(i, t):
                    part = slice(t * P, (t + 1) * P)
                    dve.wait_ge(turn_hi, 2 + TT * i + t)
                    nc.vector.tensor_tensor(u_ln[:, LO, :, part], bank_of(i, ("T", t))[:].rearrange("p (c n) -> p c n", c=C),
                                            u_ln[:, HI, :, part].bitcast(F32), ALU.subtract).then_inc(dve_read, 1)

                def turn(i, b, more):
                    def next_heads(pair):
                        if more:
                            heads(i + 1, b, 2 * pair, 2 * pair + 2)

                    next_heads(0)
                    add_out(i, 0)
                    next_heads(1)
                    add_out(i, 1)
                    norm(i, 0)
                    next_heads(2)
                    add_out(i, 2)
                    norm(i, 1)
                    next_heads(3)
                    turned(i, 0)
                    add_out(i, 3)
                    norm(i, 2)
                    next_heads(4)
                    turned(i, 1)
                    norm(i, 3)
                    next_heads(5)
                    turned(i, 2)
                    next_heads(6)
                    turned(i, 3)
                    next_heads(7)
                    dve.wait_ge(xq_out, 1 + 16 * i)
                    for g in range(G):
                        dve.wait_ge(filled, 2 + job(i, ("XQ", g)))
                        nc.vector.tensor_scalar(xq[:, g], bank_of(i, ("XQ", g))[:], bq[:, g:g + 1], None, ALU.add)\
                            .then_inc(dve_read, 1)
                        if g == 0 and more:
                            divide(i + 1)
                        if g == 2 and more:
                            normalise(i + 1)

                dve.wait_ge(w_hi, 2)
                lo_rows = slice(2 * HD, 3 * HD)
                nc.vector.tensor_tensor(f_w[lo_rows], f_raw[lo_rows], f_w[lo_rows].bitcast(F32), ALU.subtract)\
                    .then_inc(w_lo, 1)
                def split_low(n, dst):
                    dve.wait_ge(w_hi, 2 + n)
                    nc.vector.tensor_tensor(dst[:, LO], staged(stage, n), dst[:, HI].bitcast(F32), ALU.subtract)\
                        .then_inc(w_lo, 1)

                heads(0, 0, 0, H // 2)
                split_low(1, wo)
                heads(0, 0, H // 2, H)
                dve.wait_ge(const_in, 49)
                nc.vector.tensor_copy(spread[:], spread_raw[:]).then_inc(w_lo, 1)
                divide(0)
                split_low(2, wq)
                normalise(0)
                turns(dve, turn)

            @block.tensor
            def _(pe):
                def bank_free(n):
                    if not (isinstance(n, int) and n < BANKS):
                        pe.wait_ge(dve_read, 2 + n - BANKS)

                def three(out, stationary, moving, c):
                    for n, (s, m) in enumerate(PASSES):
                        mm = nc.tensor.matmul(out, stationary(s), moving(m), start=(c == 0 and n == 0),
                                              stop=(c == C - 1 and n == 2))
                    return mm

                def heads(i, lo, hi):
                    if lo == 0 and not is_first(i):
                        pe.wait_ge(q_in, 1 + 48 * i)
                    for h in range(lo, hi):
                        if is_first(i) and h % HG == 0:
                            pe.wait_ge(q0_in[h // HG], 49)
                        bank_free(ahead(i, ("QP", h)))
                        nc.tensor.matmul(bank_ahead(i, ("QP", h))[:], f_w[:, h], q3[:, h], start=True, stop=True)\
                            .then_inc(filled, 1)

                def attend_group(i, b, g):
                    pe.wait_ge(dve_read, 2 + ahead(i, ("QP", HG * g + HG - 1)))
                    if not (is_first(i) and g < 2):
                        pe.wait_ge(num_taken, G * i + g)
                    if g == 0 and not is_first(i):
                        pe.wait_ge(den_set, 1 + i)
                    slot = lambda j: qp[:, (HG * g + j) % QSLOTS]

                    def dens():
                        for j in range(HG):
                            mm = nc.tensor.matmul(p_den[j * HD:(j + 1) * HD, :], ks_w[:, b, HG * g + j], slot(j),
                                                  start=(g == 0), stop=(g == G - 1), skip_group_check=True)
                        mm.then_inc(heads_used, 1)

                    def nums():
                        for j in range(HG):
                            mm = nc.tensor.matmul(p_num[g % 2][j * HD:(j + 1) * HD, :], kv_w[:, b, HG * g + j], slot(j),
                                                  start=True, stop=True, skip_group_check=True)
                        mm.then_inc(num_full, 1)

                    nums()
                    dens()

                def spread_out(i):
                    pe.wait_ge(rec_set, 1 + 3 * i + 3)
                    for g in range(G):
                        bank_free(ahead(i, ("R", g)))
                        for s in (HI, LO):
                            mm = nc.tensor.matmul(bank_ahead(i, ("R", g))[:], spread[:, g], rec[:, s], start=(s == HI),
                                                  stop=(s == LO))
                        mm.then_inc(filled, 1)

                def out_proj(i, t):
                    bank_free(job(i, ("O", t)))
                    for g in range(G):
                        if t == 0:
                            pe.wait_ge(norm_lo, 2 + G * i + g)
                        mm = three(bank_of(i, ("O", t))[:], lambda s: u_att[:, s, g, t * P:(t + 1) * P],
                                   lambda m: wo[:, m, g], g)
                    mm.then_inc(filled, 1)

                def transposes(i, t):
                    bank_free(job(i, ("T", t)))
                    pe.wait_ge(xn_set, 2 + TT * i + t)
                    for c in range(C):
                        mm = nc.tensor.transpose(bank_of(i, ("T", t))[:, c * P:(c + 1) * P], xn[:, t % 2, c * P:(c + 1) * P],
                                                 ident[:])
                    mm.then_inc(filled, 1)

                def turn(i, b, more):
                    def next_heads(pair):
                        if more:
                            heads(i + 1, 2 * pair, 2 * pair + 2)

                    def next_group(g):
                        if more:
                            attend_group(i + 1, b, g)

                    next_heads(0)
                    out_proj(i, 0)
                    next_heads(1)
                    out_proj(i, 1)
                    next_heads(2)
                    next_group(0)
                    out_proj(i, 2)
                    next_heads(3)
                    transposes(i, 0)
                    out_proj(i, 3)
                    next_heads(4)
                    next_group(1)
                    transposes(i, 1)
                    next_heads(5)
                    transposes(i, 2)
                    next_heads(6)
                    next_group(2)
                    transposes(i, 3)
                    next_heads(7)
                    pe.wait_ge(dve_read, 2 + job(i, ("T", TT - 1)))
                    for g in range(G):
                        bank_free(job(i, ("XQ", g)))
                        for c in range(C):
                            mm = three(bank_of(i, ("XQ", g))[:], lambda s: wq[:, s, c, g * P:(g + 1) * P],
                                       lambda m: u_ln[:, m, c], c)
                        mm.then_inc(filled, 1)
                        if g == 0:
                            next_group(3)
                        if g == 2 and more:
                            spread_out(i + 1)

                pe.wait_ge(w_lo, 2)
                heads(0, 0, H // 2)
                attend_group(0, 0, 0)
                heads(0, H // 2, H)
                for g in range(1, G):
                    attend_group(0, 0, g)
                spread_out(0)
                pe.wait_ge(w_lo, 1 + 4)
                turns(pe, turn)


def attend_cross(nc, a, NB, BLK, x1_dram, xq_dram, x2_dram, x3_dram, ident, half, stage):
    SU = HG + 1
    NS = G * SU
    SLOTS = 2 * SU
    mx_jobs = lambda k: [(k, "MX", n // SU, n % SU) for n in range(TT * SU)]
    JOBS = mx_jobs(0) + [(0, "MT")]
    for k in range(BLK):
        more = k + 1 < BLK
        JOBS += ((mx_jobs(k + 1) if more else []) + [(k, "R", g) for g in range(G)] + [(k, "O", 0)]
                 + [(k + 1, "MT")] * more + [(k, "O", 1), (k, "O", 2), (k, "T", 0), (k, "O", 3)]
                 + [(k, "T", t) for t in range(1, TT)])
    POS = {key: n for n, key in enumerate(JOBS)}
    NJ, BANKS, SBANKS = len(JOBS), 3, 2
    EARLY = 3
    assert NJ % BANKS == 0 and BLK * NS % SBANKS == 0
    with ExitStack() as ctx:
        def sb(name, shape, dt=F32):
            return ctx.enter_context(nc.sbuf_tensor("cr_" + name, shape, dt))

        def sem(name):
            return primed(ctx, nc, sems, "cr_" + name)

        sems = []
        wo = sb("wo", [P, 2, C, D], F32R)
        k_w = sb("k_w", [P, 2, G, HG * P + P], F32R)
        v_w = sb("v_w", [P, D])
        v_rem = sb("v_rem", [P, G, HG, HD])
        one_col = sb("one_col", [P, G, HD])
        rem_ones = sb("rem_ones", [P, G, P])
        spread = sb("spread", [P, G, P])
        minus = sb("minus", [P, G, SU, P], BF16)
        bias = sb("bias", [P, D])
        bk = sb("bk", [P, C])
        small = sb("small", [P, 2 * HG])
        x = sb("x", [P, TT, D])
        xq_raw = sb("xq_raw", [P, C * TB])
        xq = [sb(f"xq{n}", [P, 2, C * TB], F32R) for n in range(2)]
        u = sb("u", [P, 2, C, TB], F32R)
        xn = sb("xn", [P, 2, D])
        ring = sb("ring", [P, SLOTS, TB])
        num = sb("num", [P, G, TB])
        x3 = sb("x3", [P, C, TB])
        den = sb("den", [P, 2, TB])
        kt = sb("kt", [P, 2, P + KPAD])
        stats = sb("stats", [P, TT, 6])
        mv = sb("mv", [P, TT, 2])
        rstd = sb("rstd", [P, TT])
        pause = sb("pause", [P, 1])
        mx = sb("mx", [P, 2, TT, H])
        mxb = sb("mxb", [P, TT, P], BF16)
        mxt = sb("mxt", [P, TB], BF16)
        ident_b = sb("ident_b", [P, P], BF16)
        bank = [ctx.enter_context(nc.psum_tensor(f"cr_bank{n}", [P, 512], F32)) for n in range(BANKS)]
        s_bank = [ctx.enter_context(nc.psum_tensor(f"cr_s_bank{n}", [P, 512], F32)) for n in range(SBANKS)]
        p_num = [ctx.enter_context(nc.psum_tensor(f"cr_p_num{n}", [P, 512], F32)) for n in range(2)]
        p_den = ctx.enter_context(nc.psum_tensor("cr_p_den", [P, 512], F32))

        w_hi, w_lo, const_in, late_in, zero_set = sem("w_hi"), sem("w_lo"), sem("const_in"), sem("late_in"), sem("zero_set")
        next_in = sem("next_in")
        cast_in = ctx.enter_context(nc.semaphore("cr_cast_in"))
        ctx_in, ctx_mm, ctx_act, ctx_step = sem("ctx_in"), sem("ctx_mm"), sem("ctx_act"), sem("ctx_step")
        ctx_masked, ctx_hi = sem("ctx_masked"), sem("ctx_hi")
        x_in, xq_in, xq_hi, xq_lo, x2_out, x3_out = (sem("x_in"), sem("xq_in"), sem("xq_hi"), sem("xq_lo"),
                                                     sem("x2_out"), sem("x3_out"))
        filled, dve_read, s_full, s_read = sem("filled"), sem("dve_read"), sem("s_full"), sem("s_read")
        heads_used, num_full, num_taken = sem("heads_used"), sem("num_full"), sem("num_taken")
        den_full, den_set, rec_set = sem("den_full"), sem("den_set"), sem("rec_set")
        norm_hi, norm_lo, mx_set = sem("norm_hi"), sem("norm_lo"), sem("mx_set")
        xb_set, stats_set, aggr_set, var_set = sem("xb_set"), sem("stats_set"), sem("aggr_set"), sem("var_set")
        rstd_set, xn_set = sem("rstd_set"), sem("xn_set")
        prime(nc, pause, sems)

        CTXW = P + KPAD + P
        ctx_t = sb("ctx_t", [P, C, CTXW])
        bv = sb("bv", [P, D])
        tmp = sb("tmp", [P, 2, HG * P + P])
        wk, wv, wo_raw = [staged(stage, n) for n in range(3)]
        CTX_STEPS = G + 2 + G

        def job(b, k, *what):
            return NJ * b + POS[(k, *what)]

        def bank_of(k, *what):
            return bank[POS[(k, *what)] % BANKS]

        with nc.Block() as block:
            @block.sync
            def _(sp):
                def load_context(b):
                    sp.dma_start(ctx_t[:], a["ctxT"][b].rearrange("(c p) n -> p c n", p=P)).then_inc(ctx_in, 16)

                def batch(b, more):
                    def load_xq(k):
                        sp.wait_ge(xq_lo, 1 + (b * BLK + k))
                        sp.dma_start(xq_raw[:], xq_dram[b * BLK + k]).then_inc(xq_in, 16)

                    load_xq(0)
                    load_xq(1)
                    for k in range(BLK):
                        i = b * BLK + k
                        sp.wait_ge(x2_out, 1 + 16 * i)
                        sp.dma_start(x[:].rearrange("p t d -> p (t d)"), x1_dram[i]).then_inc(x_in, 16)
                        if k + 2 < BLK:
                            load_xq(k + 2)
                        if k == 2 and more:
                            sp.wait_ge(ctx_mm, 1 + (G + 2) * (b + 1))
                            load_context(b + 1)
                        if k == 2 and not more:
                            sp.wait_ge(ctx_mm, 1 + (G + 2) * NB)
                            sp.dma_start(stage[:, 0:UNIT], a["units"][0]).then_inc(next_in, 16)
                            sp.wait_ge(x3_out, 1 + 16 * i)
                            for n in range(X3_SLOTS):
                                sp.dma_start(x3_slot(stage, n), x3_part(x3_dram, n)).then_inc(next_in, 16)
                        sp.wait_ge(dve_read, 2 + job(b, k, "O", TT - 1))
                        sp.dma_start(x2_dram[i], x[:].rearrange("p t d -> p (t d)")).then_inc(x2_out, 16)
                        sp.wait_ge(dve_read, 2 + job(b, k, "T", TT - 1))
                        sp.dma_start(x3_dram[i], x3[:].rearrange("p g t -> p (g t)")).then_inc(x3_out, 16)

                sp.dma_start(bk[:], a["bkT"]).then_inc(const_in, 16)
                sp.dma_start(small[:], a["small"]).then_inc(const_in, 16)
                load_context(0)
                sp.dma_start(bv[:], a["bv"].broadcast_to([P, D])).then_inc(const_in, 16)
                for dst, src in ((one_col, "one_col"), (rem_ones, "rem_ones"), (spread, "spread")):
                    sp.dma_start(dst[:].rearrange("p g n -> p (g n)"), a[src]).then_inc(late_in, 16)
                sp.dma_start(bias[:], a["bo"].broadcast_to([P, D])).then_inc(late_in, 16)
                with sp.Fori(0, NB - 1) as b:
                    batch(b, True)
                batch(NB - 1, False)
                sp.wait_ge(next_in, 1 + 16 * (1 + X3_SLOTS))
                sp.wait_ge(x2_out, 1 + 16 * NB * BLK)
                sp.wait_ge(x3_out, 1 + 16 * NB * BLK)

            @block.gpsimd
            def _(pool):
                nc.gpsimd.memset(mxb[:], 0.0).then_inc(zero_set, 1)
                pool.dma_start(minus[:].rearrange("p g s n -> p (g s n)"), a["minus"]).then_inc(cast_in, 16)
                pool.dma_start(ident_b[:], a["ident"]).then_inc(cast_in, 16)
                pool.wait_ge(late_in, 1 + 64)
                rows = bias[:].rearrange("p (o d) -> p o d", o=1).broadcast_to([P, TT, D])
                with pool.Fori(0, NB * BLK) as i:
                    pool.wait_ge(x_in, 17 + 16 * i)
                    nc.gpsimd.tensor_tensor(x[:], x[:], rows, ALU.add).then_inc(xb_set, 1)
                    for t in range(TT):
                        pool.wait_ge(var_set, 2 + TT * i + t)
                        nc.gpsimd.tensor_tensor(rstd[:, t:t + 1], mv[:, t, 1:2], half[:, 0:1], ALU.pow)\
                            .then_inc(rstd_set, 1)

            @block.scalar
            def _(act):
                nc.scalar.copy(wo[:, HI], wo_raw).then_inc(w_hi, 1)
                act.wait_ge(const_in, 1 + 48)
                with act.Fori(0, NB) as b:
                    for g in range(G + 1):
                        if g < G:
                            act.wait_ge(ctx_mm, 2 + ((G + 2) * b + g))
                            if g >= 2:
                                act.wait_ge(ctx_masked, 1 + 2 * (G * b + g - 1))
                            nc.scalar.activation(kt[:, g % 2], bank[g % 2][:, 0:P + KPAD], ACT.Identity,
                                                 bias=bk[:, g:g + 1]).then_inc(ctx_act, 1)
                        if g:
                            act.wait_ge(ctx_masked, 1 + 2 * (G * b + g))
                            nc.scalar.copy(k_w[:, HI, g - 1], tmp[:, (g - 1) % 2]).then_inc(ctx_hi, 1)

                    def split_xq(k):
                        act.wait_ge(xq_in, 17 + 16 * (b * BLK + k))
                        nc.scalar.copy(xq[k % 2][:, HI], xq_raw[:]).then_inc(xq_hi, 1)

                    def take_num(k, g):
                        act.wait_ge(num_full, 2 + (G * BLK * b + G * k + g))
                        nc.scalar.copy(num[:, g], p_num[g % 2][:]).then_inc(num_taken, 1)

                    split_xq(0)
                    split_xq(1)
                    for k in range(BLK):
                        for n in range(NS):
                            act.wait_ge(s_full, 2 + (NS * BLK * b + NS * k + n))
                            if n >= SLOTS:
                                act.wait_ge(heads_used, 2 + ((G - 1) * (BLK * b + k) + (n - SLOTS) // SU))
                            nc.scalar.activation(ring[:, n % SLOTS], s_bank[n % SBANKS][:], ACT.Exp,
                                                 scale=float(HD) ** -0.5).then_inc(s_read, 1)
                            if n % SU == SU - 1 and n > SU:
                                take_num(k, n // SU - 1)
                        take_num(k, G - 1)
                        for g in range(G):
                            act.wait_ge(dve_read, 2 + job(b, k, "R", g))
                            nc.scalar.copy(u[:, HI, g], num[:, g]).then_inc(norm_hi, 1)
                        if k + 2 < BLK:
                            split_xq(k + 2)

            @block.vector
            def _(dve):
                dve.wait_ge(w_hi, 2)
                nc.vector.tensor_tensor(wo[:, LO], wo_raw, wo[:, HI].bitcast(F32), ALU.subtract).then_inc(w_lo, 1)
                nc.vector.memset(mx[:], 0.0).then_inc(zero_set, 1)
                dve.wait_ge(const_in, 1 + 48)
                dve.wait_ge(zero_set, 3)
                with dve.Fori(0, NB) as b:
                    step = [0]

                    def chain(ins):
                        step[0] += 1
                        ins.then_inc(ctx_step, 1)
                        dve.wait_ge(ctx_step, 1 + step[0] + CTX_STEPS * b)

                    for g in range(G + 1):
                        if g < G:
                            dve.wait_ge(ctx_act, 2 + (G * b + g))
                            if g >= 2:
                                dve.wait_ge(ctx_step, 1 + (CTX_STEPS * b + g - 1))
                            for lo, cols in ((0, slice(0, P)), (HG * P, slice(P, P + KPAD))):
                                n = cols.stop - cols.start
                                k_all = kt[:, g % 2:g % 2 + 1, cols].broadcast_to([P, HG, n])
                                rows = small[:, 0:HG].rearrange("p (j o) -> p j o", o=1).broadcast_to([P, HG, n])
                                nc.vector.tensor_tensor(tmp[:, g % 2, lo:lo + HG * n].rearrange("p (j k) -> p j k", j=HG),
                                                        k_all, rows, ALU.mult).then_inc(ctx_masked, 1)
                        if g:
                            dve.wait_ge(ctx_hi, 1 + (G * b + g))
                            step[0] += 1
                            nc.vector.tensor_tensor(k_w[:, LO, g - 1], tmp[:, (g - 1) % 2], k_w[:, HI, g - 1].bitcast(F32),
                                                    ALU.subtract).then_inc(ctx_step, 1)
                    dve.wait_ge(ctx_step, 1 + step[0] + CTX_STEPS * b)
                    dve.wait_ge(ctx_mm, 2 + ((G + 2) * b + G))
                    chain(nc.vector.tensor_tensor(v_w[:], bank[2][:], bv[:], ALU.add))
                    dve.wait_ge(ctx_mm, 2 + ((G + 2) * b + G + 1))
                    chain(nc.vector.tensor_tensor(tmp[:, 0, 0:D], s_bank[0][:], bv[:], ALU.add))
                    rows = small[:, HG:2 * HG].rearrange("p (j o) -> p j o", o=1).broadcast_to([P, HG, HD])
                    for g in range(G):
                        chain(nc.vector.tensor_tensor(v_rem[:, g], tmp[:, 0, g * P:(g + 1) * P].rearrange(
                            "p (j d) -> p j d", j=HG), rows, ALU.mult))

                    def split_xq(k):
                        dve.wait_ge(xq_hi, 2 + (b * BLK + k))
                        nc.vector.tensor_tensor(xq[k % 2][:, LO], xq_raw[:], xq[k % 2][:, HI].bitcast(F32),
                                                ALU.subtract).then_inc(xq_lo, 1)

                    def maxima(k, t):
                        if t == 0:
                            dve.wait_ge(mx_set, 1 + 3 * (BLK * b + k))
                        for g in range(G + 1):
                            dve.wait_ge(filled, 2 + job(b, k, "MX", t, g))
                            src = bank_of(k, "MX", t, g)[:].rearrange("p (h n) -> p h n", h=HG if g < G else H)
                            dst = mx[:, 0, t, g * HG:(g + 1) * HG] if g < G else mx[:, 1, t]
                            nc.vector.tensor_reduce(dst, src, AX.X, ALU.max).then_inc(dve_read, 1)
                        if t < TT - 1:
                            return
                        dve.wait_ge(dve_read, 2 + job(b, k, "MX", t, G))
                        nc.vector.tensor_tensor(mx[:, 0], mx[:, 0], mx[:, 1], ALU.max).then_inc(mx_set, 1)
                        dve.wait_ge(mx_set, 2 + (3 * BLK * b + 3 * k))
                        nc.vector.tensor_copy(mxb[:, :, 0:H], mx[:, 0]).then_inc(mx_set, 1)
                        dve.wait_ge(mx_set, 3 + (3 * BLK * b + 3 * k))
                        nc.vector.tensor_tensor(mxb[:, :, H:2 * H], mx[:, 0], mxb[:, :, 0:H], ALU.subtract)\
                            .then_inc(mx_set, 1)

                    def add_out(k, t):
                        n = TT * BLK * b + TT * k + t
                        if t == 0:
                            dve.wait_ge(xb_set, 2 + (BLK * b + k))
                        dve.wait_ge(filled, 2 + job(b, k, "O", t))
                        nc.vector.tensor_tensor(x[:, t], x[:, t], bank_of(k, "O", t)[:], ALU.add).then_inc(dve_read, 1)
                        dve.wait_ge(dve_read, 2 + job(b, k, "O", t))
                        nc.vector.bn_stats(stats[:, t], x[:, t]).then_inc(stats_set, 1)
                        dve.wait_ge(stats_set, 2 + n)
                        nc.vector.tensor_copy(pause[:], half[:, 0:1])
                        nc.vector.bn_aggr(mv[:, t], stats[:, t]).then_inc(aggr_set, 1)
                        dve.wait_ge(aggr_set, 2 + n)
                        nc.vector.tensor_scalar(mv[:, t, 1:2], mv[:, t, 1:2], EPS, None, ALU.add).then_inc(var_set, 1)

                    def norm(k, t):
                        dve.wait_ge(rstd_set, 2 + (TT * BLK * b + TT * k + t))
                        if t >= 2:
                            dve.wait_ge(filled, 2 + job(b, k, "T", t - 2))
                        nc.vector.tensor_scalar(xn[:, t % 2], x[:, t], mv[:, t, 0:1], rstd[:, t:t + 1],
                                                ALU.subtract, ALU.mult).then_inc(xn_set, 1)

                    def turned(k, t):
                        if t == 0:
                            dve.wait_ge(x3_out, 1 + 16 * (b * BLK + k))
                        dve.wait_ge(filled, 2 + job(b, k, "T", t))
                        nc.vector.tensor_copy(x3[:, :, t * P:(t + 1) * P],
                                              bank_of(k, "T", t)[:].rearrange("p (c n) -> p c n", c=C))\
                            .then_inc(dve_read, 1)

                    def turned_maxima(k):
                        dve.wait_ge(filled, 2 + job(b, k, "MT"))
                        nc.vector.tensor_copy(mxt[:], bank_of(k, "MT")[:].bitcast(BF16)[:, 0:TB]).then_inc(dve_read, 1)

                    split_xq(0)
                    for t in range(TT):
                        maxima(0, t)
                    turned_maxima(0)
                    split_xq(1)
                    for k in range(BLK):
                        i = b * BLK + k
                        if k + 1 < BLK:
                            for t in range(TT):
                                maxima(k + 1, t)
                        dve.wait_ge(den_full, 2 + i)
                        nc.vector.tensor_scalar(den[:, 0], p_den[:], 1e-30, None, ALU.max).then_inc(den_set, 1)
                        dve.wait_ge(den_set, 2 + i)
                        for cols in (slice(0, TB // 2), slice(TB // 2, TB)):
                            nc.vector.reciprocal(den[:, 1, cols], den[:, 0, cols]).then_inc(rec_set, 1)
                        for g in range(G + 1):
                            if g < G:
                                dve.wait_ge(num_taken, 2 + (G * i + g))
                                dve.wait_ge(filled, 2 + job(b, k, "R", g))
                                nc.vector.tensor_tensor(num[:, g], num[:, g], bank_of(k, "R", g)[:], ALU.mult)\
                                    .then_inc(dve_read, 1)
                            if g:
                                dve.wait_ge(norm_hi, 1 + (G * i + g))
                                nc.vector.tensor_tensor(u[:, LO, g - 1], num[:, g - 1], u[:, HI, g - 1].bitcast(F32),
                                                        ALU.subtract).then_inc(norm_lo, 1)
                        add_out(k, 0)
                        if k + 1 < BLK:
                            turned_maxima(k + 1)
                        add_out(k, 1)
                        norm(k, 0)
                        add_out(k, 2)
                        norm(k, 1)
                        turned(k, 0)
                        add_out(k, 3)
                        norm(k, 2)
                        turned(k, 1)
                        norm(k, 3)
                        turned(k, 2)
                        turned(k, 3)
                        if k + 2 < BLK:
                            split_xq(k + 2)

            @block.tensor
            def _(pe):
                with pe.Fori(0, NB) as b:
                    pe.wait_ge(ctx_in, 17 + 16 * b)
                    pe.wait_ge(dve_read, 1 + NJ * b)
                    pe.wait_ge(s_read, 1 + NS * BLK * b)
                    for g in range(G):
                        if g >= 2:
                            pe.wait_ge(ctx_act, 1 + (G * b + g - 1))
                        for c in range(C):
                            mm = nc.tensor.matmul(bank[g % 2][:, 0:P + KPAD], wk[:, c, g * P:(g + 1) * P],
                                                  ctx_t[:, c, 0:P + KPAD], start=(c == 0), stop=(c == C - 1))
                        mm.then_inc(ctx_mm, 1)
                    for out, lo in ((bank[2], 0), (s_bank[0], P + KPAD)):
                        for c in range(C):
                            mm = nc.tensor.matmul(out[:], ctx_t[:, c, lo:lo + P], wv[:, c], start=(c == 0),
                                                  stop=(c == C - 1))
                        mm.then_inc(ctx_mm, 1)
                    pe.wait_ge(ctx_step, 1 + CTX_STEPS * (b + 1))
                    pe.wait_ge(late_in, 1 + 64)
                    pe.wait_ge(cast_in, 32)
                    pe.wait_ge(zero_set, 3)

                    def bank_free(k, *what):
                        n = POS[(k, *what)]
                        if n >= BANKS:
                            pe.wait_ge(dve_read, 2 + (NJ * b + n - BANKS))

                    def maxima(k, n):
                        q = xq[k % 2][:].rearrange("p s (g n) -> p s g n", g=G)
                        t, unit = n // SU, n % SU
                        part = slice(t * P, (t + 1) * P)
                        bank_free(k, "MX", t, unit)
                        if n == 0:
                            pe.wait_ge(xq_hi, 2 + (b * BLK + k))
                        if unit < G:
                            mm = nc.tensor.matmul(bank_of(k, "MX", t, unit)[:], q[:, HI, unit, part],
                                                  k_w[:, HI, unit, 0:HG * P], start=True, stop=True)
                        else:
                            for g in range(G):
                                mm = nc.tensor.matmul(bank_of(k, "MX", t, G)[:, g * P:(g + 1) * P], q[:, HI, g, part],
                                                      k_w[:, HI, g, HG * P:HG * P + P], start=(g == 0),
                                                      stop=(g == G - 1), skip_group_check=True)
                        mm.then_inc(filled, 1)

                    def turn_maxima(k):
                        bank_free(k, "MT")
                        pe.wait_ge(mx_set, 4 + 3 * (b * BLK + k))
                        for t in range(TT):
                            mm = nc.tensor.transpose(bank_of(k, "MT")[:].bitcast(BF16)[:, t * P:(t + 1) * P], mxb[:, t],
                                                     ident_b[:])
                        mm.then_inc(filled, 1)

                    def scores(k, n):
                        g, j = n // SU, n % SU
                        q = xq[k % 2][:].rearrange("p s (g n) -> p s g n", g=G)
                        if n == 0:
                            pe.wait_ge(xq_lo, 2 + (b * BLK + k))
                        if NS * k + n >= SBANKS:
                            pe.wait_ge(s_read, 2 + (NS * BLK * b + NS * k + n - SBANKS))
                        for c, (s, m) in enumerate(PASSES):
                            nc.tensor.matmul(s_bank[n % SBANKS][:], k_w[:, s, g, j * P:(j + 1) * P], q[:, m, g],
                                             start=(c == 0), stop=False)

                    def shift(k, n):
                        nc.tensor.matmul(s_bank[n % SBANKS][:], minus[:, n // SU, n % SU], mxt[:], start=False,
                                         stop=True).then_inc(s_full, 1)

                    def unit(k, n):
                        scores(k, n)
                        if n == 0:
                            pe.wait_ge(dve_read, 2 + job(b, k, "MT"))
                        shift(k, n)

                    def attend_group(k, g):
                        n = G * BLK * b + G * k + g
                        pe.wait_ge(s_read, 2 + (NS * BLK * b + NS * k + SU * g + SU - 1))
                        slot = [ring[:, (SU * g + j) % SLOTS] for j in range(SU)]

                        def dens():
                            if g == 0:
                                pe.wait_ge(den_set, 1 + (b * BLK + k))
                            for j in range(HG):
                                nc.tensor.matmul(p_den[j * HD:(j + 1) * HD, :], one_col[:, g], slot[j], start=(g == 0),
                                                 stop=False, skip_group_check=True)
                            return nc.tensor.matmul(p_den[:], rem_ones[:, g], slot[HG], start=False, stop=(g == G - 1),
                                                    skip_group_check=True)

                        def nums():
                            pe.wait_ge(num_taken, n if k or g >= 2 else 1 + G * BLK * b)
                            for j in range(HG):
                                h = HG * g + j
                                nc.tensor.matmul(p_num[g % 2][j * HD:(j + 1) * HD, :], v_w[:, h * HD:(h + 1) * HD],
                                                 slot[j], start=True, stop=False, skip_group_check=True)
                            return nc.tensor.matmul(p_num[g % 2][:], v_rem[:, g].rearrange("p j d -> p (j d)"), slot[HG],
                                                    start=False, stop=True, skip_group_check=True)

                        if g < G - 1:
                            nums().then_inc(num_full, 1)
                            dens().then_inc(heads_used, 1)
                        else:
                            dens().then_inc(den_full, 1)
                            nums().then_inc(num_full, 1)

                    def out_proj(k, t):
                        bank_free(k, "O", t)
                        n = 0
                        for g in range(G):
                            if t == 0:
                                pe.wait_ge(norm_lo, 2 + (G * (BLK * b + k) + g))
                            for s, m in PASSES:
                                mm = nc.tensor.matmul(bank_of(k, "O", t)[:], u[:, s, g, t * P:(t + 1) * P], wo[:, m, g],
                                                      start=(n == 0), stop=(n == 3 * G - 1))
                                n += 1
                        mm.then_inc(filled, 1)

                    def transposes(k, t):
                        bank_free(k, "T", t)
                        pe.wait_ge(xn_set, 2 + (TT * BLK * b + TT * k + t))
                        for c in range(C):
                            mm = nc.tensor.transpose(bank_of(k, "T", t)[:, c * P:(c + 1) * P],
                                                     xn[:, t % 2, c * P:(c + 1) * P], ident[:])
                        mm.then_inc(filled, 1)

                    for n in range(NS):
                        maxima(0, n)
                    turn_maxima(0)
                    for k in range(BLK):
                        i = b * BLK + k
                        more = k + 1 < BLK
                        first = EARLY if k else 0
                        for n in range(NS):
                            if n >= first:
                                unit(k, n)
                                if more:
                                    share = lambda m: NS * (m - first) // (NS - first)
                                    for m in range(share(n), share(n + 1)):
                                        maxima(k + 1, m)
                            if n % SU == SU - 1 and n > SU:
                                attend_group(k, n // SU - 1)
                        attend_group(k, G - 1)

                        def spread_out(g, half, last):
                            cols = slice(half * TB // 2, (half + 1) * TB // 2)
                            mm = nc.tensor.matmul(bank_of(k, "R", g)[:, cols], spread[:, g], den[:, 1, cols],
                                                  start=True, stop=True, skip_group_check=True)
                            if last:
                                mm.then_inc(filled, 1)

                        pe.wait_ge(rec_set, 2 + 2 * i)
                        for g in range(BANKS):
                            bank_free(k, "R", g)
                            spread_out(g, 0, False)
                        pe.wait_ge(rec_set, 3 + 2 * i)
                        for g in range(BANKS):
                            spread_out(g, 1, True)
                        for g in range(BANKS, G):
                            bank_free(k, "R", g)
                            spread_out(g, 0, False)
                            spread_out(g, 1, True)
                        out_proj(k, 0)
                        if more:
                            turn_maxima(k + 1)
                        out_proj(k, 1)
                        out_proj(k, 2)
                        transposes(k, 0)
                        out_proj(k, 3)
                        transposes(k, 1)
                        if more:
                            unit(k + 1, 0)
                            unit(k + 1, 1)
                        transposes(k, 2)
                        if more:
                            unit(k + 1, 2)
                        transposes(k, 3)


def experts(nc, a, NB, BLK, x2_dram, x3_dram, out_bat, ident, stage):
    NT = BLK * TT
    WG, WU, WD = 0, C * FE, 2 * C * FE
    with ExitStack() as ctx:
        def sb(name, shape, dt=F32):
            return ctx.enter_context(nc.sbuf_tensor("ex_" + name, shape, dt))

        def sem(name):
            return primed(ctx, nc, sems, "ex_" + name)

        sems = []

        x3 = sb("x3", [P, 2, BLK, C * TB], F32R)
        acc = sb("acc", [P, NT, D])
        w_raw = stage[:, 0:UNIT]
        w = sb("w", [P, 2, 2, UNIT], F32R)
        s_g = sb("s_g", [P, FT, TB])
        h = sb("h", [P, FT, TB])
        ht = sb("ht", [P, 2, 2, FT, TB], F32R)
        r_raw = sb("r_raw", [P, C, P])
        r_w = sb("r_w", [P, 2, C, P], F32R)
        lt = sb("lt", [P, NT, E])
        total = sb("total", [P, NT])
        top = sb("top", [P, NT])
        ex = sb("ex", [P, NT, E])
        gt = sb("gt", [P, NT, E, E])
        lower = sb("lower", [P, E * E])
        rank = sb("rank", [P, NT, E])
        rank2 = sb("rank2", [P, NT, E])
        share = sb("share", [P, NT, UNITS])
        pg = [ctx.enter_context(nc.psum_tensor(f"ex_pg{n}", [P, 512], F32)) for n in range(2 * FT)]
        pd = [ctx.enter_context(nc.psum_tensor(f"ex_pd{n}", [P, 512], F32)) for n in range(4)]

        x3_in, x3_hi, x3_lo = [sem(f"x3_in{n}") for n in range(X3_SLOTS)], sem("x3_hi"), sem("x3_lo")
        acc_in, out_done = [sem(f"acc_in{k}") for k in range(BLK)], [sem(f"out_done{k}") for k in range(BLK)]
        const_in = sem("const_in")
        w_in, w_hi, w_lo = sem("w_in"), sem("w_hi"), sem("w_lo")
        r_hi, r_lo = sem("r_hi"), sem("r_lo")
        lg_full, lg_taken, lt_full, lt_taken = sem("lg_full"), sem("lg_taken"), sem("lt_full"), sem("lt_taken")
        own, exp_set, share_set = sem("own"), sem("exp_set"), sem("share_set")
        OWN = 13
        gu_full, silu_set, h_set, ht_hi, ht_lo = (sem("gu_full"), sem("silu_set"), sem("h_set"), sem("ht_hi"),
                                                  sem("ht_lo"))
        d_full, d_taken = sem("d_full"), sem("d_taken")
        prime(nc, total, sems)

        PAIRS = UNITS // 2
        STEPS = 2 * BLK
        HALF = X3_PART
        NX = BLK * C * TB // HALF
        lg = [(s_g, h)[k // FT][0:E, k % FT] for k in range(BLK)]

        with nc.Block() as block:
            @block.sync
            def _(sp):
                sp.dma_start(r_raw[:], a["router"].rearrange("(c p) n -> p c n", p=P)).then_inc(const_in, 16)
                sp.dma_start(lower[:], a["lower"]).then_inc(const_in, 16)
                def load_x3(m):
                    if m >= X3_SLOTS:
                        sp.wait_ge(x3_lo, 1 + m - X3_SLOTS + 1)
                        sp.dma_start(x3_slot(stage, m), x3_part(x3_dram, m)).then_inc(x3_in[m % X3_SLOTS], 16)

                def load_acc(b, k):
                    if b:
                        sp.wait_ge(out_done[k], 1 + 16 * b)
                    sp.dma_start(acc[:, k * TT:(k + 1) * TT].rearrange("p t d -> p (t d)"), x2_dram[b * BLK + k])\
                        .then_inc(acc_in[k], 16)

                for n in range(NX):
                    load_x3(n)
                for k in range(BLK):
                    load_acc(0, k)
                for b in range(NB):
                    with sp.Fori(0, UNITS) as e:
                        sp.wait_ge(w_lo, 1 + e + (b * UNITS + 1))
                        sp.dma_start(w_raw, a["units"][e + 1]).then_inc(w_in, 16)
                    more = b + 1 < NB
                    if more:
                        for n in range(X3_SLOTS):
                            load_x3(NX * (b + 1) + n)
                    for k in range(BLK):
                        sp.wait_ge(d_taken, 1 + TT * (PAIRS * STEPS * (b + 1) - BLK + k + 1))
                        sp.dma_start(out_bat[b][:, k * TT:(k + 1) * TT], acc[:, k * TT:(k + 1) * TT])\
                            .then_inc(out_done[k], 16)
                        if more and 0 < k < BLK - 1:
                            load_acc(b + 1, k - 1)
                    if more:
                        for n in range(X3_SLOTS, NX):
                            load_x3(NX * (b + 1) + n)
                        load_acc(b + 1, BLK - 2)
                        load_acc(b + 1, BLK - 1)
                for k in range(BLK):
                    sp.wait_ge(out_done[k], 1 + 16 * NB)

            @block.gpsimd
            def _(pool):
                nc.gpsimd.memset(share[:], 1.0).then_inc(share_set, 1)

            @block.scalar
            def _(act):
                for b in range(NB):
                    if b:
                        act.wait_ge(gu_full, 1 + 2 * FT * STEPS * PAIRS * b)
                    for n in range(NX):
                        k, part = n // 2, n % 2
                        m = NX * b + n
                        if m >= X3_SLOTS:
                            act.wait_ge(x3_in[m % X3_SLOTS], 1 + 16 * (m // X3_SLOTS))
                        nc.scalar.copy(x3[:, HI, k, part * HALF:(part + 1) * HALF], x3_slot(stage, m)).then_inc(x3_hi, 1)
                        if m == 1:
                            act.wait_ge(const_in, 1 + 32)
                            nc.scalar.copy(r_w[:, HI], r_raw[:]).then_inc(r_hi, 1)
                    if b == 0:
                        nc.scalar.copy(w[:, 0, HI], w_raw).then_inc(w_hi, 1)
                    act.wait_ge(own, 1 + OWN * b + 2)
                    nc.scalar.activation(ex[:], ex[:], ACT.Exp).then_inc(exp_set, 1)
                    with act.Fori(0, PAIRS) as p:
                        q = p + b * PAIRS
                        for s in range(STEPS):
                            step = q * STEPS + s
                            for f in range(FT):
                                act.wait_ge(gu_full, 1 + step * (2 * FT) + 2 * f + 1)
                                act.wait_ge(h_set, 1 + step * FT + (f + 1 - FT if s else 0))
                                nc.scalar.activation(s_g[:, f], pg[2 * f][:], ACT.Silu).then_inc(silu_set, 1)
                            for f in range(FT):
                                act.wait_ge(h_set, 1 + step * FT + f + 1)
                                nc.scalar.copy(ht[:, s % 2, HI, f], h[:, f]).then_inc(ht_hi, 1)
                            if s == 1:
                                act.wait_ge(w_in, 1 + q * 32 + 16)
                                nc.scalar.copy(w[:, 1, HI], w_raw).then_inc(w_hi, 1)
                            if s == BLK + 1:
                                act.wait_ge(w_in, 1 + q * 32 + 32)
                                nc.scalar.copy(w[:, 0, HI], w_raw).then_inc(w_hi, 1)

            @block.vector
            def _(dve):
                def split_w(slot, n):
                    dve.wait_ge(w_hi, 1 + n)
                    nc.vector.tensor_tensor(w[:, slot, LO], w_raw, w[:, slot, HI].bitcast(F32),
                                            ALU.subtract).then_inc(w_lo, 1)

                def take_logits(b, k):
                    if b:
                        dve.wait_ge(ht_lo, 1 + FT * STEPS * PAIRS * b)
                    dve.wait_ge(lg_full, 1 + BLK * b + k + 1)
                    nc.vector.tensor_copy(lg[k], pg[k][0:E, :]).then_inc(lg_taken, 1)

                def router(b):
                    dve.wait_ge(lt_full, 1 + b + 1)
                    nc.vector.tensor_copy(lt[:].rearrange("p n e -> p (n e)"), pd[0][:, 0:NT * E]).then_inc(lt_taken, 1)
                    dve.wait_ge(lt_taken, 1 + b + 1)
                    count = [OWN * b]

                    def chain(ins):
                        count[0] += 1
                        ins.then_inc(own, 1)
                        dve.wait_ge(own, 1 + count[0])

                    per_e = lt[:].rearrange("p n (e o) -> p n e o", o=1).broadcast_to([P, NT, E, E])
                    per_f = lt[:].rearrange("p n (o e) -> p n o e", o=1).broadcast_to([P, NT, E, E])
                    low = lower[:].rearrange("p (o n) -> p o n", o=1).broadcast_to([P, NT, E * E])
                    gt_flat = gt[:].rearrange("p n e f -> p n (e f)")
                    per_n = lambda t: t[:].rearrange("p (n o) -> p n o", o=1).broadcast_to([P, NT, E])
                    chain(nc.vector.tensor_reduce(top[:], lt[:], AX.X, ALU.max))
                    chain(nc.vector.tensor_tensor(ex[:], lt[:], per_n(top), ALU.subtract))
                    chain(nc.vector.tensor_tensor(gt[:], per_f, per_e, ALU.is_gt))
                    chain(nc.vector.tensor_reduce(rank[:], gt[:], AX.X, ALU.add))
                    chain(nc.vector.tensor_tensor(gt[:], per_f, per_e, ALU.is_equal))
                    chain(nc.vector.tensor_tensor(gt_flat, gt_flat, low, ALU.mult))
                    chain(nc.vector.tensor_reduce(rank2[:], gt[:], AX.X, ALU.add))
                    chain(nc.vector.tensor_tensor(rank[:], rank[:], rank2[:], ALU.add))
                    chain(nc.vector.tensor_scalar(rank[:], rank[:], TOP - 0.5, None, ALU.is_lt))
                    dve.wait_ge(exp_set, 1 + b + 1)
                    chain(nc.vector.tensor_reduce(top[:], ex[:], AX.X, ALU.add))
                    chain(nc.vector.reciprocal(total[:], top[:]))
                    chain(nc.vector.tensor_tensor(ex[:], ex[:], per_n(total), ALU.mult))
                    chain(nc.vector.tensor_tensor(share[:, :, 0:E], ex[:], rank[:], ALU.mult))
                    assert count[0] == OWN * (b + 1)

                def add_down(b, e, step, s):
                    k = s % BLK
                    dve.wait_ge(acc_in[k], 1 + 16 * (b + 1))
                    for t in range(TT):
                        n = k * TT + t
                        dve.wait_ge(d_full, 1 + step * TT + t + 1)
                        nc.vector.scalar_tensor_tensor(acc[:, n], pd[t][:], share[:, n, bass.ds(e + s // BLK, 1)],
                                                       acc[:, n], ALU.mult, ALU.add).then_inc(d_taken, 1)

                for b in range(NB):
                    for n in range(NX):
                        k, part = n // 2, slice((n % 2) * HALF, (n % 2 + 1) * HALF)
                        dve.wait_ge(x3_hi, 1 + NX * b + n + 1)
                        nc.vector.tensor_tensor(x3[:, LO, k, part], x3_slot(stage, NX * b + n),
                                                x3[:, HI, k, part].bitcast(F32), ALU.subtract).then_inc(x3_lo, 1)
                        if b == 0 and n == 1:
                            dve.wait_ge(r_hi, 2)
                            nc.vector.tensor_tensor(r_w[:, LO], r_raw[:], r_w[:, HI].bitcast(F32), ALU.subtract)\
                                .then_inc(r_lo, 1)
                        if n % 2 and k:
                            take_logits(b, k - 1)
                    take_logits(b, BLK - 1)
                    if b == 0:
                        split_w(0, 1)
                        dve.wait_ge(share_set, 2)
                    router(b)
                    with dve.Fori(0, PAIRS) as p:
                        q = p + b * PAIRS
                        for s in range(STEPS):
                            step = q * STEPS + s
                            for f in range(FT):
                                dve.wait_ge(ht_lo, 1 + step * FT + (f + 1 - FT if s else 0))
                                dve.wait_ge(silu_set, 1 + step * FT + f + 1)
                                dve.wait_ge(gu_full, 1 + step * (2 * FT) + 2 * f + 2)
                                nc.vector.tensor_tensor(h[:, f], s_g[:, f], pg[2 * f + 1][:], ALU.mult).then_inc(h_set, 1)
                            for f in range(FT):
                                dve.wait_ge(ht_hi, 1 + step * FT + f + 1)
                                nc.vector.tensor_tensor(ht[:, s % 2, LO, f], h[:, f], ht[:, s % 2, HI, f].bitcast(F32),
                                                        ALU.subtract).then_inc(ht_lo, 1)
                            if s == 1:
                                split_w(1, q * 2 + 2)
                            if s == BLK + 1:
                                split_w(0, q * 2 + 3)
                            if s:
                                add_down(b, p * 2, step - 1, s - 1)
                        add_down(b, p * 2, q * STEPS + (STEPS - 1), STEPS - 1)

            @block.tensor
            def _(pe):
                pe.wait_ge(r_lo, 2)

                def router(b):
                    for k in range(BLK):
                        pe.wait_ge(x3_lo, 1 + NX * b + 2 * k + 2)
                        if b:
                            pe.wait_ge(h_set, 1 + FT * STEPS * PAIRS * b)
                        n = 0
                        for c in range(C):
                            for s, m in PASSES:
                                mm = nc.tensor.matmul(pg[k][:], r_w[:, s, c], x3[:, m, k, c * TB:(c + 1) * TB],
                                                      start=(n == 0), stop=(n == 3 * C - 1))
                                n += 1
                        mm.then_inc(lg_full, 1)
                    pe.wait_ge(lg_taken, 1 + BLK * (b + 1))
                    if b:
                        pe.wait_ge(d_taken, 1 + PAIRS * STEPS * TT * b)
                    for k in range(BLK):
                        for t in range(TT):
                            n = k * TT + t
                            mm = nc.tensor.transpose(pd[0][:, n * E:(n + 1) * E], lg[k][:, t * P:(t + 1) * P],
                                                     ident[0:E, 0:E])
                    mm.then_inc(lt_full, 1)

                def gate_up(s, step):
                    k, slot = s % BLK, s // BLK
                    for f in range(FT):
                        for which, start in ((0, WG), (1, WU)):
                            pe.wait_ge((silu_set, h_set)[which], 1 + step * FT + (f + 1 - FT if s else 0))
                            n = 0
                            for c in range(C):
                                col = start + c * FE + f * P
                                for sp_, m in PASSES:
                                    mm = nc.tensor.matmul(pg[2 * f + which][:], w[:, slot, sp_, col:col + P],
                                                          x3[:, m, k, c * TB:(c + 1) * TB],
                                                          start=(n == 0), stop=(n == 3 * C - 1))
                                    n += 1
                            mm.then_inc(gu_full, 1)

                def down(s, step):
                    slot = s // BLK
                    pe.wait_ge(ht_lo, 1 + step * FT + FT)
                    for t in range(TT):
                        pe.wait_ge(d_taken, 1 + step * TT + (t + 1 - TT if s else 0))
                        n = 0
                        for f in range(FT):
                            for sp_, m in PASSES:
                                mm = nc.tensor.matmul(pd[t][:], ht[:, s % 2, sp_, f, t * P:(t + 1) * P],
                                                      w[:, slot, m, WD + f * D:WD + (f + 1) * D],
                                                      start=(n == 0), stop=(n == 3 * FT - 1))
                                n += 1
                        mm.then_inc(d_full, 1)

                for b in range(NB):
                    router(b)
                    pe.wait_ge(lt_taken, 1 + b + 1)
                    with pe.Fori(0, PAIRS) as p:
                        q = p + b * PAIRS
                        for s in range(STEPS):
                            if s % BLK == 0:
                                pe.wait_ge(w_lo, 1 + q * 2 + (s // BLK + 1))
                            gate_up(s, q * STEPS + s)
                            if s:
                                down(s - 1, q * STEPS + (s - 1))
                        down(STEPS - 1, q * STEPS + (STEPS - 1))


def kernel(**inputs):
    import concourse.bacc as bacc
    from concourse.bass_utils import run_bass_kernel_spmd

    f = {k.removeprefix("L0_"): np.asarray(v) for k, v in inputs.items()}
    proj = f["attn_proj_matrix"]
    features = np.zeros((P, G, HG, F), np.float32)
    for h in range(H):
        g, j = h // HG, h % HG
        features[j * HD:(j + 1) * HD, g, j] = proj[h]
    ctx = f["ctx_1024"].transpose(0, 2, 1)
    rest = np.concatenate([ctx[:, :, P:], np.repeat(ctx[:, :, -1:], KPAD - KREM, 2)], 2)
    ctx_t = np.concatenate([ctx[:, :, :P], rest, rest, rest, rest, rest], 2)

    def chunks(w):
        return w.reshape(-1, P, w.shape[1]).transpose(1, 0, 2).reshape(P, -1)

    gates = list(f["ffn_w_gate"]) + np.split(f["ffn_ws_gate"], 2, axis=1)
    ups = list(f["ffn_w_up"]) + np.split(f["ffn_ws_up"], 2, axis=1)
    downs = list(f["ffn_w_down"]) + np.split(f["ffn_ws_down"], 2, axis=0)
    units = [np.concatenate([chunks(g), chunks(u), chunks(d)], 1) for g, u, d in zip(gates, ups, downs)]
    router = np.zeros((D, P), np.float32)
    router[:, :E] = f["ffn_router_w"]
    arrays = {
        "x": f["x"], "w_qkv": f["attn_w_qkv"], "features": features.reshape(P, -1),
        "features3": np.concatenate([proj.transpose(1, 0, 2).reshape(HD, -1)] * 3, 0), "w_out": f["attn_w_out"],
        "b_out": f["attn_b_out"].reshape(1, D), "ctxT": ctx_t,
        "WqT": f["xattn_Wq"].T, "WkT": f["xattn_Wk"].T, "WvT": f["xattn_Wv"].T, "WoT": f["xattn_Wo"].T,
        "bqT": f["xattn_bq"].reshape(C, P).T, "bkT": f["xattn_bk"].reshape(C, P).T,
        "bv": f["xattn_bv"].reshape(1, D), "bo": f["xattn_bo"].reshape(1, D),
        "router": router, "units": np.stack(units + units[:1]),
    }
    arrays.update(constants())
    arrays = {"in_" + k: np.ascontiguousarray(v) for k, v in arrays.items()}

    nc = bacc.Bacc("TRN2", target_bir_lowering=False, num_devices=1)
    aps = {k[3:]: nc.dram_tensor(k, v.shape, mybir.dt.from_np(v.dtype), kind="ExternalInput").ap()
           for k, v in arrays.items()}
    out = nc.dram_tensor("out", f["x"].shape, F32, kind="ExternalOutput").ap()
    decoder_kernel(nc, aps, out)
    got = run_bass_kernel_spmd(nc, [arrays], core_ids=[0])
    return got.results[0]["out"]
```
